# Optimizing a Trainium2 kernel written in Bass

```python
import numpy as np
import jax
import jax.numpy as jnp

def _softmax(x, axis=-1):
    return jax.nn.softmax(x, axis=axis)

def _gelu(x):
    return jax.nn.gelu(x, approximate=True)

def _silu(x):
    return jax.nn.silu(x)

def _sigmoid(x):
    return jax.nn.sigmoid(x)

def _layernorm(x, axis=-1, eps=1e-05):
    m = jnp.mean(x, axis=axis, keepdims=True)
    v = jnp.var(x, axis=axis, keepdims=True)
    return (x - m) / jnp.sqrt(v + eps)

def _scatter_add(tgt, idx, src, axis=0):
    return tgt.at[idx].add(src)

def _segment_sum(src, seg, n):
    return jax.ops.segment_sum(src, seg, n)
kernel_name = 'mk_adj_resnorm_d4_adj_r2_09accc'

def setup_inputs(seed: int=0):
    np.random.seed(seed)
    _w = jnp.asarray

    def _rec_inputs():
        import jax
        import jax.numpy as jnp
        _gk = jax.random.key(seed)
        x = -0.0003929 + 0.9999 * jax.random.normal(jax.random.fold_in(_gk, 1), (16, 512, 128), jnp.float32)
        _a = jax.random.bernoulli(jax.random.fold_in(_gk, 2), 0.0078125, (512, 512))
        _a = jnp.logical_or(_a, jnp.swapaxes(_a, -1, -2))
        _a = jnp.logical_or(_a, jnp.eye(512, dtype=bool))
        _af = _a.astype(jnp.float32)
        _af = _af * jax.random.uniform(jax.random.fold_in(_gk, 3), (512, 512), jnp.float32, 0.05, 1)
        adj = _af
        return (x, adj)
    x, adj = _rec_inputs()

    def _L0_gnn_setup():
        import jax, jax.numpy as jnp
        import numpy as np
        B, N, H, OUT, RANK = (64, 512, 128, 128, 10)
        ORDER = 2

        def _conv(x, adj):
            return x * jnp.sum(adj, axis=1)[None, :, None]
        key = jax.random.key(seed)
        ks = jax.random.split(key, 6)
        x = jax.random.normal(ks[0], (B, N, H), dtype=jnp.float32)
        support0 = jax.random.uniform(ks[1], (N, N), dtype=jnp.float32)
        support1 = jax.random.uniform(ks[2], (N, N), dtype=jnp.float32)
        node_vec1 = jax.random.normal(ks[3], (N, RANK), dtype=jnp.float32)
        node_vec2 = jax.random.normal(ks[4], (RANK, N), dtype=jnp.float32)
        d_in = (ORDER * 3 + 1) * H
        W = jax.random.normal(ks[5], (d_in, OUT), dtype=jnp.float32) * (1.0 / np.sqrt(d_in))
        b = jnp.zeros((OUT,), dtype=jnp.float32)
        return {'x': x, 'support0': support0, 'support1': support1, 'node_vec1': node_vec1, 'node_vec2': node_vec2, 'W': W, 'b': b}
    _L0_gnn_all = _L0_gnn_setup()
    _L0_gnn_in = {k: v for k, v in _L0_gnn_all.items() if k in ('node_vec1', 'node_vec2', 'W', 'b')}
    del _L0_gnn_all

    def _L1_gnn_setup():
        import jax, jax.numpy as jnp
        import numpy as np
        EPS = 1e-05

        def _batchnorm(x, gamma, beta):
            mu = jnp.mean(x, axis=0)
            var = jnp.var(x, axis=0)
            return (x - mu) * jax.lax.rsqrt(var + EPS) * gamma + beta
        key = jax.random.key(seed)
        ks = jax.random.split(key, 4)
        b, n, d, h, o = (32, 1024, 128, 256, 128)
        features = jax.random.normal(ks[0], (b, n, d), dtype=jnp.float32)
        A = jax.random.uniform(ks[1], (n, n), dtype=jnp.float32)
        lim1 = float(np.sqrt(6.0 / (d + h)))
        W1 = jax.random.uniform(ks[2], (h, d), minval=-lim1, maxval=lim1, dtype=jnp.float32)
        b1 = jnp.zeros((h,), jnp.float32)
        lim2 = float(np.sqrt(6.0 / (h + o)))
        W2 = jax.random.uniform(ks[3], (o, h), minval=-lim2, maxval=lim2, dtype=jnp.float32)
        b2 = jnp.zeros((o,), jnp.float32)
        g1 = jnp.ones((h,), jnp.float32)
        be1 = jnp.zeros((h,), jnp.float32)
        g2 = jnp.ones((o,), jnp.float32)
        be2 = jnp.zeros((o,), jnp.float32)
        return {'features': features, 'A': A, 'W1': W1, 'b1': b1, 'g1': g1, 'be1': be1, 'W2': W2, 'b2': b2, 'g2': g2, 'be2': be2}
    _L1_gnn_all = _L1_gnn_setup()
    _L1_gnn_in = {k: v for k, v in _L1_gnn_all.items() if k in ('W1', 'b1', 'g1', 'be1', 'W2', 'b2', 'g2', 'be2')}
    del _L1_gnn_all

    def _L2_gnn_setup():
        import jax, jax.numpy as jnp
        import numpy as np
        B, T, D, H = (64, 1024, 128, 128)
        MAX_SKIP = 4

        def _lstm_last(Wih, Whh, bih, bhh, xs):
            N, _, Hd = xs.shape
            bias = bih + bhh

            def step(carry, x_t):
                h, c = carry
                g = x_t @ Wih.T + h @ Whh.T + bias
                i, f, gg, o = jnp.split(g, 4, axis=-1)
                c = jax.nn.sigmoid(f) * c + jax.nn.sigmoid(i) * jnp.tanh(gg)
                h = jax.nn.sigmoid(o) * jnp.tanh(c)
                return ((h, c), None)
            init = (jnp.zeros((N, Hd), xs.dtype), jnp.zeros((N, Hd), xs.dtype))
            (h_last, _), _ = jax.lax.scan(step, init, jnp.swapaxes(xs, 0, 1))
            return h_last
        key = jax.random.key(seed)
        ks = jax.random.split(key, 8)
        s = 0.05
        x = jax.random.normal(ks[0], (B, T, D), jnp.float32)
        adj = jax.random.uniform(ks[1], (T, T), jnp.float32) / T
        Wg0 = jax.random.normal(ks[2], (D, H), jnp.float32) * s
        bg0 = jnp.zeros((H,), jnp.float32)
        Wg1 = jax.random.normal(ks[3], (H, H), jnp.float32) * s
        bg1 = jnp.zeros((H,), jnp.float32)
        Wih = jax.random.normal(ks[4], (MAX_SKIP, 4 * H, H), jnp.float32) * s
        Whh = jax.random.normal(ks[5], (MAX_SKIP, 4 * H, H), jnp.float32) * s
        bih = jax.random.normal(ks[6], (MAX_SKIP, 4 * H), jnp.float32) * s
        bhh = jax.random.normal(ks[7], (MAX_SKIP, 4 * H), jnp.float32) * s
        return dict(x=x, adj=adj, Wg0=Wg0, bg0=bg0, Wg1=Wg1, bg1=bg1, Wih=Wih, Whh=Whh, bih=bih, bhh=bhh)
    _L2_gnn_all = _L2_gnn_setup()
    _L2_gnn_in = {k: v for k, v in _L2_gnn_all.items() if k in ('Wg0', 'bg0', 'Wg1', 'bg1', 'Wih', 'Whh', 'bih', 'bhh')}
    del _L2_gnn_all

    def _L3_gnn_setup():
        import jax, jax.numpy as jnp
        import numpy as np
        N_STEPS = 8
        SPATIAL_SCALE = 1.0
        key = jax.random.key(seed)
        ks = jax.random.split(key, 6)
        B, N, D = (32, 512, 128)
        x = jax.random.normal(ks[0], (B, N, D), dtype=jnp.float32)
        adj_mx = jax.random.uniform(ks[1], (N, N), dtype=jnp.float32) / N
        alpha_train = jnp.ones((N,), dtype=jnp.float32)
        w = jnp.eye(D, dtype=jnp.float32) + 0.01 * jax.random.normal(ks[2], (D, D), dtype=jnp.float32)
        d = jax.random.uniform(ks[3], (D,), dtype=jnp.float32)
        fc_in_w = jax.random.normal(ks[4], (D, D), dtype=jnp.float32) * (1.0 / np.sqrt(D))
        fc_in_b = jnp.zeros((D,), dtype=jnp.float32)
        return {'x': x, 'adj_mx': adj_mx, 'alpha_train': alpha_train, 'w': w, 'd': d, 'fc_in_w': fc_in_w, 'fc_in_b': fc_in_b, 'vt': 0}
    _L3_gnn_all = _L3_gnn_setup()
    _L3_gnn_in = {k: v for k, v in _L3_gnn_all.items() if k in ('alpha_train', 'w', 'd', 'fc_in_w', 'fc_in_b')}
    del _L3_gnn_all
    return {'x': x, 'adj': adj, 'L0_gnn_node_vec1': _L0_gnn_in['node_vec1'], 'L0_gnn_node_vec2': _L0_gnn_in['node_vec2'], 'L0_gnn_W': _L0_gnn_in['W'], 'L0_gnn_b': _L0_gnn_in['b'], 'L1_gnn_W1': _L1_gnn_in['W1'], 'L1_gnn_b1': _L1_gnn_in['b1'], 'L1_gnn_g1': _L1_gnn_in['g1'], 'L1_gnn_be1': _L1_gnn_in['be1'], 'L1_gnn_W2': _L1_gnn_in['W2'], 'L1_gnn_b2': _L1_gnn_in['b2'], 'L1_gnn_g2': _L1_gnn_in['g2'], 'L1_gnn_be2': _L1_gnn_in['be2'], 'L2_gnn_Wg0': _L2_gnn_in['Wg0'], 'L2_gnn_bg0': _L2_gnn_in['bg0'], 'L2_gnn_Wg1': _L2_gnn_in['Wg1'], 'L2_gnn_bg1': _L2_gnn_in['bg1'], 'L2_gnn_Wih': _L2_gnn_in['Wih'], 'L2_gnn_Whh': _L2_gnn_in['Whh'], 'L2_gnn_bih': _L2_gnn_in['bih'], 'L2_gnn_bhh': _L2_gnn_in['bhh'], 'L3_gnn_alpha_train': _L3_gnn_in['alpha_train'], 'L3_gnn_w': _L3_gnn_in['w'], 'L3_gnn_d': _L3_gnn_in['d'], 'L3_gnn_fc_in_w': _L3_gnn_in['fc_in_w'], 'L3_gnn_fc_in_b': _L3_gnn_in['fc_in_b']}

def reference(x, adj, L0_gnn_node_vec1, L0_gnn_node_vec2, L0_gnn_W, L0_gnn_b, L1_gnn_W1, L1_gnn_b1, L1_gnn_g1, L1_gnn_be1, L1_gnn_W2, L1_gnn_b2, L1_gnn_g2, L1_gnn_be2, L2_gnn_Wg0, L2_gnn_bg0, L2_gnn_Wg1, L2_gnn_bg1, L2_gnn_Wih, L2_gnn_Whh, L2_gnn_bih, L2_gnn_bhh, L3_gnn_alpha_train, L3_gnn_w, L3_gnn_d, L3_gnn_fc_in_w, L3_gnn_fc_in_b):
    import jax
    import jax.numpy as jnp

    def _L0_gnn_ref(x, support0, support1, node_vec1, node_vec2, W, b):
        import jax, jax.numpy as jnp
        import numpy as np
        B, N, H, OUT, RANK = (64, 512, 128, 128, 10)
        ORDER = 2

        def _conv(x, adj):
            return x * jnp.sum(adj, axis=1)[None, :, None]
        adaptive = jax.nn.softmax(jax.nn.relu(node_vec1 @ node_vec2), axis=1)
        outputs = [x]
        for adj in (support0, support1, adaptive):
            x1 = _conv(x, adj)
            outputs.append(x1)
            for _ in range(2, ORDER + 1):
                x1 = _conv(x1, adj)
                outputs.append(x1)
        out = jnp.concatenate(outputs, axis=2)
        out = out @ W + b
        return out

    def _L1_gnn_ref(features, A, W1, b1, g1, be1, W2, b2, g2, be2):
        import jax, jax.numpy as jnp
        import numpy as np
        EPS = 1e-05

        def _batchnorm(x, gamma, beta):
            mu = jnp.mean(x, axis=0)
            var = jnp.var(x, axis=0)
            return (x - mu) * jax.lax.rsqrt(var + EPS) * gamma + beta
        b, n, d = features.shape
        A_norm = A + jnp.eye(n, dtype=A.dtype)
        deg = jnp.sum(A_norm, axis=0) + jnp.sum(A_norm, axis=1) - jnp.diagonal(A_norm)
        dinv = jax.lax.rsqrt(deg)
        A_hat = A_norm * dinv[:, None] * dinv[None, :]
        agg = jnp.einsum('nm,bmd->bnd', A_hat, features)
        x = agg.reshape(-1, d)
        h = jax.nn.relu(_batchnorm(x @ W1.T + b1, g1, be1))
        out = h @ W2.T + b2
        out = _batchnorm(out, g2, be2)
        return out.reshape(b, n, -1)

    def _L2_gnn_ref(x, adj, Wg0, bg0, Wg1, bg1, Wih, Whh, bih, bhh):
        import jax, jax.numpy as jnp
        import numpy as np
        B, T, D, H = (64, 1024, 128, 128)
        MAX_SKIP = 4

        def _lstm_last(Wih, Whh, bih, bhh, xs):
            N, _, Hd = xs.shape
            bias = bih + bhh

            def step(carry, x_t):
                h, c = carry
                g = x_t @ Wih.T + h @ Whh.T + bias
                i, f, gg, o = jnp.split(g, 4, axis=-1)
                c = jax.nn.sigmoid(f) * c + jax.nn.sigmoid(i) * jnp.tanh(gg)
                h = jax.nn.sigmoid(o) * jnp.tanh(c)
                return ((h, c), None)
            init = (jnp.zeros((N, Hd), xs.dtype), jnp.zeros((N, Hd), xs.dtype))
            (h_last, _), _ = jax.lax.scan(step, init, jnp.swapaxes(xs, 0, 1))
            return h_last
        h = jax.nn.relu(jnp.einsum('ts,bsh->bth', adj, x @ Wg0 + bg0))
        h = jax.nn.relu(jnp.einsum('ts,bsh->bth', adj, h @ Wg1 + bg1))
        Bv, Tv, Hd = h.shape
        for p in range(1, MAX_SKIP + 1):
            nw = Tv // p
            wins = h[:, :nw * p, :].reshape(Bv * nw, p, Hd)
            last = _lstm_last(Wih[p - 1], Whh[p - 1], bih[p - 1], bhh[p - 1], wins)
            idx = jnp.arange(nw) * p + (p - 1)
            h = h.at[:, idx, :].set(last.reshape(Bv, nw, Hd))
        return h

    def _L3_gnn_ref(x, adj_mx, alpha_train, w, d, fc_in_w, fc_in_b, vt):
        import jax, jax.numpy as jnp
        import numpy as np
        N_STEPS = 8
        SPATIAL_SCALE = 1.0
        x0 = jax.lax.stop_gradient(x)
        h = jnp.einsum('bnd,ed->bne', x, fc_in_w) + fc_in_b
        alph = jax.nn.sigmoid(alpha_train)[:, None]
        d_clamped = jnp.clip(d, 0.0, 1.0)
        w_eff = w * d_clamped @ w.T
        dt = jnp.float32(SPATIAL_SCALE / N_STEPS)

        def euler_step(h, _):
            ax = jnp.einsum('nm,bmd->bnd', adj_mx, h)
            f = alph * 0.5 * (ax - h) + h @ w_eff - h + x0
            return (h + dt * f, None)
        h, _ = jax.lax.scan(euler_step, h, None, length=N_STEPS)
        return h
    x = _layernorm(x + _L0_gnn_ref(x, adj, adj, L0_gnn_node_vec1, L0_gnn_node_vec2, L0_gnn_W, L0_gnn_b), axis=-1)
    x = _layernorm(x + _L1_gnn_ref(x, adj, L1_gnn_W1, L1_gnn_b1, L1_gnn_g1, L1_gnn_be1, L1_gnn_W2, L1_gnn_b2, L1_gnn_g2, L1_gnn_be2), axis=-1)
    x = _layernorm(x + _L2_gnn_ref(x, adj, L2_gnn_Wg0, L2_gnn_bg0, L2_gnn_Wg1, L2_gnn_bg1, L2_gnn_Wih, L2_gnn_Whh, L2_gnn_bih, L2_gnn_bhh), axis=-1)
    x = _layernorm(x + _L3_gnn_ref(x, adj, L3_gnn_alpha_train, L3_gnn_w, L3_gnn_d, L3_gnn_fc_in_w, L3_gnn_fc_in_b, 0), axis=-1)
    return x

_drawn_inputs = setup_inputs


def setup_inputs(seed=0):
    import zlib

    import numpy as np

    out = dict(_drawn_inputs(seed))
    spreads = {'L0_gnn_b': (0.0, 0.389),
     'L1_gnn_b1': (0.0, 2.0),
     'L1_gnn_g1': (1.0, 0.2),
     'L1_gnn_be1': (0.0, 0.1),
     'L1_gnn_b2': (0.0, 2.0),
     'L1_gnn_g2': (1.0, 0.2),
     'L1_gnn_be2': (0.0, 0.1),
     'L2_gnn_bg0': (0.0, 0.1),
     'L2_gnn_bg1': (0.0, 0.375),
     'L3_gnn_alpha_train': (1.0, 0.6),
     'L3_gnn_fc_in_b': (0.0, 0.1)}
    factors = {'L0_gnn_node_vec1': 200.0, 'L0_gnn_node_vec2': 200.0, 'L2_gnn_Whh': 8.0}
    for name, (base, spread) in spreads.items():
        noise = np.random.default_rng([zlib.crc32(name.encode()), seed]).standard_normal(out[name].shape)
        drawn = base * np.exp(spread * noise) if base else spread * noise
        out[name] = jnp.asarray(drawn.astype(out[name].dtype))
    for name, factor in factors.items():
        out[name] = (out[name] * factor).astype(out[name].dtype)
    return out
```

```python
from contextlib import ExitStack
from math import comb

import concourse.bass as bass
from concourse import mybir

F32 = mybir.dt.float32
F32R = mybir.dt.float32r
ALU = mybir.AluOpType
ACT = mybir.ActivationFunctionType
AX_X = mybir.AxisListType.X

P = 128
B = 16
N = 512
D = 128
NT = N // P
HID = 256
HT = HID // P
SKIPS = 4
GB = 2
G = B // GB
STEPS = 8
DT = 1.0 / STEPS
EPS = 1e-5
PAIRS = [(p, t, j) for p in range(1, SKIPS + 1) for t in range(p) for j in (range(GB) if p == 1 else [None])]
CELLS = len(PAIRS)
GATES = [3 if t == 0 else 4 for _, t, _ in PAIRS]
GATES_ALL = sum(GATES)


def need(eng, sem, value):
    if isinstance(value, int) and value <= 0:
        return
    eng.wait_ge(sem, value)


class Chain:

    def __init__(self, eng, sem):
        self.eng, self.sem, self.base, self.n = eng, sem, 0, 0

    def link(self, ins):
        self.n += 1
        ins.then_inc(self.sem, 1)
        self.eng.wait_ge(self.sem, self.base + self.n)


def f32(ap):
    return ap.bitcast(F32)


def program(nc, x_t, adj_n, adj_t, nv1_t, nv2, l0_w, l0_b, w1_t, bn1, w2_t, bn2, wg, bg0, bg1,
            wih_t, whh_t, bih, bhh, alpha, l3_w_t, l3_d, fc_w, fc_b, eye, out):
    o2_dram = nc.dram_tensor("o2_spill", (B, P, N), F32, kind="Internal").ap()
    x1_dram = nc.dram_tensor("x1_spill", (B, P, N), F32, kind="Internal").ap()
    x2_dram = nc.dram_tensor("x2_spill", (B, P, N), F32, kind="Internal").ap()
    with ExitStack() as whole:
        def sem(name):
            return whole.enter_context(nc.semaphore(name))

        exponent = whole.enter_context(nc.sbuf_tensor("exponent", [P, 8], F32))
        banks = [whole.enter_context(nc.psum_tensor(f"bank{i}", [P, 512], F32)) for i in range(8)]
        ident = whole.enter_context(nc.sbuf_tensor("ident", [P, P], F32))
        scale2 = whole.enter_context(nc.sbuf_tensor("scale2", [P, 1], F32))
        shift2 = whole.enter_context(nc.sbuf_tensor("shift2", [P, 1], F32))
        first_half(nc, sem, banks, ident, exponent, scale2, shift2, x_t, adj_n, adj_t, nv1_t, nv2, l0_w, l0_b,
                   w1_t, bn1, w2_t, bn2, eye, x1_dram, o2_dram)
        second_half(nc, sem, banks, ident, exponent, scale2, shift2, adj_n, adj_t, wg, bg0, bg1, wih_t, whh_t, bih, bhh,
                    alpha, l3_w_t, l3_d, fc_w, fc_b, x1_dram, o2_dram, x2_dram, out)


class Roots:

    def __init__(self, asked, rooted, exponent):
        self.asked, self.rooted, self.exponent, self.base, self.n = asked, rooted, exponent, 0, 0

    def ask(self, dve, ins):
        self.n += 1
        ins.then_inc(self.asked, 1)
        dve.wait_ge(self.rooted, self.base + self.n)

    def answer(self, nc, pool, ap):
        self.n += 1
        pool.wait_ge(self.asked, self.base + self.n)
        nc.gpsimd.tensor_tensor(ap, ap, self.exponent[:, 0:ap.shape[-1]], ALU.pow).then_inc(self.rooted, 1)


def layer_norm(nc, dve, chain, roots, src, dst, stats, mv, rstd, tiles):
    for i in range(tiles):
        ins = nc.vector.bn_stats(stats[:, i, :], src[i])
    chain.link(ins)
    even, odd = stats[:, 0:tiles, 0:3], stats[:, 0:tiles, 3:6]
    nc.vector.tensor_tensor(mv[:, 0, :], even[:, :, 1], odd[:, :, 1], ALU.add)
    nc.vector.tensor_tensor(mv[:, 1, :], even[:, :, 1], odd[:, :, 1], ALU.subtract)
    chain.link(nc.vector.tensor_tensor(mv[:, 2, :], even[:, :, 2], odd[:, :, 2], ALU.add))
    nc.vector.tensor_scalar(mv[:, 0, :], mv[:, 0, :], 0.5, None, ALU.mult)
    nc.vector.tensor_scalar(mv[:, 2, :], mv[:, 2, :], 1.0 / D, EPS, ALU.mult, ALU.add)
    chain.link(nc.vector.scalar_tensor_tensor(out=mv[:, 1, :], in0=mv[:, 1, :], scalar=0.25, in1=mv[:, 1, :],
                                              op0=ALU.mult, op1=ALU.mult))
    roots.ask(dve, nc.vector.tensor_tensor(rstd[:, 0:tiles], mv[:, 1, :], mv[:, 2, :], ALU.add))
    for i in range(tiles):
        ins = nc.vector.tensor_scalar(dst[i], src[i], mv[:, 0, i:i + 1], rstd[:, i:i + 1], ALU.subtract, ALU.mult)
    return ins


LN_LINKS = 3
AHEAD = 3


def matmul3(pe, dst, lhs, rhs, start, stop, **kw):
    (lh, ll), (rh, rl) = lhs, rhs
    pe.matmul(dst, lh, rh, start=start, stop=False, **kw)
    pe.matmul(dst, lh, rl, start=False, stop=False, **kw)
    return pe.matmul(dst, ll, rh, start=False, stop=stop, **kw)


def first_half(nc, sem, banks, ident, exponent, scale2, shift2, x_t, adj_n, adj_t, nv1_t, nv2, l0_w, l0_b,
               w1_t, bn1, w2_t, bn2, eye, x1_dram, o2_dram):
    RANK = nv2.shape[0]
    with ExitStack() as ctx:
        def sb(name, shape, dt=F32):
            return ctx.enter_context(nc.sbuf_tensor(name, shape, dt))

        adjn = sb("adjn", [P, NT, N])
        adjt = sb("adjt", [P, NT, N])
        nv1s = sb("nv1s", [RANK, N])
        nv2s = sb("nv2s", [RANK, N])
        wraw = sb("wraw", [P, 7, D])
        wmix = sb("wmix", [P, 5, D])
        wmix_h, wmix_l = sb("wmix_h", [P, 5, D], F32R), sb("wmix_l", [P, 5, D], F32R)
        ahat_h, ahat_l = sb("ahat_h", [P, NT, N], F32R), sb("ahat_l", [P, NT, N], F32R)
        w1raw, w2raw = sb("w1raw", [P, HID]), sb("w2raw", [P, HT, D])
        w1h, w1l = sb("w1h", [P, HID], F32R), sb("w1l", [P, HID], F32R)
        w2h, w2l = sb("w2h", [P, HT, D], F32R), sb("w2l", [P, HT, D], F32R)
        bias0 = sb("bias0", [P, D])
        bn1s, bn2s = sb("bn1s", [P, 3, HT]), sb("bn2s", [P, 3])
        ones = sb("ones", [P, P])
        logits = sb("logits", [P, NT, N])
        coef = sb("coef", [P, 4, NT])
        deg = sb("deg", [P, 4, NT])
        dinv = sb("dinv", [P, NT])
        diag = sb("diag", [P, NT, P])
        smax = sb("smax", [P, 4, NT])
        xt = sb("xt", [P, 2, N])
        xth, xtl = sb("xth", [P, 2, N], F32R), sb("xtl", [P, 2, N], F32R)
        mix = sb("mix", [P, NT, D])
        x1 = sb("x1", [P, 2, NT, D])
        x1h, x1l = sb("x1h", [P, NT, D], F32R), sb("x1l", [P, NT, D], F32R)
        aggh, aggl = sb("aggh", [P, N], F32R), sb("aggl", [P, N], F32R)
        z = sb("z", [P, HT, B, N])
        zstats = sb("zstats", [P, HT, B, 6])
        stats, mv, rstd = sb("stats", [P, NT, 6]), sb("mv", [P, 3, NT]), sb("rstd", [P, NT])
        zmv, sc1, sh1 = sb("zmv", [P, HT, 2]), sb("sc1", [P, HT]), sb("sh1", [P, HT])
        act1 = sb("act1", [P, 2, HT, N])
        r_h, r_l = sb("r_h", [P, 2, HT, N], F32R), sb("r_l", [P, 2, HT, N], F32R)
        o2 = sb("o2", [P, 2, N])
        ostats, omv = sb("ostats", [P, B, 6]), sb("omv", [P, 2])

        asked, rooted = sem("asked"), sem("rooted")
        exponent_ready = sem("exponent_ready")
        c_adj, c_w, c_rest = sem("c_adj"), sem("c_w"), sem("c_rest")
        dve1, act_setup, pe_setup = sem("dve1"), sem("act_setup"), sem("pe_setup")
        dve_setup = sem("dve_setup")
        weights_ready = sem("weights_ready")
        xt_loaded, xt_hi, xt_lo = sem("xt_loaded"), sem("xt_hi"), sem("xt_lo")
        prod_done, mixed, mix_done = sem("prod_done"), sem("mixed"), sem("mix_done")
        x1_ready, x1_hi, x1_lo, x1_stored = sem("x1_ready"), sem("x1_hi"), sem("x1_lo"), [sem("x1_stored0"), sem("x1_stored1")]
        agg_done, agg_hi, agg_lo = sem("agg_done"), sem("agg_hi"), sem("agg_lo")
        z_done, z_kept, z_counted = sem("z_done"), sem("z_kept"), sem("z_counted")
        bn1_ready = sem("bn1_ready")
        r_ready, r_hi = sem("r_ready"), sem("r_hi")
        r_lo = [sem("r_lo0"), sem("r_lo1")]
        o2_done, o2_kept, o2_counted, o2_stored = sem("o2_done"), sem("o2_kept"), sem("o2_counted"), [sem("o2_stored0"), sem("o2_stored1")]

        PROD = banks[0:4]
        BASE = banks[4:6]
        AGG = banks[6]
        ZB = [banks[6], banks[7]]

        block = ctx.enter_context(nc.Block())

        def tile(ap, i):
            return ap[:, i * P:(i + 1) * P]

        def stores_before(b, par):
            return 8 * (b - par)

        @block.sync
        def _(sp):
            sp.dma_start(adjn[:], adj_n).then_inc(c_adj, 16)
            sp.dma_start(adjt[:], adj_t).then_inc(c_adj, 16)
            sp.dma_start(nv1s[:], nv1_t).then_inc(c_w, 16)
            sp.dma_start(nv2s[:], nv2).then_inc(c_w, 16)
            sp.dma_start(ident[:], eye).then_inc(c_w, 16)
            sp.dma_start(wraw[:], l0_w).then_inc(c_w, 16)
            sp.dma_start(xt[:, 0, :], x_t[0]).then_inc(xt_loaded, 16)
            for dst, src in ((bias0, l0_b), (w1raw, w1_t), (w2raw, w2_t), (bn1s, bn1), (bn2s, bn2)):
                sp.dma_start(dst[:], src).then_inc(c_rest, 16)

            def slot(b, par, has_next):
                if has_next:
                    need(sp, xt_hi, b)
                    need(sp, xt_lo, b)
                    sp.dma_start(xt[:, 1 - par, :], x_t[b + 1]).then_inc(xt_loaded, 16)
                sp.wait_ge(x1_ready, b + 1)
                sp.dma_start(x1_dram[b], x1[:, par, :, :].rearrange("p t d -> p (t d)")).then_inc(x1_stored[par], 16)

            for b in range(AHEAD):
                slot(b, b % 2, True)
            with sp.Fori(0, (B - AHEAD - 1) // 2) as i:
                slot(2 * i + AHEAD, 1, True)
                slot(2 * i + AHEAD + 1, 0, True)
            slot(B - 1, 1, False)

            def spill(b, par):
                sp.wait_ge(o2_kept, b + 1)
                sp.dma_start(o2_dram[b], o2[:, par, :]).then_inc(o2_stored[par], 16)

            with sp.Fori(0, B // 2) as i:
                spill(2 * i, 0)
                spill(2 * i + 1, 1)
            for par in range(2):
                sp.wait_ge(x1_stored[par], 16 * B // 2)
                sp.wait_ge(o2_stored[par], 16 * B // 2)

        @block.gpsimd
        def _(pool):
            roots = Roots(asked, rooted, exponent)
            nc.gpsimd.memset(exponent[:], -0.5).then_inc(exponent_ready, 1)
            pool.wait_ge(exponent_ready, 1)
            roots.answer(nc, pool, dinv[:])

            def split_x(b, par):
                pool.wait_ge(xt_hi, b + 1)
                nc.gpsimd.tensor_tensor(xtl[:, par, :], xt[:, par, :], f32(xth[:, par, :]),
                                        ALU.subtract).then_inc(xt_lo, 1)

            def slot(b, par, has_next):
                if has_next:
                    split_x(b + 1, 1 - par)
                roots.answer(nc, pool, rstd[:])
                pool.wait_ge(x1_hi, b + 1)
                nc.gpsimd.tensor_tensor(x1l[:], x1[:, par, :, :], f32(x1h[:]), ALU.subtract).then_inc(x1_lo, 1)

            split_x(0, 0)
            for b in range(AHEAD):
                slot(b, b % 2, True)
            with pool.Fori(0, (B - AHEAD - 1) // 2) as i:
                roots.base, roots.n = i * 2 + AHEAD + 1, 0
                slot(2 * i + AHEAD, 1, True)
                slot(2 * i + AHEAD + 1, 0, True)
            roots.base, roots.n = B, 0
            slot(B - 1, 1, False)
            roots.answer(nc, pool, sc1[:])

            def low_r(b, par):
                pool.wait_ge(r_hi, b + 1)
                need(pool, o2_done, b - 1)
                nc.gpsimd.tensor_tensor(r_l[:, par, 0, :], act1[:, par, 0, :], f32(r_h[:, par, 0, :]),
                                        ALU.subtract).then_inc(r_lo[0], 1)

            low_r(0, 0)
            low_r(1, 1)
            with pool.Fori(1, B // 2) as i:
                low_r(2 * i, 0)
                low_r(2 * i + 1, 1)
            roots.answer(nc, pool, scale2[:])

        @block.scalar
        def _(act):
            for t in range(NT):
                act.wait_ge(dve_setup, 1)
                ins = nc.scalar.activation(logits[:, t, :], logits[:, t, :], ACT.Exp, bias=smax[:, 1, t:t + 1],
                                           accum_out=smax[:, 2, t:t + 1])
            ins.then_inc(act_setup, 1)
            act.wait_ge(dve_setup, 2)
            nc.scalar.copy(ahat_h[:], adjt[:]).then_inc(act_setup, 1)
            nc.scalar.copy(wmix_h[:], wmix[:]).then_inc(act_setup, 1)
            act.wait_ge(c_rest, 80)
            nc.scalar.copy(w1h[:], w1raw[:]).then_inc(act_setup, 1)
            nc.scalar.copy(w2h[:], w2raw[:]).then_inc(act_setup, 1)

            def split_x(b, par):
                act.wait_ge(xt_loaded, 16 * (b + 1))
                need(act, prod_done, NT * (b - 1))
                nc.scalar.copy(xth[:, par, :], xt[:, par, :]).then_inc(xt_hi, 1)

            def high_agg(b):
                act.wait_ge(agg_done, b + 1)
                nc.scalar.copy(aggh[:], AGG[:]).then_inc(agg_hi, 1)

            def keep_z(b):
                for h in range(HT):
                    act.wait_ge(z_done, HT * b + h + 1)
                    nc.scalar.copy(z[:, h, b, :], ZB[h][:]).then_inc(z_kept, 1)

            def slot(b, par, has_prev, has_next):
                if has_next:
                    split_x(b + 1, 1 - par)
                if has_prev:
                    high_agg(b - 1)
                    keep_z(b - 1)
                act.wait_ge(x1_ready, b + 1)
                nc.scalar.copy(x1h[:], x1[:, par, :, :]).then_inc(x1_hi, 1)

            split_x(0, 0)
            for b in range(AHEAD):
                slot(b, b % 2, b > 0, True)
            with act.Fori(0, (B - AHEAD - 1) // 2) as i:
                slot(2 * i + AHEAD, 1, True, True)
                slot(2 * i + AHEAD + 1, 0, True, True)
            slot(B - 1, 1, True, False)
            high_agg(B - 1)
            keep_z(B - 1)

            act.wait_ge(bn1_ready, 1)

            def relu(b, par):
                for h in range(HT):
                    need(act, r_lo[h], b - 1)
                for h in range(HT):
                    ins = nc.scalar.activation(act1[:, par, h, :], z[:, h, b, :], ACT.Relu,
                                               bias=sh1[:, h:h + 1], scale=sc1[:, h:h + 1])
                ins.then_inc(r_ready, 1)

            def keep_o2(b, par):
                act.wait_ge(o2_done, b + 1)
                need(act, o2_stored[par], stores_before(b, par))
                need(act, o2_counted, b - 1)
                nc.scalar.copy(o2[:, par, :], banks[par][:]).then_inc(o2_kept, 1)

            relu(0, 0)
            relu(1, 1)
            keep_o2(0, 0)
            relu(2, 0)
            keep_o2(1, 1)
            with act.Fori(1, B // 2 - 1) as i:
                relu(2 * i + 1, 1)
                keep_o2(2 * i, 0)
                relu(2 * i + 2, 0)
                keep_o2(2 * i + 1, 1)
            relu(B - 1, 1)
            keep_o2(B - 2, 0)
            keep_o2(B - 1, 1)

        @block.vector
        def _(dve):
            chain = Chain(dve, dve1)
            roots = Roots(asked, rooted, exponent)
            dve.wait_ge(c_adj, 32)
            nc.vector.reduce_sum(coef[:, 0, :], adjn[:], AX_X)
            nc.vector.reduce_sum(deg[:, 0, :], adjt[:], AX_X)
            dve.wait_ge(c_w, 64)
            for t in range(NT):
                ins = nc.vector.tensor_tensor(diag[:, t, :], tile(adjn[:, t, :], t), ident[:], ALU.mult)
            chain.link(ins)
            nc.vector.reduce_sum(deg[:, 1, :], diag[:], AX_X)
            chain.link(nc.vector.tensor_tensor(deg[:, 2, :], coef[:, 0, :], deg[:, 0, :], ALU.add))
            chain.link(nc.vector.tensor_tensor(deg[:, 3, :], deg[:, 2, :], deg[:, 1, :], ALU.subtract))
            roots.ask(dve, nc.vector.tensor_scalar(dinv[:], deg[:, 3, :], 1.0, None, ALU.add))
            nc.vector.memset(ones[:], 1.0)
            for t in range(NT):
                nc.vector.tensor_tensor(tile(adjt[:, t, :], t), tile(adjt[:, t, :], t), ident[:], ALU.add)
                ins = nc.vector.tensor_scalar(diag[:, t, :], ident[:], dinv[:, t:t + 1], None, ALU.mult)
            chain.link(ins)
            dve.wait_ge(pe_setup, 1)
            for t in range(NT):
                ins = nc.vector.tensor_scalar(logits[:, t, :], banks[t][:], 0.0, None, ALU.max)
            chain.link(ins)
            chain.link(nc.vector.reduce_max(smax[:, 0, :], logits[:], AX_X))
            nc.vector.tensor_scalar(smax[:, 1, :], smax[:, 0, :], -1.0, None, ALU.mult).then_inc(dve_setup, 1)
            dve.wait_ge(pe_setup, 2)
            for t in range(NT):
                nc.vector.scalar_tensor_tensor(out=adjt[:, t, :], in0=adjt[:, t, :], scalar=dinv[:, t:t + 1],
                                               in1=banks[4][:], op0=ALU.mult, op1=ALU.mult)
            nc.vector.tensor_tensor(wmix[:, 0, :], wraw[:, 0, :], ident[:], ALU.add)
            nc.vector.tensor_tensor(wmix[:, 1:3, :], wraw[:, 1:3, :], wraw[:, 3:5, :], ALU.add)
            nc.vector.tensor_copy(wmix[:, 3:5, :], wraw[:, 5:7, :]).then_inc(dve_setup, 1)
            dve.wait_ge(act_setup, 1)
            chain.link(nc.vector.reciprocal(smax[:, 3, :], smax[:, 2, :]))
            for t in range(NT):
                ins = nc.vector.tensor_scalar(logits[:, t, :], logits[:, t, :], smax[:, 3, t:t + 1], None, ALU.mult)
            chain.link(ins)
            nc.vector.tensor_tensor(coef[:, 1, :], coef[:, 0, :], coef[:, 0, :], ALU.mult)
            chain.link(nc.vector.reduce_sum(coef[:, 2, :], logits[:], AX_X))
            nc.vector.tensor_tensor(coef[:, 3, :], coef[:, 2, :], coef[:, 2, :], ALU.mult)
            dve.wait_ge(act_setup, 3)
            nc.vector.tensor_tensor(ahat_l[:], adjt[:], f32(ahat_h[:]), ALU.subtract)
            nc.vector.tensor_tensor(wmix_l[:], wmix[:], f32(wmix_h[:]), ALU.subtract).then_inc(weights_ready, 1)
            dve.wait_ge(act_setup, 5)
            nc.vector.tensor_tensor(w1l[:], w1raw[:], f32(w1h[:]), ALU.subtract)
            chain.link(nc.vector.tensor_tensor(w2l[:], w2raw[:], f32(w2h[:]), ALU.subtract))
            dve.sem_inc(weights_ready, 1)

            def combine(b, first):
                for q, k in enumerate((1, 2, 3, 4)):
                    for t in (first, first + 1):
                        if q == 0:
                            dve.wait_ge(prod_done, NT * b + t + 1)
                        ins = nc.vector.scalar_tensor_tensor(
                            out=mix[:, t, :], in0=tile(PROD[t][:], k - 1), scalar=coef[:, k - 1, t:t + 1],
                            in1=bias0[:] if q == 0 else mix[:, t, :], op0=ALU.mult, op1=ALU.add)
                    if q < 3:
                        chain.link(ins)
                ins.then_inc(mixed, 1)

            def count_z(b):
                for h in range(HT):
                    dve.wait_ge(z_kept, HT * b + h + 1)
                    ins = nc.vector.bn_stats(zstats[:, h, b, :], z[:, h, b, :])
                ins.then_inc(z_counted, 1)

            def low_agg(b):
                dve.wait_ge(agg_hi, b + 1)
                nc.vector.tensor_tensor(aggl[:], AGG[:], f32(aggh[:]), ALU.subtract).then_inc(agg_lo, 1)

            def slot(b, par, has_prev):
                need(dve, x1_ready, b)
                combine(b, 0)
                if has_prev:
                    low_agg(b - 1)
                combine(b, 2)
                dve.wait_ge(mixed, 2 * b + 2)
                chain.link(nc.vector.tensor_tensor(mix[:].rearrange("p t d -> p (t d)"),
                                                   mix[:].rearrange("p t d -> p (t d)"), BASE[par][:], ALU.add))
                dve.sem_inc(mix_done, 1)
                if has_prev:
                    count_z(b - 1)
                need(dve, x1_stored[par], stores_before(b, par))
                need(dve, x1_lo, b - 1)
                layer_norm(nc, dve, chain, roots, [mix[:, t, :] for t in range(NT)], [x1[:, par, t, :] for t in range(NT)],
                           stats, mv, rstd, NT).then_inc(x1_ready, 1)

            LINKS = 6 + 1 + LN_LINKS
            for b in range(AHEAD):
                slot(b, b % 2, b > 0)
            after = chain.n
            with dve.Fori(0, (B - AHEAD - 1) // 2) as i:
                chain.base, chain.n = i * (2 * LINKS) + after, 0
                roots.base, roots.n = i * 2 + AHEAD + 1, 0
                slot(2 * i + AHEAD, 1, True)
                slot(2 * i + AHEAD + 1, 0, True)
                assert chain.n == 2 * LINKS
            chain.base, chain.n = after + (B - AHEAD - 1) * LINKS, 0
            roots.base, roots.n = B, 0
            slot(B - 1, 1, True)
            low_agg(B - 1)
            count_z(B - 1)

            dve.wait_ge(z_counted, B)
            for h in range(HT):
                ins = nc.vector.bn_aggr(zmv[:, h, :], zstats[:, h, :, :].rearrange("p b s -> p (b s)"))
            chain.link(ins)
            nc.vector.tensor_tensor(sh1[:], zmv[:, :, 0], bn1s[:, 0, :], ALU.add)
            roots.ask(dve, nc.vector.tensor_scalar(sc1[:], zmv[:, :, 1], EPS, None, ALU.add))
            nc.vector.tensor_tensor(sh1[:], bn1s[:, 0, :], sh1[:], ALU.subtract)
            chain.link(nc.vector.tensor_tensor(sc1[:], sc1[:], bn1s[:, 1, :], ALU.mult))
            chain.link(nc.vector.tensor_tensor(sh1[:], sh1[:], sc1[:], ALU.mult))
            nc.vector.tensor_tensor(sh1[:], sh1[:], bn1s[:, 2, :], ALU.add).then_inc(bn1_ready, 1)

            def split_r(b, par):
                dve.wait_ge(r_ready, b + 1)
                need(dve, o2_done, b - 1)
                nc.vector.tensor_copy(r_h[:, par, :, :], act1[:, par, :, :]).then_inc(r_hi, 1)
                dve.wait_ge(r_hi, b + 1)
                nc.vector.tensor_tensor(r_l[:, par, 1, :], act1[:, par, 1, :], f32(r_h[:, par, 1, :]),
                                        ALU.subtract).then_inc(r_lo[1], 1)

            def count_o2(b, par):
                dve.wait_ge(o2_kept, b + 1)
                nc.vector.bn_stats(ostats[:, b, :], o2[:, par, :]).then_inc(o2_counted, 1)

            split_r(0, 0)
            split_r(1, 1)
            count_o2(0, 0)
            with dve.Fori(1, B // 2) as i:
                split_r(2 * i, 0)
                count_o2(2 * i - 1, 1)
                split_r(2 * i + 1, 1)
                count_o2(2 * i, 0)
            count_o2(B - 1, 1)
            dve.wait_ge(o2_counted, B)
            chain.link(nc.vector.bn_aggr(omv[:], ostats[:].rearrange("p b s -> p (b s)")))
            nc.vector.tensor_tensor(shift2[:], omv[:, 0:1], bn2s[:, 0:1], ALU.add)
            roots.ask(dve, nc.vector.tensor_scalar(scale2[:], omv[:, 1:2], EPS, None, ALU.add))
            nc.vector.tensor_tensor(shift2[:], bn2s[:, 0:1], shift2[:], ALU.subtract)
            chain.link(nc.vector.tensor_tensor(scale2[:], scale2[:], bn2s[:, 1:2], ALU.mult))
            chain.link(nc.vector.tensor_tensor(shift2[:], shift2[:], scale2[:], ALU.mult))
            chain.link(nc.vector.tensor_tensor(shift2[:], shift2[:], bn2s[:, 2:3], ALU.add))

        @block.tensor
        def _(pe):
            pe.wait_ge(c_w, 64)
            for t in range(NT):
                mm = pe.matmul(banks[t][:], tile(nv1s[:], t), nv2s[:], start=True, stop=True)
            mm.then_inc(pe_setup, 1)
            pe.wait_ge(dve1, 4)
            for t in range(NT):
                mm = pe.matmul(tile(banks[4][:], t), ones[:], diag[:, t, :], start=True, stop=True)
            mm.then_inc(pe_setup, 1)
            pe.wait_ge(weights_ready, 1)

            def products(b, par, t):
                if t == 0:
                    pe.wait_ge(xt_hi, b + 1)
                    pe.wait_ge(xt_lo, b + 1)
                    need(pe, mix_done, b - 1)
                if t % 2 == 0:
                    need(pe, mixed, 2 * b + t // 2 - 1)
                x = (tile(xth[:, par, :], t), tile(xtl[:, par, :], t))
                wh, wl = wmix_h[:].rearrange("p k d -> p (k d)"), wmix_l[:].rearrange("p k d -> p (k d)")
                matmul3(pe, tile(BASE[par][:], t), x, (wh[:, 0:D], wl[:, 0:D]), True, True)
                matmul3(pe, PROD[t][:], x, (wh[:, D:5 * D], wl[:, D:5 * D]), True, True).then_inc(prod_done, 1)

            def aggregate(b):
                pe.wait_ge(x1_hi, b + 1)
                pe.wait_ge(x1_lo, b + 1)
                need(pe, z_kept, HT * b)
                for t in range(NT):
                    mm = matmul3(pe, AGG[:], (x1h[:, t, :], x1l[:, t, :]), (ahat_h[:, t, :], ahat_l[:, t, :]),
                                 t == 0, t == NT - 1)
                mm.then_inc(agg_done, 1)

            def hidden(b):
                pe.wait_ge(agg_lo, b + 1)
                for h in range(HT):
                    matmul3(pe, ZB[h][:], (tile(w1h[:], h), tile(w1l[:], h)), (aggh[:], aggl[:]),
                            True, True).then_inc(z_done, 1)

            def slot(b, par, has_prev):
                products(b, par, 0)
                products(b, par, 1)
                if has_prev:
                    aggregate(b - 1)
                products(b, par, 2)
                products(b, par, 3)
                if has_prev:
                    hidden(b - 1)

            slot(0, 0, False)
            pe.wait_ge(weights_ready, 2)
            for b in range(1, AHEAD):
                slot(b, b % 2, True)
            with pe.Fori(0, (B - AHEAD - 1) // 2) as i:
                slot(2 * i + AHEAD, 1, True)
                slot(2 * i + AHEAD + 1, 0, True)
            slot(B - 1, 1, True)
            aggregate(B - 1)
            hidden(B - 1)

            def second(b, par):
                pe.wait_ge(r_hi, b + 1)
                for h in range(HT):
                    pe.wait_ge(r_lo[h], b + 1)
                need(pe, o2_kept, b - 1)
                for h in range(HT):
                    mm = matmul3(pe, banks[par][:], (w2h[:, h, :], w2l[:, h, :]),
                                 (r_h[:, par, h, :], r_l[:, par, h, :]), h == 0, h == HT - 1)
                mm.then_inc(o2_done, 1)

            second(0, 0)
            second(1, 1)
            with pe.Fori(1, B // 2) as i:
                second(2 * i, 0)
                second(2 * i + 1, 1)


BABY = 3
POWERS = [1, 2, 3, 6]
KS = STEPS + 1


def second_half(nc, sem, banks, ident, exponent, scale2, shift2, adj_n, adj_t, wg, bg0, bg1, wih_t, whh_t, bih, bhh,
                alpha, l3_w_t, l3_d, fc_w, fc_b, x1_dram, o2_dram, x2_dram, out):
    with ExitStack() as ctx:
        def sb(name, shape, dt=F32):
            return ctx.enter_context(nc.sbuf_tensor(name, shape, dt))

        adj_h, adj_l = sb("adj_h", [P, NT, N], F32R), sb("adj_l", [P, NT, N], F32R)
        pow_h = sb("pow_h", [P, len(POWERS), NT, N], F32R)
        pow_l = sb("pow_l", [P, len(POWERS), NT, N], F32R)
        wih_h, wih_l = sb("wih_h", [P, SKIPS, 4 * D], F32R), sb("wih_l", [P, SKIPS, 4 * D], F32R)
        whh_h, whh_l = sb("whh_h", [P, SKIPS - 1, 4 * D], F32R), sb("whh_l", [P, SKIPS - 1, 4 * D], F32R)
        gate_bias = sb("gate_bias", [P, SKIPS, 4])
        e_h, e_l = sb("e_h", [P, BABY, BABY, D], F32R), sb("e_l", [P, BABY, BABY, D], F32R)
        wg_h, wg_l = sb("wg_h", [P, 2, D], F32R), sb("wg_l", [P, 2, D], F32R)
        conv_bias = sb("conv_bias", [P, NT, D])
        rows_bc = sb("rows_bc", [P, N])
        bg1s = sb("bg1s", [P, 1])
        euler_bias = sb("euler_bias", [P, NT, D])
        ident_r = sb("ident_r", [P, P], F32R)
        constants(nc, sem, banks, ident, adj_n, adj_t, wg, bg0, bg1, wih_t, whh_t, bih, bhh, alpha, l3_w_t, l3_d,
                  fc_w, fc_b, adj_h, adj_l, pow_h, pow_l, wih_h, wih_l, whh_h, whh_l, gate_bias, e_h, e_l,
                  wg_h, wg_l, conv_bias, rows_bc, bg1s, euler_bias, ident_r)
        groups(nc, sem, banks, ident, exponent, scale2, shift2, adj_h, adj_l, pow_h, pow_l, wih_h, wih_l, whh_h, whh_l,
               gate_bias, e_h, e_l, wg_h, wg_l, conv_bias, rows_bc, bg1s, euler_bias, ident_r,
               x1_dram, o2_dram, x2_dram, out)


def constants(nc, sem, banks, ident, adj_n, adj_t, wg, bg0, bg1, wih_t, whh_t, bih, bhh, alpha, l3_w_t, l3_d,
              fc_w, fc_b, adj_h, adj_l, pow_h, pow_l, wih_h, wih_l, whh_h, whh_l, gate_bias, e_h, e_l,
              wg_h, wg_l, conv_bias, rows_bc, bg1s, euler_bias, ident_r):
    with ExitStack() as ctx:
        def sb(name, shape, dt=F32):
            return ctx.enter_context(nc.sbuf_tensor(name, shape, dt))

        an, at = sb("an", [P, NT, N]), sb("at", [P, NT, N])
        nat_h, nat_l = sb("nat_h", [P, NT, N], F32R), sb("nat_l", [P, NT, N], F32R)
        ones2 = sb("ones2", [P, P])
        cols = sb("cols", [P, 2, NT])
        alphas = sb("alphas", [P, NT])
        diags = sb("diags", [P, 2, NT, P])
        wihs, whhs = sb("wihs", [P, SKIPS, 4 * D]), sb("whhs", [P, SKIPS - 1, 4 * D])
        bihs, bhhs = sb("bihs", [P, SKIPS, 4]), sb("bhhs", [P, SKIPS, 4])
        wgs, bg0s = sb("wgs", [P, 2, D]), sb("bg0s", [P, D])
        lw, lws, ld, fcw, fcb = sb("lw", [P, D]), sb("lws", [P, D]), sb("ld", [P, 1]), sb("fcw", [P, D]), sb("fcb", [P, 1])
        bp = sb("bp", [P, KS, D])
        fb = sb("fb", [P, KS, D])
        e = sb("e", [P, BABY, BABY, D])
        bcols = sb("bcols", [P, KS, KS])
        vec = sb("vec", [P, NT, KS])
        vec_t = sb("vec_t", [KS, N])
        bc = sb("bc", [KS, D])

        k_adj, k_small, k_rest = sem("k_adj"), sem("k_small"), sem("k_rest")
        k_dve, k_act, k_pe, k_chain, k_pool = sem("k_dve"), sem("k_act"), sem("k_pe"), sem("k_chain"), sem("k_pool")
        p_done, p_hi, p_lo = sem("p_done"), sem("p_hi"), sem("p_lo")
        v_done, v_kept = sem("v_done"), sem("v_kept")
        b_done, b_kept = sem("b_done"), sem("b_kept")
        f_done = sem("f_done")
        bc_done, bc_kept, vt_done, vt_kept, q_done = sem("bc_done"), sem("bc_kept"), sem("vt_done"), sem("vt_kept"), sem("q_done")

        block = ctx.enter_context(nc.Block())

        def tile(ap, i):
            return ap[:, i * P:(i + 1) * P]

        @block.sync
        def _(sp):
            sp.dma_start(an[:], adj_n).then_inc(k_adj, 16)
            sp.dma_start(at[:], adj_t).then_inc(k_adj, 16)
            for dst, src in ((alphas, alpha), (lw, l3_w_t), (ld, l3_d), (fcw, fc_w), (fcb, fc_b)):
                sp.dma_start(dst[:], src).then_inc(k_small, 16)
            for dst, src in ((wihs, wih_t), (whhs, whh_t), (bihs, bih), (bhhs, bhh), (wgs, wg), (bg0s, bg0), (bg1s, bg1)):
                sp.dma_start(dst[:], src).then_inc(k_rest, 16)

        @block.gpsimd
        def _(pool):
            nc.gpsimd.memset(bcols[:], 0.0).then_inc(k_pool, 1)
            pool.wait_ge(k_rest, 112)
            pool.wait_ge(k_act, 3)
            nc.gpsimd.tensor_tensor(wih_l[:], wihs[:], f32(wih_h[:]), ALU.subtract)
            nc.gpsimd.tensor_tensor(whh_l[:], whhs[:], f32(whh_h[:]), ALU.subtract)
            nc.gpsimd.tensor_tensor(wg_l[:], wgs[:], f32(wg_h[:]), ALU.subtract)
            nc.gpsimd.tensor_tensor(gate_bias[:], bihs[:], bhhs[:], ALU.add)

        @block.scalar
        def _(act):
            act.wait_ge(k_small, 80)
            nc.scalar.activation(alphas[:], alphas[:], ACT.Sigmoid).then_inc(k_act, 1)
            act.wait_ge(k_adj, 32)
            nc.scalar.copy(adj_h[:], at[:]).then_inc(k_act, 1)
            act.wait_ge(k_rest, 112)
            nc.scalar.copy(wih_h[:], wihs[:])
            nc.scalar.copy(whh_h[:], whhs[:])
            nc.scalar.copy(wg_h[:], wgs[:]).then_inc(k_act, 1)
            act.wait_ge(k_dve, 3)
            nc.scalar.copy(nat_h[:], an[:]).then_inc(k_act, 1)
            nc.scalar.copy(pow_h[:, 0, :, :], at[:]).then_inc(k_act, 1)

            def high(dst, first):
                for t in range(NT):
                    act.wait_ge(p_done, first + t + 1)
                    nc.scalar.copy(dst[:, t, :], banks[t][:]).then_inc(p_hi, 1)

            high(pow_h[:, 1, :, :], 0)
            high(pow_h[:, 2, :, :], NT)
            high(nat_h, 2 * NT)
            high(pow_h[:, 3, :, :], 3 * NT)
            act.wait_ge(k_dve, 4)
            nc.scalar.copy(e_h[:], e[:]).then_inc(k_act, 1)

        @block.vector
        def _(dve):
            chain = Chain(dve, k_chain)
            nc.vector.memset(ones2[:], 1.0)
            nc.vector.tensor_copy(ident_r[:], ident[:])
            nc.vector.tensor_copy(bp[:, 0, :], ident[:])
            dve.wait_ge(k_adj, 32)
            chain.link(nc.vector.reduce_sum(cols[:, 0, :], an[:], AX_X))
            dve.wait_ge(k_act, 1)
            chain.link(nc.vector.tensor_scalar(cols[:, 1, :], alphas[:], DT * 0.5, None, ALU.mult))
            for v in range(2):
                for t in range(NT):
                    ins = nc.vector.tensor_scalar(diags[:, v, t, :], ident[:], cols[:, v, t:t + 1], None, ALU.mult)
            ins.then_inc(k_dve, 1)
            chain.link(nc.vector.tensor_scalar(ld[:], ld[:], 0.0, 1.0, ALU.max, ALU.min))
            nc.vector.tensor_scalar(lws[:], lw[:], ld[:, 0:1], None, ALU.mult).then_inc(k_dve, 1)
            dve.wait_ge(k_act, 2)
            chain.link(nc.vector.tensor_tensor(adj_l[:], at[:], f32(adj_h[:]), ALU.subtract))
            for t in range(NT):
                nc.vector.tensor_tensor(tile(an[:, t, :], t), tile(an[:, t, :], t), ident[:], ALU.subtract)
                ins = nc.vector.tensor_tensor(tile(at[:, t, :], t), tile(at[:, t, :], t), ident[:], ALU.subtract)
            chain.link(ins)
            dve.wait_ge(k_pe, 2)
            nc.vector.tensor_copy(rows_bc[:], banks[4][:])
            for t in range(NT):
                nc.vector.tensor_scalar(an[:, t, :], an[:, t, :], cols[:, 1, t:t + 1], None, ALU.mult)
                ins = nc.vector.tensor_tensor(at[:, t, :], at[:, t, :], banks[5][:], ALU.mult)
            ins.then_inc(k_dve, 1)
            chain.link(nc.vector.memset(vec[:, :, 0], 1.0))
            dve.wait_ge(k_dve, 3)
            nc.vector.reduce_sum(vec[:, :, 1], an[:], AX_X).then_inc(v_kept, 1)
            dve.wait_ge(k_rest, 112)
            for t in range(NT):
                nc.vector.tensor_scalar(conv_bias[:, t, :], bg0s[:], cols[:, 0, t:t + 1], None, ALU.mult)
            dve.wait_ge(k_act, 4)
            nc.vector.tensor_tensor(nat_l[:], an[:], f32(nat_h[:]), ALU.subtract)
            dve.wait_ge(k_act, 5)
            nc.vector.tensor_tensor(pow_l[:, 0, :, :], at[:], f32(pow_h[:, 0, :, :]), ALU.subtract).then_inc(p_lo, 1)
            dve.wait_ge(k_pe, 3)
            chain.link(nc.vector.tensor_scalar(bp[:, 1, :], ident[:], 1.0 - DT, None, ALU.mult))
            nc.vector.scalar_tensor_tensor(out=bp[:, 1, :], in0=tile(banks[6][:], 0), scalar=DT, in1=bp[:, 1, :],
                                           op0=ALU.mult, op1=ALU.add).then_inc(b_kept, 1)
            dve.wait_ge(k_pool, 1)
            for k in range(KS):
                ins = nc.vector.tensor_scalar(bcols[:, k, k:k + 1], fcb[:], float(comb(STEPS, k)), None, ALU.mult)
            chain.link(ins)
            dve.wait_ge(b_done, 1)
            nc.vector.tensor_copy(bp[:, 2, :], tile(banks[6][:], 0)).then_inc(b_kept, 1)
            dve.wait_ge(b_done, 2)
            nc.vector.tensor_copy(bp[:, 3:5, :].rearrange("p k d -> p (k d)"), banks[7][:, 0:2 * D]).then_inc(b_kept, 1)
            dve.wait_ge(b_done, 3)
            nc.vector.tensor_copy(bp[:, 5:9, :].rearrange("p k d -> p (k d)"), banks[6][:]).then_inc(b_kept, 1)
            dve.wait_ge(v_done, 1)
            nc.vector.tensor_copy(vec[:, :, 2], banks[5][:, 0:NT]).then_inc(v_kept, 1)

            def low(dst, hi, first):
                for t in range(NT):
                    dve.wait_ge(p_hi, first + t + 1)
                    nc.vector.tensor_tensor(dst[:, t, :], banks[t][:], f32(hi[:, t, :]), ALU.subtract).then_inc(p_lo, 1)

            low(pow_l[:, 1, :, :], pow_h[:, 1, :, :], 0)
            for q, (a, b) in enumerate(((0, 4), (4, 8), (8, 9))):
                dve.wait_ge(f_done, q + 1)
                ins = nc.vector.tensor_copy(fb[:, a:b, :].rearrange("p k d -> p (k d)"),
                                            banks[6 + q % 2][:, 0:(b - a) * D])
                if q == 0:
                    ins.then_inc(b_kept, 1)
            chain.link(ins)
            low(pow_l[:, 2, :, :], pow_h[:, 2, :, :], NT)
            for k in range(KS):
                ins = nc.vector.tensor_scalar(e[:, k % BABY, k // BABY, :], fb[:, STEPS - k, :],
                                              float(comb(STEPS, k)), None, ALU.mult)
            chain.link(ins)
            for j in range(STEPS):
                for k in range(STEPS - j):
                    ek = e[:, k % BABY, k // BABY, :]
                    factor = DT * comb(j + k, k) + (1.0 if j == 0 and k == 0 else 0.0)
                    ins = nc.vector.scalar_tensor_tensor(out=ek, in0=bp[:, j, :], scalar=factor, in1=ek,
                                                         op0=ALU.mult, op1=ALU.add)
                if j < STEPS - 1:
                    chain.link(ins)
            ins.then_inc(k_dve, 1)
            low(nat_l, nat_h, 2 * NT)
            dve.wait_ge(v_done, 2)
            nc.vector.tensor_copy(vec[:, :, 3:6], banks[5][:, 0:3 * NT].rearrange("p (t k) -> p t k", k=3)).then_inc(v_kept, 1)
            dve.wait_ge(bc_done, 1)
            nc.vector.tensor_copy(bc[:], banks[7][0:KS, 0:D]).then_inc(bc_kept, 1)
            dve.wait_ge(v_done, 3)
            nc.vector.tensor_copy(vec[:, :, 6:9], banks[6][:, 0:3 * NT].rearrange("p (t k) -> p t k", k=3)).then_inc(v_kept, 1)
            dve.wait_ge(vt_done, 1)
            nc.vector.tensor_copy(vec_t[:], banks[5][0:KS, :]).then_inc(vt_kept, 1)
            low(pow_l[:, 3, :, :], pow_h[:, 3, :, :], 3 * NT)
            dve.wait_ge(k_act, 6)
            nc.vector.tensor_tensor(e_l[:], e[:], f32(e_h[:]), ALU.subtract)
            dve.wait_ge(q_done, 1)
            nc.vector.tensor_copy(euler_bias[:].rearrange("p t d -> p (t d)"), banks[7][:])

        @block.tensor
        def _(pe):
            pe.wait_ge(k_dve, 1)
            for v in range(2):
                for t in range(NT):
                    mm = pe.matmul(tile(banks[4 + v][:], t), ones2[:], diags[:, v, t, :], start=True, stop=True)
                mm.then_inc(k_pe, 1)
            pe.wait_ge(k_small, 80)
            pe.wait_ge(k_dve, 2)
            pe.matmul(tile(banks[6][:], 0), lws[:], lw[:], start=True, stop=True).then_inc(k_pe, 1)

            def bflat(a, b):
                return bp[:, a:b, :].rearrange("p k d -> p (k d)")

            def product(lh, ll, rh, rl, first):
                for t in range(NT):
                    need(pe, p_lo, first - NT + t + 2)
                    for m in range(NT):
                        mm = matmul3(pe, banks[t][:], (tile(lh[:, m, :], t), tile(ll[:, m, :], t)),
                                     (rh[:, m, :], rl[:, m, :]), m == 0, m == NT - 1)
                    mm.then_inc(p_done, 1)

            pe.wait_ge(p_lo, 1)
            product(nat_h, nat_l, pow_h[:, 0, :, :], pow_l[:, 0, :, :], 0)
            pe.wait_ge(b_kept, 1)
            pe.matmul(tile(banks[6][:], 0), bp[:, 1, :], bp[:, 1, :], start=True, stop=True).then_inc(b_done, 1)
            pe.wait_ge(b_kept, 2)
            pe.matmul(banks[7][:, 0:2 * D], bp[:, 2, :], bflat(1, 3), start=True, stop=True).then_inc(b_done, 1)
            pe.wait_ge(b_kept, 3)
            pe.matmul(banks[6][:], bp[:, 4, :], bflat(1, 5), start=True, stop=True).then_inc(b_done, 1)
            pe.wait_ge(v_kept, 1)
            for t in range(NT):
                for m in range(NT):
                    mm = pe.matmul(banks[5][:, t:t + 1], tile(at[:, m, :], t), vec[:, m, 1:2],
                                   start=(m == 0), stop=(m == NT - 1))
            mm.then_inc(v_done, 1)
            pe.wait_ge(b_kept, 4)
            for q, (a, b) in enumerate(((0, 4), (4, 8), (8, 9))):
                if q == 2:
                    pe.wait_ge(b_kept, 5)
                pe.matmul(banks[6 + q % 2][:, 0:(b - a) * D], fcw[:], bflat(a, b), start=True, stop=True).then_inc(f_done, 1)
            pe.wait_ge(p_lo, 1 + NT)
            product(nat_h, nat_l, pow_h[:, 1, :, :], pow_l[:, 1, :, :], NT)
            pe.wait_ge(p_lo, 1 + 2 * NT)
            for t in range(NT):
                for m in range(NT):
                    pe.matmul(tile(banks[t][:], m), tile(pow_h[:, 2, m, :], t), ident_r[:], start=True, stop=False)
                    mm = pe.matmul(tile(banks[t][:], m), tile(pow_l[:, 2, m, :], t), ident_r[:], start=False, stop=True)
                mm.then_inc(p_done, 1)

            def cube(bank, src):
                for t in range(NT):
                    for m in range(NT):
                        for q, half in enumerate((pow_h, pow_l)):
                            mm = pe.matmul(bank[:, 3 * t:3 * t + 3], f32(tile(half[:, 2, m, :], t)),
                                           vec[:, m, src:src + 3], start=(m == 0 and q == 0),
                                           stop=(m == NT - 1 and q == 1))
                mm.then_inc(v_done, 1)

            pe.wait_ge(v_kept, 2)
            cube(banks[5], 0)
            for k in range(KS):
                mm = pe.matmul(banks[7][0:KS, 0:D], bcols[:, k, :], bp[:, STEPS - k, :], start=(k == 0), stop=(k == KS - 1))
            mm.then_inc(bc_done, 1)
            pe.wait_ge(v_kept, 3)
            cube(banks[6], 3)
            pe.wait_ge(v_kept, 4)
            for t in range(NT):
                mm = pe.transpose(tile(banks[5][0:KS, :], t), vec[:, t, :], ident[:])
            mm.then_inc(vt_done, 1)
            pe.wait_ge(p_lo, 1 + 3 * NT)
            product(nat_h, nat_l, pow_h[:, 2, :, :], pow_l[:, 2, :, :], 3 * NT)
            pe.wait_ge(vt_kept, 1)
            pe.wait_ge(bc_kept, 1)
            for t in range(NT):
                mm = pe.matmul(tile(banks[7][:], t), tile(vec_t[:], t), bc[:], start=True, stop=True)
            mm.then_inc(q_done, 1)


def groups(nc, sem, banks, ident, exponent, scale2, shift2, adj_h, adj_l, pow_h, pow_l, wih_h, wih_l, whh_h, whh_l,
           gate_bias, e_h, e_l, wg_h, wg_l, conv_bias, rows_bc, bg1s, euler_bias, ident_r,
           x1_dram, o2_dram, x2_dram, out):
    with ExitStack() as ctx:
        def sb(name, shape, dt=F32):
            return ctx.enter_context(nc.sbuf_tensor(name, shape, dt))

        o2 = sb("o2b", [P, N])
        x1 = sb("x1b", [P, NT, D])
        x2 = sb("x2b", [P, NT, D])
        node_h, node_l = sb("node_h", [P, NT, D], F32R), sb("node_l", [P, NT, D], F32R)
        gat_h, gat_l = sb("gat_h", [P, N], F32R), sb("gat_l", [P, N], F32R)
        pre = sb("pre", [P, N])
        stats, mv, rstd = sb("lstats", [P, NT, 6]), sb("lmv", [P, 3, NT]), sb("lrstd", [P, NT])
        stats8, mv8, rstd8 = sb("stats8", [P, NT * GB, 6]), sb("mv8", [P, 3, NT * GB]), sb("rstd8", [P, NT * GB])
        hh, hl = sb("hh", [P, GB, N], F32R), sb("hl", [P, GB, N], F32R)
        gate = [sb(f"gate{i}", [P, N]) for i in range(4)]
        cell, tanc = sb("cell", [P, N]), sb("tanc", [P, N])
        st_h, st_l = sb("st_h", [P, N], F32R), sb("st_l", [P, N], F32R)
        y = sb("y", [P, NT, GB, D])
        x3h, x3l = sb("x3h", [P, NT, D], F32R), sb("x3l", [P, NT, D], F32R)
        th, tl = sb("th", [P, BABY, N], F32R), sb("tl", [P, BABY, N], F32R)
        gh, gl = sb("gh", [P, 2, NT, GB, D], F32R), sb("gl", [P, 2, NT, GB, D], F32R)

        s = {name: sem(name) for name in (
            "front_loaded", "normed2", "o2_turned", "x2_ready", "x2_stored", "x2_hi", "x2_lo", "h1_hi", "h1_lo",
            "gathered", "gat_hi", "gat_lo", "weighted", "pre0_ready", "pre1_ready", "h_hi", "h_ready",
            "gate_sum", "gate_on", "cell_ready", "tanh_ready", "state_ready",
            "y_loaded", "h_turned", "x3_ready", "x3_hi", "x3_lo", "power_done", "power_hi", "power_lo",
            "coef_done", "coef_hi", "coef_lo", "giant_done", "y_summed", "out_ready", "out_stored", "links")}
        front_loaded, normed2, o2_turned, x2_ready, x2_stored = (s[k] for k in ("front_loaded", "normed2", "o2_turned", "x2_ready", "x2_stored"))
        x2_hi, x2_lo, h1_hi, h1_lo, gathered, gat_hi, gat_lo = (s[k] for k in ("x2_hi", "x2_lo", "h1_hi", "h1_lo", "gathered", "gat_hi", "gat_lo"))
        weighted, pre0_ready, pre1_ready, h_hi, h_ready = (s[k] for k in ("weighted", "pre0_ready", "pre1_ready", "h_hi", "h_ready"))
        gate_sum, gate_on, cell_ready, tanh_ready, state_ready = (s[k] for k in ("gate_sum", "gate_on", "cell_ready", "tanh_ready", "state_ready"))
        y_loaded, h_turned, x3_ready, x3_hi, x3_lo = (s[k] for k in ("y_loaded", "h_turned", "x3_ready", "x3_hi", "x3_lo"))
        power_done, power_hi, power_lo, coef_done, coef_hi, coef_lo = (s[k] for k in ("power_done", "power_hi", "power_lo", "coef_done", "coef_hi", "coef_lo"))
        giant_done, y_summed, out_ready, out_stored, links = (s[k] for k in ("giant_done", "y_summed", "out_ready", "out_stored", "links"))

        GATE_BANK = {0: 0, 2: 1, 1: 2, 3: 3}
        FB = banks[4:6]
        UB = banks[6:8]
        out_v = out.rearrange("b (t p) d -> b p t d", p=P)

        def tile(ap, i):
            return ap[:, i * P:(i + 1) * P]

        def flat(ap):
            return ap.rearrange("p t d -> p (t d)")

        def shape_of(c):
            p, t, j = PAIRS[c]
            nw = N // p
            first = next(i for i, q in enumerate(PAIRS) if q[0] == p)
            return p, t, j, nw, (N if j is not None else GB * nw), sum(GATES[:c]), first

        def window(ap, c):
            p, t, j, nw, _, _, _ = shape_of(c)
            return ap[:, j, :] if j is not None else ap[:, :, t:p * (nw - 1) + t + 1:p]

        def flat_like(ap, c):
            _, _, j, nw, n, _, _ = shape_of(c)
            return ap[:, 0:n] if j is not None else ap[:, 0:n].rearrange("p (j w) -> p j w", j=GB)

        FILL = [["turn0"], ["gather0_0", "x3t_0"], ["weight0_0", "powers_0"], ["gather1_0", "coefs_0"],
                ["weight1_0", "x3t_1"], ["turn1", "powers_1"], ["gather0_1", "coefs_1"], ["weight0_1", "giant_0"],
                ["gather1_1", "giant_1"], ["weight1_1"], []]
        L3_NAMES = ("x3t", "powers", "coefs", "giant")

        def step(g, cell_step, pieces, lstm, l3, front, last):
            for c in range(CELLS):
                if lstm:
                    cell_step(g, c)
                for name in FILL[c]:
                    kind = name.split("_")[0]
                    if kind in L3_NAMES:
                        if l3:
                            pieces[kind](g - 1, int(name[-1]))
                    elif front:
                        pieces[kind.rstrip("01") if kind.startswith("turn") else kind](g + 1, int(name[-1]))
            last(g, lstm, front)

        def run(eng, cell_step, pieces, last, counters=()):
            step(-1, cell_step, pieces, False, False, True, last)
            step(0, cell_step, pieces, True, False, True, last)
            ahead = [c.n for c, _ in counters]
            with eng.Fori(1, G - 1) as g:
                for (c, per_step), n in zip(counters, ahead):
                    c.base, c.n = (g - 1) * per_step + n, 0
                step(g, cell_step, pieces, True, True, True, last)
                assert all(c.n == per_step for c, per_step in counters)
            for (c, per_step), n in zip(counters, ahead):
                c.base, c.n = (G - 2) * per_step + n, 0
            step(G - 1, cell_step, pieces, True, True, False, last)
            step(G, cell_step, pieces, False, True, False, last)

        LINKS_STEP = 0
        LINKS_STEP += GB * (1 + LN_LINKS)
        LINKS_STEP += sum(1 for _, t, _ in PAIRS if t > 0) + CELLS
        LINKS_STEP += GB * (1 + LN_LINKS)
        LINKS_STEP += LN_LINKS

        ROOTS_STEP = 2 * GB + 1
        asked2, rooted2 = sem("asked2"), sem("rooted2")

        block = ctx.enter_context(nc.Block())

        @block.sync
        def _(sp):
            def turn(g, j):
                n = GB * g + j
                need(sp, x2_ready, n)
                sp.dma_start(o2[:], o2_dram[n]).then_inc(front_loaded, 16)
                sp.dma_start(flat(x1[:]), x1_dram[n]).then_inc(front_loaded, 16)
                sp.wait_ge(x2_ready, n + 1)
                sp.dma_start(x2_dram[n], flat(x2[:])).then_inc(x2_stored, 16)

            def giant(g, half):
                if half == 1:
                    sp.wait_ge(out_ready, g + 1)
                    for j in range(GB):
                        sp.dma_start(out_v[GB * g + j], y[:, :, j, :]).then_inc(out_stored, 16)

            def last(g, lstm, front):
                if lstm:
                    need(sp, out_stored, 16 * GB * g)
                    for j in range(GB):
                        n = GB * g + j
                        sp.wait_ge(x2_stored, 16 * (n + 1))
                        sp.dma_start(y[:, :, j, :], x2_dram[n].rearrange("p (t d) -> p t d", d=D)).then_inc(y_loaded, 16)

            nop = lambda g, j: None
            run(sp, lambda g, c: None, {"turn": turn, "gather0": nop, "gather1": nop, "weight0": nop, "weight1": nop,
                                        "x3t": nop, "powers": nop, "coefs": nop, "giant": giant}, last)
            sp.wait_ge(out_stored, 16 * B)

        @block.gpsimd
        def _(pool):
            roots = Roots(asked2, rooted2, exponent)

            def turn(g, j):
                n = GB * g + j
                roots.answer(nc, pool, rstd[:])
                pool.wait_ge(x2_hi, n + 1)
                nc.gpsimd.tensor_tensor(node_l[:], x2[:], f32(node_h[:]), ALU.subtract).then_inc(x2_lo, 1)

            def x3t(g, j):
                n = GB * g + j
                pool.wait_ge(x3_hi, n + 1)
                nc.gpsimd.tensor_tensor(x3l[:], y[:, :, j, :], f32(x3h[:]), ALU.subtract).then_inc(x3_lo, 1)

            def giant(g, half):
                if half == 1:
                    roots.answer(nc, pool, rstd8[:])

            def last(g, lstm, front):
                if lstm:
                    for j in range(GB):
                        roots.answer(nc, pool, rstd[:])

            nop = lambda g, j: None
            run(pool, lambda g, c: None, {"turn": turn, "gather0": nop, "gather1": nop, "weight0": nop, "weight1": nop,
                                          "x3t": x3t, "powers": nop, "coefs": nop, "giant": giant}, last, ((roots, ROOTS_STEP),))

        @block.scalar
        def _(act):
            def cell_step(g, c):
                p, t, j, nw, n, before, first = shape_of(c)
                gates = [q for q in (0, 2, 1, 3) if t > 0 or q != 1]
                need(act, cell_ready, CELLS * g + c)
                for i, q in enumerate(gates):
                    act.wait_ge(gate_sum, GATES_ALL * g + before + i + 1)
                    if q in (1, 3):
                        need(act, state_ready, CELLS * g + c)
                    nc.scalar.activation(gate[q][:, 0:n], banks[GATE_BANK[q]][:, 0:n], ACT.Tanh if q == 2 else ACT.Sigmoid,
                                         bias=gate_bias[:, p - 1, q:q + 1]).then_inc(gate_on, 1)
                act.wait_ge(cell_ready, CELLS * g + c + 1)
                nc.scalar.activation(tanc[:, 0:n], cell[:, 0:n], ACT.Tanh).then_inc(tanh_ready, 1)

            def turn(g, j):
                n = GB * g + j
                act.wait_ge(x2_ready, n + 1)
                nc.scalar.copy(node_h[:], x2[:]).then_inc(x2_hi, 1)

            def gather(g, j, conv):
                act.wait_ge(gathered, 2 * (GB * g + j) + conv + 1)
                nc.scalar.copy(gat_h[:], FB[j][:]).then_inc(gat_hi, 1)

            def weight0(g, j):
                act.wait_ge(pre0_ready, GB * g + j + 1)
                nc.scalar.activation(flat(node_h[:]), pre[:], ACT.Relu).then_inc(h1_hi, 1)

            def x3t(g, j):
                n = GB * g + j
                act.wait_ge(x3_ready, n + 1)
                nc.scalar.copy(x3h[:], y[:, :, j, :]).then_inc(x3_hi, 1)
                act.wait_ge(power_done, BABY * n + 1)
                nc.scalar.copy(th[:, 0, :], UB[j][:]).then_inc(power_hi, 1)

            def powers(g, j):
                for k in range(1, BABY):
                    act.wait_ge(power_done, BABY * (GB * g + j) + k + 1)
                    nc.scalar.copy(th[:, k, :], UB[(j + k) % 2][:]).then_inc(power_hi, 1)

            def coefs(g, j):
                for t in range(NT):
                    act.wait_ge(coef_done, NT * (GB * g + j) + t + 1)
                    nc.scalar.copy(gh[:, :, t, j, :], UB[t % 2][:, D:3 * D].rearrange("p (k d) -> p k d", d=D)).then_inc(coef_hi, 1)

            def last(g, lstm, front):
                if front:
                    for j in range(GB):
                        act.wait_ge(pre1_ready, GB * (g + 1) + j + 1)
                        nc.scalar.activation(hh[:, j, :], pre[:], ACT.Relu).then_inc(h_hi, 1)

            run(act, cell_step, {"turn": turn, "gather0": lambda g, j: gather(g, j, 0), "gather1": lambda g, j: gather(g, j, 1),
                                 "weight0": weight0, "weight1": lambda g, j: None, "x3t": x3t, "powers": powers,
                                 "coefs": coefs, "giant": lambda g, j: None}, last)

        @block.vector
        def _(dve):
            chain = Chain(dve, links)
            roots = Roots(asked2, rooted2, exponent)

            def cell_step(g, c):
                p, t, j, nw, n, before, first = shape_of(c)
                dve.wait_ge(gate_on, GATES_ALL * g + before + 2)
                if t == 0:
                    need(dve, tanh_ready, CELLS * g + c)
                    nc.vector.tensor_tensor(cell[:, 0:n], gate[0][:, 0:n], gate[2][:, 0:n], ALU.mult).then_inc(cell_ready, 1)
                else:
                    nc.vector.tensor_tensor(gate[0][:, 0:n], gate[0][:, 0:n], gate[2][:, 0:n], ALU.mult)
                    dve.wait_ge(gate_on, GATES_ALL * g + before + 3)
                    chain.link(nc.vector.tensor_tensor(gate[1][:, 0:n], gate[1][:, 0:n], cell[:, 0:n], ALU.mult))
                    nc.vector.tensor_tensor(cell[:, 0:n], gate[0][:, 0:n], gate[1][:, 0:n], ALU.add).then_inc(cell_ready, 1)
                dve.wait_ge(tanh_ready, CELLS * g + c + 1)
                dve.wait_ge(gate_on, GATES_ALL * g + before + GATES[c])
                if t == p - 1:
                    dst_h, dst_l = window(hh, c), window(hl, c)
                else:
                    dst_h, dst_l = flat_like(st_h, c), flat_like(st_l, c)
                o, tc, whole_h = flat_like(gate[3], c), flat_like(tanc, c), flat_like(gate[1], c)
                nc.vector.tensor_tensor(dst_h, o, tc, ALU.mult)
                chain.link(nc.vector.tensor_tensor(whole_h, o, tc, ALU.mult))
                nc.vector.tensor_tensor(dst_l, whole_h, f32(dst_h), ALU.subtract).then_inc(state_ready, 1)

            def turn(g, j):
                n = GB * g + j
                dve.wait_ge(front_loaded, 32 * (n + 1))
                nc.vector.tensor_scalar(o2[:], o2[:], scale2[:, 0:1], shift2[:, 0:1], ALU.mult, ALU.add).then_inc(normed2, 1)
                dve.wait_ge(o2_turned, n + 1)
                need(dve, x2_stored, 16 * n)
                need(dve, x2_lo, n)
                chain.link(nc.vector.tensor_tensor(flat(x2[:]), FB[j][:], flat(x1[:]), ALU.add))
                tiles = [x2[:, t, :] for t in range(NT)]
                layer_norm(nc, dve, chain, roots, tiles, tiles, stats, mv, rstd, NT).then_inc(x2_ready, 1)

            def gather(g, j, conv):
                dve.wait_ge(gat_hi, 2 * (GB * g + j) + conv + 1)
                nc.vector.tensor_tensor(gat_l[:], FB[j][:], f32(gat_h[:]), ALU.subtract).then_inc(gat_lo, 1)

            def weight0(g, j):
                n = GB * g + j
                dve.wait_ge(weighted, 2 * n + 1)
                nc.vector.tensor_tensor(pre[:], FB[j][:], flat(conv_bias[:]), ALU.add).then_inc(pre0_ready, 1)
                dve.wait_ge(h1_hi, n + 1)
                nc.vector.scalar_tensor_tensor(out=flat(node_l[:]), in0=pre[:], scalar=0.0, in1=f32(flat(node_h[:])),
                                               op0=ALU.max, op1=ALU.subtract).then_inc(h1_lo, 1)

            def x3t(g, j):
                n = GB * g + j
                dve.wait_ge(power_hi, BABY * n + 1)
                nc.vector.tensor_tensor(tl[:, 0, :], UB[j][:], f32(th[:, 0, :]), ALU.subtract).then_inc(power_lo, 1)

            def powers(g, j):
                for k in range(1, BABY):
                    dve.wait_ge(power_hi, BABY * (GB * g + j) + k + 1)
                    nc.vector.tensor_tensor(tl[:, k, :], UB[(j + k) % 2][:], f32(th[:, k, :]), ALU.subtract).then_inc(power_lo, 1)

            def coefs(g, j):
                n = GB * g + j
                dve.wait_ge(x3_lo, n + 1)
                for t in range(NT):
                    dve.wait_ge(coef_hi, NT * n + t + 1)
                    nc.vector.tensor_tensor(y[:, t, j, :], UB[t % 2][:, 0:D], euler_bias[:, t, :], ALU.add)
                    nc.vector.tensor_tensor(gl[:, :, t, j, :], UB[t % 2][:, D:3 * D].rearrange("p (k d) -> p k d", d=D),
                                            f32(gh[:, :, t, j, :]), ALU.subtract).then_inc(coef_lo, 1)

            def giant(g, half):
                dve.wait_ge(giant_done, 2 * g + half + 1)
                part = y[:, 2 * half:2 * half + 2, :, :].rearrange("p t j d -> p (t j d)")
                ins = nc.vector.tensor_tensor(part, part, UB[half][:], ALU.add)
                ins.then_inc(y_summed, 1)
                if half == 1:
                    dve.wait_ge(y_summed, 2 * g + 2)
                    tiles = [y[:, t, j, :] for t in range(NT) for j in range(GB)]
                    layer_norm(nc, dve, chain, roots, tiles, tiles, stats8, mv8, rstd8, NT * GB).then_inc(out_ready, 1)

            def last(g, lstm, front):
                if lstm:
                    for j in range(GB):
                        n = GB * g + j
                        dve.wait_ge(y_loaded, 16 * GB * (g + 1))
                        dve.wait_ge(h_turned, n + 1)
                        chain.link(nc.vector.tensor_tensor(y[:, :, j, :], UB[j][:].rearrange("p (t d) -> p t d", d=D),
                                                           y[:, :, j, :], ALU.add))
                        tiles = [y[:, t, j, :] for t in range(NT)]
                        layer_norm(nc, dve, chain, roots, tiles, tiles, stats, mv, rstd, NT).then_inc(x3_ready, 1)
                if front:
                    for j in range(GB):
                        n = GB * (g + 1) + j
                        dve.wait_ge(weighted, 2 * n + 2)
                        need(dve, h_ready, n)
                        dve.wait_ge(h1_lo, GB * (g + 2))
                        if lstm:
                            dve.wait_ge(h_turned, GB * (g + 1))
                        nc.vector.scalar_tensor_tensor(out=pre[:], in0=rows_bc[:], scalar=bg1s[:, 0:1], in1=FB[j][:],
                                                       op0=ALU.mult, op1=ALU.add).then_inc(pre1_ready, 1)
                        dve.wait_ge(h_hi, n + 1)
                        nc.vector.scalar_tensor_tensor(out=hl[:, j, :], in0=pre[:], scalar=0.0, in1=f32(hh[:, j, :]),
                                                       op0=ALU.max, op1=ALU.subtract).then_inc(h_ready, 1)

            run(dve, cell_step, {"turn": turn, "gather0": lambda g, j: gather(g, j, 0), "gather1": lambda g, j: gather(g, j, 1),
                                 "weight0": weight0, "weight1": lambda g, j: None, "x3t": x3t, "powers": powers,
                                 "coefs": coefs, "giant": giant}, last, ((chain, LINKS_STEP), (roots, ROOTS_STEP)))

        @block.tensor
        def _(pe):
            def cell_step(g, c):
                p, t, j, nw, n, before, first = shape_of(c)
                gates = [q for q in (0, 2, 1, 3) if t > 0 or q != 1]
                if j is not None:
                    pe.wait_ge(h_ready, GB * g + j + 1)
                else:
                    pe.wait_ge(state_ready, CELLS * g + first)
                need(pe, gate_on, GATES_ALL * g + before)
                for q in gates:
                    mm = matmul3(pe, flat_like(banks[GATE_BANK[q]], c), (tile(wih_h[:, p - 1, :], q), tile(wih_l[:, p - 1, :], q)),
                                 (window(hh, c), window(hl, c)), True, t == 0)
                    if t == 0:
                        mm.then_inc(gate_sum, 1)
                if t > 0:
                    pe.wait_ge(state_ready, CELLS * g + c)
                    for q in gates:
                        matmul3(pe, banks[GATE_BANK[q]][:, 0:n], (tile(whh_h[:, p - 2, :], q), tile(whh_l[:, p - 2, :], q)),
                                (st_h[:, 0:n], st_l[:, 0:n]), False, True).then_inc(gate_sum, 1)

            def turn(g, j):
                n = GB * g + j
                pe.wait_ge(normed2, n + 1)
                need(pe, pre1_ready, n - 1)
                for t in range(NT):
                    mm = pe.transpose(tile(FB[j][:], t), tile(o2[:], t), ident[:])
                mm.then_inc(o2_turned, 1)

            def gather(g, j, conv):
                n = GB * g + j
                if conv == 0:
                    pe.wait_ge(x2_lo, n + 1)
                else:
                    pe.wait_ge(h1_lo, n + 1)
                for t in range(NT):
                    mm = matmul3(pe, FB[j][:], (node_h[:, t, :], node_l[:, t, :]), (adj_h[:, t, :], adj_l[:, t, :]),
                                 t == 0, t == NT - 1)
                mm.then_inc(gathered, 1)

            def weight0(g, j):
                pe.wait_ge(gat_lo, 2 * (GB * g + j) + 1)
                for t in range(NT):
                    mm = matmul3(pe, tile(FB[j][:], t), (tile(gat_h[:], t), tile(gat_l[:], t)),
                                 (wg_h[:, 0, :], wg_l[:, 0, :]), True, True)
                mm.then_inc(weighted, 1)

            def weight1(g, j):
                pe.wait_ge(gat_lo, 2 * (GB * g + j) + 2)
                matmul3(pe, FB[j][:], (wg_h[:, 1, :], wg_l[:, 1, :]), (gat_h[:], gat_l[:]), True, True).then_inc(weighted, 1)

            def x3t(g, j):
                n = GB * g + j
                pe.wait_ge(x3_ready, n + 1)
                if j > 0:
                    pe.wait_ge(coef_lo, NT * n)
                for t in range(NT):
                    mm = pe.transpose(tile(UB[j][:], t), y[:, t, j, :], ident[:])
                mm.then_inc(power_done, 1)

            def powers(g, j):
                n = GB * g + j
                pe.wait_ge(x3_lo, n + 1)
                pe.wait_ge(x3_ready, GB * (g + 1))
                for k in range(1, BABY):
                    if j > 0 or k > 1:
                        pe.wait_ge(power_lo, BABY * n + k - 1)
                    for t in range(NT):
                        mm = matmul3(pe, UB[(j + k) % 2][:], (x3h[:, t, :], x3l[:, t, :]),
                                     (pow_h[:, k - 1, t, :], pow_l[:, k - 1, t, :]), t == 0, t == NT - 1)
                    mm.then_inc(power_done, 1)

            def coefs(g, j):
                n = GB * g + j
                pe.wait_ge(power_lo, BABY * (n + 1))
                for t in range(NT):
                    if t >= 2:
                        pe.wait_ge(coef_lo, NT * n + t - 1)
                    for k in range(BABY):
                        mm = matmul3(pe, UB[t % 2][:, 0:3 * D], (tile(th[:, k, :], t), tile(tl[:, k, :], t)),
                                     (e_h[:, k, :, :].rearrange("p a d -> p (a d)"), e_l[:, k, :, :].rearrange("p a d -> p (a d)")),
                                     k == 0, k == BABY - 1)
                    mm.then_inc(coef_done, 1)

            def giant(g, half):
                pe.wait_ge(coef_lo, NT * GB * (g + 1))
                for t in (2 * half, 2 * half + 1):
                    dst = UB[half][:, (t % 2) * GB * D:(t % 2 + 1) * GB * D]
                    for k in range(2):
                        for m in range(NT):
                            mm = matmul3(pe, dst, (tile(pow_h[:, 2 + k, m, :], t), tile(pow_l[:, 2 + k, m, :], t)),
                                         (gh[:, k, m, :, :].rearrange("p j d -> p (j d)"), gl[:, k, m, :, :].rearrange("p j d -> p (j d)")),
                                         k == 0 and m == 0, k == 1 and m == NT - 1)
                mm.then_inc(giant_done, 1)

            def last(g, lstm, front):
                if lstm:
                    pe.wait_ge(state_ready, CELLS * (g + 1))
                    need(pe, y_summed, 2 * g)
                    for j in range(GB):
                        for t in range(NT):
                            pe.matmul(tile(UB[j][:], t), tile(hh[:, j, :], t), ident_r[:], start=True, stop=False)
                            mm = pe.matmul(tile(UB[j][:], t), tile(hl[:, j, :], t), ident_r[:], start=False, stop=True)
                        mm.then_inc(h_turned, 1)

            run(pe, cell_step, {"turn": turn, "gather0": lambda g, j: gather(g, j, 0), "gather1": lambda g, j: gather(g, j, 1),
                                "weight0": weight0, "weight1": weight1, "x3t": x3t, "powers": powers,
                                "coefs": coefs, "giant": giant}, last)


def kernel(**inputs):
    import numpy as np
    import concourse.bacc as bacc
    from concourse.bass_utils import run_bass_kernel_spmd

    v = {k: np.asarray(a) for k, a in inputs.items()}

    def rows(a):
        return a.reshape(-1, P, a.shape[-1]).transpose(1, 0, 2)

    def column(a):
        return a.reshape(-1, P).T

    laid = [
        ("x_t", v["x"].transpose(0, 2, 1)),
        ("adj_n", rows(v["adj"])),
        ("adj_t", rows(v["adj"].T)),
        ("nv1_t", v["L0_gnn_node_vec1"].T),
        ("nv2", v["L0_gnn_node_vec2"]),
        ("l0_w", rows(v["L0_gnn_W"])),
        ("l0_b", np.tile(v["L0_gnn_b"], (P, 1))),
        ("w1_t", v["L1_gnn_W1"].T),
        ("bn1", np.stack([column(v["L1_gnn_" + k]) for k in ("b1", "g1", "be1")], 1)),
        ("w2_t", rows(v["L1_gnn_W2"].T)),
        ("bn2", np.stack([v["L1_gnn_" + k] for k in ("b2", "g2", "be2")], 1)),
        ("wg", np.stack([v["L2_gnn_Wg0"], v["L2_gnn_Wg1"]], 1)),
        ("bg0", np.tile(v["L2_gnn_bg0"], (P, 1))),
        ("bg1", v["L2_gnn_bg1"][:, None]),
        ("wih_t", v["L2_gnn_Wih"].transpose(2, 0, 1)),
        ("whh_t", v["L2_gnn_Whh"][1:].transpose(2, 0, 1)),
        ("bih", v["L2_gnn_bih"].reshape(SKIPS, 4, P).transpose(2, 0, 1)),
        ("bhh", v["L2_gnn_bhh"].reshape(SKIPS, 4, P).transpose(2, 0, 1)),
        ("alpha", column(v["L3_gnn_alpha_train"])),
        ("l3_w_t", v["L3_gnn_w"].T),
        ("l3_d", v["L3_gnn_d"][:, None]),
        ("fc_w", v["L3_gnn_fc_in_w"]),
        ("fc_b", v["L3_gnn_fc_in_b"][:, None]),
        ("eye", np.eye(P, dtype=np.float32)),
    ]
    nc = bacc.Bacc("TRN2", target_bir_lowering=False, num_devices=1)
    arrays, args = {}, []
    for name, a in laid:
        a = np.ascontiguousarray(a)
        arrays[f"in_{name}_dram"] = a
        args.append(nc.dram_tensor(f"in_{name}_dram", a.shape, mybir.dt.from_np(a.dtype), kind="ExternalInput").ap())
    args.append(nc.dram_tensor("out_dram", (B, N, D), F32, kind="ExternalOutput").ap())
    program(nc, *args)
    r = run_bass_kernel_spmd(nc, [arrays], core_ids=[0])
    return r.results[0]["out_dram"]
```

```python
from contextlib import ExitStack
from math import comb

import concourse.bass as bass
from concourse import mybir

F32 = mybir.dt.float32
F32R = mybir.dt.float32r
ALU = mybir.AluOpType
ACT = mybir.ActivationFunctionType
AX_X = mybir.AxisListType.X

P = 128
B = 16
N = 512
D = 128
NT = N // P
HID = 256
HT = HID // P
SKIPS = 4
GB = 2
G = B // GB
STEPS = 8
DT = 1.0 / STEPS
EPS = 1e-5
PAIRS = [(p, t, j) for p in range(1, SKIPS + 1) for t in range(p) for j in (range(GB) if p == 1 else [None])]
CELLS = len(PAIRS)
GATES = [3 if t == 0 else 4 for _, t, _ in PAIRS]
GATES_ALL = sum(GATES)


def need(eng, sem, value):
    if isinstance(value, int) and value <= 0:
        return
    eng.wait_ge(sem, value)


class Chain:

    def __init__(self, eng, sem):
        self.eng, self.sem, self.base, self.n = eng, sem, 0, 0

    def link(self, ins):
        self.n += 1
        ins.then_inc(self.sem, 1)
        self.eng.wait_ge(self.sem, self.base + self.n)


def f32(ap):
    return ap.bitcast(F32)


def program(nc, x_t, adj_n, adj_t, nv1_t, nv2, l0_w, l0_b, w1_t, bn1, w2_t, bn2, wg, bg0, bg1,
            wih_t, whh_t, bih, bhh, alpha, l3_w_t, l3_d, fc_w, fc_b, eye, out):
    o2_dram = nc.dram_tensor("o2_spill", (B, P, N), F32, kind="Internal").ap()
    x1_dram = nc.dram_tensor("x1_spill", (B, P, N), F32, kind="Internal").ap()
    x2_dram = nc.dram_tensor("x2_spill", (B, P, N), F32, kind="Internal").ap()
    with ExitStack() as whole:
        def sem(name):
            return whole.enter_context(nc.semaphore(name))

        def sb(name, shape, dt=F32):
            return whole.enter_context(nc.sbuf_tensor(name, shape, dt))

        exponent = whole.enter_context(nc.sbuf_tensor("exponent", [P, 8], F32))
        banks = [whole.enter_context(nc.psum_tensor(f"bank{i}", [P, 512], F32)) for i in range(8)]
        ident = whole.enter_context(nc.sbuf_tensor("ident", [P, P], F32))
        scale2 = whole.enter_context(nc.sbuf_tensor("scale2", [P, 1], F32))
        shift2 = whole.enter_context(nc.sbuf_tensor("shift2", [P, 1], F32))
        adj_h, adj_l = sb("adj_h", [P, NT, N], F32R), sb("adj_l", [P, NT, N], F32R)
        wih_h, wih_l = sb("wih_h", [P, SKIPS, 4 * D], F32R), sb("wih_l", [P, SKIPS, 4 * D], F32R)
        whh_h, whh_l = sb("whh_h", [P, SKIPS - 1, 4 * D], F32R), sb("whh_l", [P, SKIPS - 1, 4 * D], F32R)
        wg_h, wg_l = sb("wg_h", [P, 2, D], F32R), sb("wg_l", [P, 2, D], F32R)
        gate_bias = sb("gate_bias", [P, SKIPS, 4])
        first_half(nc, sem, banks, ident, exponent, scale2, shift2, x_t, adj_n, adj_t, nv1_t, nv2, l0_w, l0_b,
                   w1_t, bn1, w2_t, bn2, eye, wg, wih_t, whh_t, bih, bhh, adj_h, adj_l, wih_h, wih_l, whh_h, whh_l,
                   wg_h, wg_l, gate_bias, x1_dram, o2_dram)
        second_half(nc, sem, banks, ident, exponent, scale2, shift2, adj_n, adj_t, bg0, bg1, alpha, l3_w_t, l3_d,
                    fc_w, fc_b, adj_h, adj_l, wih_h, wih_l, whh_h, whh_l, wg_h, wg_l, gate_bias,
                    x1_dram, o2_dram, x2_dram, out)


class Roots:

    def __init__(self, asked, rooted, exponent):
        self.asked, self.rooted, self.exponent, self.base, self.n = asked, rooted, exponent, 0, 0

    def ask(self, dve, ins):
        self.n += 1
        ins.then_inc(self.asked, 1)
        dve.wait_ge(self.rooted, self.base + self.n)

    def answer(self, nc, pool, ap):
        self.n += 1
        pool.wait_ge(self.asked, self.base + self.n)
        nc.gpsimd.tensor_tensor(ap, ap, self.exponent[:, 0:ap.shape[-1]], ALU.pow).then_inc(self.rooted, 1)


def moments(nc, chain, stats, mv, tiles):
    even, odd = stats[:, 0:tiles, 0:3], stats[:, 0:tiles, 3:6]
    nc.vector.tensor_tensor(mv[:, 0, :], even[:, :, 1], odd[:, :, 1], ALU.add)
    nc.vector.tensor_tensor(mv[:, 1, :], even[:, :, 1], odd[:, :, 1], ALU.subtract)
    chain.link(nc.vector.tensor_tensor(mv[:, 2, :], even[:, :, 2], odd[:, :, 2], ALU.add))
    nc.vector.tensor_scalar(mv[:, 0, :], mv[:, 0, :], 0.5, None, ALU.mult)
    nc.vector.tensor_scalar(mv[:, 2, :], mv[:, 2, :], 1.0 / D, EPS, ALU.mult, ALU.add)
    chain.link(nc.vector.scalar_tensor_tensor(out=mv[:, 1, :], in0=mv[:, 1, :], scalar=0.25, in1=mv[:, 1, :],
                                              op0=ALU.mult, op1=ALU.mult))


def layer_norm(nc, dve, chain, roots, src, dst, stats, mv, rstd, tiles):
    for i in range(tiles):
        ins = nc.vector.bn_stats(stats[:, i, :], src[i])
    chain.link(ins)
    moments(nc, chain, stats, mv, tiles)
    roots.ask(dve, nc.vector.tensor_tensor(rstd[:, 0:tiles], mv[:, 1, :], mv[:, 2, :], ALU.add))
    for i in range(tiles):
        ins = nc.vector.tensor_scalar(dst[i], src[i], mv[:, 0, i:i + 1], rstd[:, i:i + 1], ALU.subtract, ALU.mult)
    return ins


LN_LINKS = 3
AHEAD = 3


def matmul3(pe, dst, lhs, rhs, start, stop, **kw):
    (lh, ll), (rh, rl) = lhs, rhs
    pe.matmul(dst, lh, rh, start=start, stop=False, **kw)
    pe.matmul(dst, lh, rl, start=False, stop=False, **kw)
    return pe.matmul(dst, ll, rh, start=False, stop=stop, **kw)


def first_half(nc, sem, banks, ident, exponent, scale2, shift2, x_t, adj_n, adj_t, nv1_t, nv2, l0_w, l0_b,
               w1_t, bn1, w2_t, bn2, eye, wg, wih_t, whh_t, bih, bhh, adj_h, adj_l, wih_h, wih_l, whh_h, whh_l,
               wg_h, wg_l, gate_bias, x1_dram, o2_dram):
    RANK = nv2.shape[0]
    with ExitStack() as ctx:
        def sb(name, shape, dt=F32):
            return ctx.enter_context(nc.sbuf_tensor(name, shape, dt))

        adjn = sb("adjn", [P, NT, N])
        adjt = sb("adjt", [P, NT, N])
        logits = sb("logits", [P, NT, N])
        nv1s = sb("nv1s", [RANK, N])
        nv2s = sb("nv2s", [RANK, N])
        wraw = sb("wraw", [P, 7, D])
        wmix = sb("wmix", [P, 5, D])
        wmix_h, wmix_l = sb("wmix_h", [P, 5, D], F32R), sb("wmix_l", [P, 5, D], F32R)
        ahat_h, ahat_l = sb("ahat_h", [P, NT, N], F32R), sb("ahat_l", [P, NT, N], F32R)
        w1raw, w2raw = sb("w1raw", [P, HID]), sb("w2raw", [P, HT, D])
        w1h, w1l = sb("w1h", [P, HID], F32R), sb("w1l", [P, HID], F32R)
        w2h, w2l = sb("w2h", [P, HT, D], F32R), sb("w2l", [P, HT, D], F32R)
        bias0, bias_h, bias_l = sb("bias0", [1, D]), sb("bias_h", [1, D], F32R), sb("bias_l", [1, D], F32R)
        wgs, bihs, bhhs = sb("wgs", [P, 2, D]), sb("bihs", [P, SKIPS, 4]), sb("bhhs", [P, SKIPS, 4])
        bn1s, bn2s = sb("bn1s", [P, 3, HT]), sb("bn2s", [P, 3])
        ones, ones_r = sb("ones", [P, P]), sb("ones_r", [1, P], F32R)
        coef = sb("coef", [P, 4, NT])
        deg = sb("deg", [P, 4, NT])
        dinv = sb("dinv", [P, NT])
        diag = sb("diag", [P, NT, P])
        smax = sb("smax", [P, 4, NT])
        xt = sb("xt", [P, 2, N])
        xth, xtl = sb("xth", [P, 2, N], F32R), sb("xtl", [P, 2, N], F32R)
        mix = sb("mix", [P, 2, NT, D])
        x1 = sb("x1", [P, 2, NT, D])
        x1h, x1l = sb("x1h", [P, NT, D], F32R), sb("x1l", [P, NT, D], F32R)
        aggh, aggl = sb("aggh", [P, N], F32R), sb("aggl", [P, N], F32R)
        z = sb("z", [P, HT, B, N])
        zstats = sb("zstats", [P, HT, B, 6])
        stats, mv, rstd, shift = sb("stats", [P, NT, 6]), sb("mv", [P, 3, NT]), sb("rstd", [P, NT]), sb("shift", [P, NT])
        zmv, sc1, sh1 = sb("zmv", [P, HT, 2]), sb("sc1", [P, HT]), sb("sh1", [P, HT])
        act1 = adjn[:].rearrange("p (q h) n -> p q h n", q=2)
        r_h, r_l = ahat_h[:].rearrange("p (q h) n -> p q h n", q=2), ahat_l[:].rearrange("p (q h) n -> p q h n", q=2)
        o2 = xt
        ostats, omv = sb("ostats", [P, B, 6]), sb("omv", [P, 2])

        asked, rooted = sem("asked"), sem("rooted")
        exponent_ready = sem("exponent_ready")
        c_adj, c_w, c_nv, c_rest, c_again = sem("c_adj"), sem("c_w"), sem("c_nv"), sem("c_rest"), sem("c_again")
        dve1, pe_setup = sem("dve1"), sem("pe_setup")
        logits_ready, max_ready, exp_ready = sem("logits_ready"), sem("max_ready"), sem("exp_ready")
        wmix_ready, wmix_hi, dinv_spread, ahat_ready, ahat_hi = (
            sem(k) for k in ("wmix_ready", "wmix_hi", "dinv_spread", "ahat_ready", "ahat_hi"))
        wsmall_hi, kept_hi = sem("wsmall_hi"), sem("kept_hi")
        weights_ready = sem("weights_ready")
        xt_loaded, xt_hi, xt_lo = [sem("xt_loaded0"), sem("xt_loaded1")], sem("xt_hi"), sem("xt_lo")
        prod_done, scaled, mixed, mix_done = sem("prod_done"), sem("scaled"), sem("mixed"), sem("mix_done")
        shift_ready = sem("shift_ready")
        x1_ready, x1_hi, x1_lo, x1_stored = sem("x1_ready"), sem("x1_hi"), sem("x1_lo"), [sem("x1_stored0"), sem("x1_stored1")]
        agg_done, agg_hi, agg_lo = sem("agg_done"), sem("agg_hi"), sem("agg_lo")
        z_done, z_kept, z_counted = sem("z_done"), sem("z_kept"), sem("z_counted")
        bn1_ready = sem("bn1_ready")
        r_ready, r_hi = sem("r_ready"), sem("r_hi")
        r_lo = [sem("r_lo0"), sem("r_lo1")]
        o2_done, o2_kept, o2_counted, o2_stored = sem("o2_done"), sem("o2_kept"), sem("o2_counted"), [sem("o2_stored0"), sem("o2_stored1")]

        PROD = banks[0:4]
        BASE = banks[4:6]
        AGG = banks[6]
        ZB = [banks[6], banks[7]]

        block = ctx.enter_context(nc.Block())

        def tile(ap, i):
            return ap[:, i * P:(i + 1) * P]

        def stores_before(b, par):
            return 8 * (b - par)

        def phase_a(eng, slot, in_loop=None):
            for b in range(AHEAD):
                slot(b, b % 2, True, b >= 1, b >= 2)
            after = in_loop(None, None) if in_loop else None
            with eng.Fori(0, (B - AHEAD - 1) // 2) as i:
                if in_loop:
                    in_loop(i, after)
                slot(2 * i + AHEAD, 1, True, True, True)
                slot(2 * i + AHEAD + 1, 0, True, True, True)
            if in_loop:
                in_loop((B - AHEAD - 1) // 2, after)
            for b in range(B - 1, B + 2):
                slot(b, b % 2, b < B, b < B + 1, True)

        @block.sync
        def _(sp):
            sp.dma_start(nv1s[:], nv1_t).then_inc(c_nv, 16)
            sp.dma_start(nv2s[:], nv2).then_inc(c_nv, 16)
            sp.dma_start(adjn[:], adj_n).then_inc(c_adj, 16)
            sp.dma_start(xt[:, 0, :], x_t[0]).then_inc(xt_loaded[0], 16)
            sp.dma_start(adjt[:], adj_t).then_inc(c_adj, 16)
            for dst, src in ((w1raw, w1_t), (w2raw, w2_t), (bn1s, bn1), (bn2s, bn2), (wgs, wg), (bihs, bih), (bhhs, bhh)):
                sp.dma_start(dst[:], src).then_inc(c_rest, 16)

            def slot(b, par, now, one, two):
                if now and not (isinstance(b, int) and b == B - 1):
                    need(sp, xt_hi, b)
                    need(sp, xt_lo, b)
                    sp.dma_start(xt[:, 1 - par, :], x_t[b + 1]).then_inc(xt_loaded[1 - par], 16)
                if one:
                    sp.wait_ge(x1_ready, b)
                    sp.dma_start(x1_dram[b - 1], x1[:, 1 - par, :, :].rearrange("p t d -> p (t d)")).then_inc(x1_stored[1 - par], 16)
                if isinstance(b, int) and b == 1:
                    sp.wait_ge(weights_ready, 2)
                    for dst, src in ((adjt[:], adj_t), (adjn[:], wih_t), (logits[:, 0:SKIPS - 1, :], whh_t)):
                        sp.dma_start(dst, src).then_inc(c_again, 16)

            phase_a(sp, slot)

            def spill(b, par):
                sp.wait_ge(o2_kept, b + 1)
                sp.dma_start(o2_dram[b], o2[:, par, :]).then_inc(o2_stored[par], 16)

            with sp.Fori(0, B // 2) as i:
                spill(2 * i, 0)
                spill(2 * i + 1, 1)
            for par in range(2):
                sp.wait_ge(x1_stored[par], 16 * B // 2)
                sp.wait_ge(o2_stored[par], 16 * B // 2)

        @block.gpsimd
        def _(pool):
            roots = Roots(asked, rooted, exponent)
            nc.gpsimd.memset(exponent[:], -0.5).then_inc(exponent_ready, 1)
            pool.wait_ge(exponent_ready, 1)
            roots.answer(nc, pool, dinv[:])

            def split_x(b, par):
                pool.wait_ge(xt_hi, b + 1)
                nc.gpsimd.tensor_tensor(xtl[:, par, :], xt[:, par, :], f32(xth[:, par, :]),
                                        ALU.subtract).then_inc(xt_lo, 1)

            def slot(b, par, now, one, two):
                if one:
                    pool.wait_ge(x1_hi, b)
                    nc.gpsimd.tensor_tensor(x1l[:], x1[:, 1 - par, :, :], f32(x1h[:]), ALU.subtract).then_inc(x1_lo, 1)
                if now and not (isinstance(b, int) and b == B - 1):
                    split_x(b + 1, 1 - par)
                if now:
                    roots.answer(nc, pool, rstd[:])

            def in_loop(i, after):
                if i is not None:
                    roots.base, roots.n = i * 2 + AHEAD + 1, 0

            split_x(0, 0)
            phase_a(pool, slot, in_loop)
            roots.answer(nc, pool, sc1[:])
            pool.wait_ge(kept_hi, 2)
            nc.gpsimd.tensor_tensor(whh_l[:], logits[:, 0:SKIPS - 1, :], f32(whh_h[:]), ALU.subtract)
            nc.gpsimd.tensor_tensor(wg_l[:], wgs[:], f32(wg_h[:]), ALU.subtract)
            nc.gpsimd.tensor_tensor(gate_bias[:], bihs[:], bhhs[:], ALU.add)

            def low_r(b, par):
                pool.wait_ge(r_hi, b + 1)
                need(pool, o2_done, b - 1)
                nc.gpsimd.tensor_tensor(r_l[:, par, 0, :], act1[:, par, 0, :], f32(r_h[:, par, 0, :]),
                                        ALU.subtract).then_inc(r_lo[0], 1)

            low_r(0, 0)
            low_r(1, 1)
            with pool.Fori(1, B // 2) as i:
                low_r(2 * i, 0)
                low_r(2 * i + 1, 1)
            roots.answer(nc, pool, scale2[:])

        @block.scalar
        def _(act):
            act.dma_start(ident[:], eye).then_inc(c_w, 16)
            act.dma_start(wraw[:], l0_w).then_inc(c_w, 16)
            act.dma_start(bias0[:], l0_b).then_inc(c_w, 16)
            act.wait_ge(pe_setup, 1)
            for t in range(NT):
                ins = nc.scalar.activation(logits[:, t, :], banks[t][:], ACT.Relu)
            ins.then_inc(logits_ready, 1)
            act.wait_ge(wmix_ready, 1)
            nc.scalar.copy(wmix_h[:], wmix[:])
            nc.scalar.copy(bias_h[:], bias0[:]).then_inc(wmix_hi, 1)
            act.wait_ge(max_ready, 1)
            for t in range(NT):
                ins = nc.scalar.activation(logits[:, t, :], logits[:, t, :], ACT.Exp, bias=smax[:, 1, t:t + 1],
                                           accum_out=smax[:, 2, t:t + 1])
            ins.then_inc(exp_ready, 1)

            def split_x(b, par):
                act.wait_ge(xt_loaded[par], stores_before(b, par) + 16)
                need(act, prod_done, NT * (b - 1))
                nc.scalar.copy(xth[:, par, :], xt[:, par, :]).then_inc(xt_hi, 1)

            def scale_first(b, par, t):
                act.wait_ge(prod_done, NT * b + t + 1)
                nc.scalar.activation(mix[:, par, t, :], tile(PROD[t][:], 0), ACT.Identity,
                                     scale=coef[:, 0, t:t + 1]).then_inc(scaled, 1)

            def norm(b, par):
                act.wait_ge(shift_ready, b + 1)
                need(act, x1_stored[par], stores_before(b, par))
                need(act, x1_lo, b - 1)
                for t in range(NT):
                    ins = nc.scalar.activation(x1[:, par, t, :], mix[:, par, t, :], ACT.Identity,
                                               scale=rstd[:, t:t + 1], bias=shift[:, t:t + 1])
                ins.then_inc(x1_ready, 1)
                act.wait_ge(x1_ready, b + 1)
                need(act, agg_done, b)
                nc.scalar.copy(x1h[:], x1[:, par, :, :]).then_inc(x1_hi, 1)

            def slot(b, par, now, one, two):
                if two:
                    act.wait_ge(agg_done, b - 1)
                    nc.scalar.copy(aggh[:], AGG[:]).then_inc(agg_hi, 1)
                if now:
                    if isinstance(b, int) and b == 0:
                        act.wait_ge(dinv_spread, 1)
                    scale_first(b, par, 0)
                    scale_first(b, par, 1)
                if one:
                    norm(b - 1, 1 - par)
                if now:
                    scale_first(b, par, 2)
                    scale_first(b, par, 3)
                    if not (isinstance(b, int) and b == B - 1):
                        split_x(b + 1, 1 - par)
                if two:
                    for h in range(HT):
                        act.wait_ge(z_done, HT * (b - 2) + h + 1)
                        nc.scalar.copy(z[:, h, b - 2, :], ZB[h][:]).then_inc(z_kept, 1)
                if isinstance(b, int) and b == 0:
                    act.wait_ge(ahat_ready, 1)
                    nc.scalar.copy(ahat_h[:], adjt[:]).then_inc(ahat_hi, 1)
                    act.wait_ge(c_rest, 16 * 7)
                    nc.scalar.copy(w1h[:], w1raw[:])
                    nc.scalar.copy(w2h[:], w2raw[:]).then_inc(wsmall_hi, 1)
                if isinstance(b, int) and b == 2:
                    act.wait_ge(c_again, 48)
                    nc.scalar.copy(adj_h[:], adjt[:])
                    nc.scalar.copy(wih_h[:], adjn[:]).then_inc(kept_hi, 1)
                    nc.scalar.copy(whh_h[:], logits[:, 0:SKIPS - 1, :])
                    nc.scalar.copy(wg_h[:], wgs[:]).then_inc(kept_hi, 1)

            split_x(0, 0)
            phase_a(act, slot)
            act.wait_ge(bn1_ready, 1)

            def relu(b, par):
                for h in range(HT):
                    need(act, r_lo[h], b - 1)
                for h in range(HT):
                    ins = nc.scalar.activation(act1[:, par, h, :], z[:, h, b, :], ACT.Relu,
                                               bias=sh1[:, h:h + 1], scale=sc1[:, h:h + 1])
                ins.then_inc(r_ready, 1)

            def keep_o2(b, par):
                act.wait_ge(o2_done, b + 1)
                need(act, o2_stored[par], stores_before(b, par))
                need(act, o2_counted, b - 1)
                nc.scalar.copy(o2[:, par, :], banks[par][:]).then_inc(o2_kept, 1)

            relu(0, 0)
            relu(1, 1)
            keep_o2(0, 0)
            relu(2, 0)
            keep_o2(1, 1)
            with act.Fori(1, B // 2 - 1) as i:
                relu(2 * i + 1, 1)
                keep_o2(2 * i, 0)
                relu(2 * i + 2, 0)
                keep_o2(2 * i + 1, 1)
            relu(B - 1, 1)
            keep_o2(B - 2, 0)
            keep_o2(B - 1, 1)

        @block.vector
        def _(dve):
            chain = Chain(dve, dve1)
            roots = Roots(asked, rooted, exponent)
            chain.link(nc.vector.memset(ones[:], 1.0))
            chain.link(nc.vector.tensor_copy(ones_r[:], ones[0:1, :]))
            dve.wait_ge(c_w, 48)
            nc.vector.tensor_tensor(wmix[:, 0, :], wraw[:, 0, :], ident[:], ALU.add)
            nc.vector.tensor_tensor(wmix[:, 1:3, :], wraw[:, 1:3, :], wraw[:, 3:5, :], ALU.add)
            nc.vector.tensor_copy(wmix[:, 3:5, :], wraw[:, 5:7, :]).then_inc(wmix_ready, 1)
            dve.wait_ge(logits_ready, 1)
            chain.link(nc.vector.reduce_max(smax[:, 0, :], logits[:], AX_X))
            nc.vector.tensor_scalar(smax[:, 1, :], smax[:, 0, :], -1.0, None, ALU.mult).then_inc(max_ready, 1)
            dve.wait_ge(wmix_hi, 1)
            nc.vector.tensor_tensor(bias_l[:], bias0[:], f32(bias_h[:]), ALU.subtract)
            nc.vector.tensor_tensor(wmix_l[:], wmix[:], f32(wmix_h[:]), ALU.subtract).then_inc(weights_ready, 1)
            dve.wait_ge(c_adj, 32)
            nc.vector.reduce_sum(coef[:, 0, :], adjn[:], AX_X)
            nc.vector.reduce_sum(deg[:, 0, :], adjt[:], AX_X)
            for t in range(NT):
                ins = nc.vector.tensor_tensor(diag[:, t, :], tile(adjn[:, t, :], t), ident[:], ALU.mult)
            chain.link(ins)
            nc.vector.reduce_sum(deg[:, 1, :], diag[:], AX_X)
            chain.link(nc.vector.tensor_tensor(deg[:, 2, :], coef[:, 0, :], deg[:, 0, :], ALU.add))
            chain.link(nc.vector.tensor_tensor(deg[:, 3, :], deg[:, 2, :], deg[:, 1, :], ALU.subtract))
            roots.ask(dve, nc.vector.tensor_scalar(dinv[:], deg[:, 3, :], 1.0, None, ALU.add))
            for t in range(NT):
                nc.vector.tensor_tensor(tile(adjt[:, t, :], t), tile(adjt[:, t, :], t), ident[:], ALU.add)
                ins = nc.vector.tensor_scalar(diag[:, t, :], ident[:], dinv[:, t:t + 1], None, ALU.mult)
            ins.then_inc(dinv_spread, 1)
            dve.wait_ge(exp_ready, 1)
            chain.link(nc.vector.reciprocal(smax[:, 3, :], smax[:, 2, :]))
            for t in range(NT):
                ins = nc.vector.tensor_scalar(logits[:, t, :], logits[:, t, :], smax[:, 3, t:t + 1], None, ALU.mult)
            chain.link(ins)
            nc.vector.tensor_tensor(coef[:, 1, :], coef[:, 0, :], coef[:, 0, :], ALU.mult)
            chain.link(nc.vector.reduce_sum(coef[:, 2, :], logits[:], AX_X))
            chain.link(nc.vector.tensor_tensor(coef[:, 3, :], coef[:, 2, :], coef[:, 2, :], ALU.mult))

            def ahat():
                dve.wait_ge(pe_setup, 2)
                for t in range(NT):
                    ins = nc.vector.scalar_tensor_tensor(out=adjt[:, t, :], in0=adjt[:, t, :], scalar=dinv[:, t:t + 1],
                                                         in1=banks[7][:], op0=ALU.mult, op1=ALU.mult)
                ins.then_inc(ahat_ready, 1)
                dve.wait_ge(ahat_hi, 1)
                nc.vector.tensor_tensor(ahat_l[:], adjt[:], f32(ahat_h[:]), ALU.subtract)
                dve.wait_ge(wsmall_hi, 1)
                nc.vector.tensor_tensor(w1l[:], w1raw[:], f32(w1h[:]), ALU.subtract)
                nc.vector.tensor_tensor(w2l[:], w2raw[:], f32(w2h[:]), ALU.subtract).then_inc(weights_ready, 1)

            def combine(b, par, first):
                for k in (1, 2, 3):
                    for t in (first, first + 1):
                        if k == 1:
                            dve.wait_ge(scaled, NT * b + t + 1)
                        ins = nc.vector.scalar_tensor_tensor(
                            out=mix[:, par, t, :], in0=tile(PROD[t][:], k), scalar=coef[:, k, t:t + 1],
                            in1=mix[:, par, t, :], op0=ALU.mult, op1=ALU.add)
                    if k < 3:
                        chain.link(ins)
                ins.then_inc(mixed, 1)

            def slot(b, par, now, one, two):
                if one:
                    dve.wait_ge(rooted, b + 1)
                    nc.vector.scalar_tensor_tensor(out=shift[:], in0=mv[:, 0, :], scalar=-1.0, in1=rstd[:],
                                                   op0=ALU.mult, op1=ALU.mult).then_inc(shift_ready, 1)
                if now:
                    combine(b, par, 0)
                if two:
                    dve.wait_ge(agg_hi, b - 1)
                    nc.vector.tensor_tensor(aggl[:], AGG[:], f32(aggh[:]), ALU.subtract).then_inc(agg_lo, 1)
                if now:
                    combine(b, par, 2)
                    dve.wait_ge(mixed, 2 * b + 2)
                    m = mix[:, par, :, :].rearrange("p t d -> p (t d)")
                    nc.vector.tensor_tensor(m, m, BASE[par][:], ALU.add).then_inc(mix_done, 1)
                    dve.wait_ge(mix_done, b + 1)
                    need(dve, x1_ready, b)
                    for t in range(NT):
                        ins = nc.vector.bn_stats(stats[:, t, :], mix[:, par, t, :])
                    chain.link(ins)
                    moments(nc, chain, stats, mv, NT)
                    roots.n += 1
                    nc.vector.tensor_tensor(rstd[:], mv[:, 1, :], mv[:, 2, :], ALU.add).then_inc(asked, 1)
                if isinstance(b, int) and b == 0:
                    ahat()
                if two:
                    for h in range(HT):
                        dve.wait_ge(z_kept, HT * (b - 2) + h + 1)
                        ins = nc.vector.bn_stats(zstats[:, h, b - 2, :], z[:, h, b - 2, :])
                    ins.then_inc(z_counted, 1)
                if isinstance(b, int) and b == 2:
                    dve.wait_ge(kept_hi, 1)
                    nc.vector.tensor_tensor(adj_l[:], adjt[:], f32(adj_h[:]), ALU.subtract)
                    nc.vector.tensor_tensor(wih_l[:], adjn[:], f32(wih_h[:]), ALU.subtract)

            LINKS = 2 * 2 + LN_LINKS

            def in_loop(i, after):
                if i is None:
                    return chain.n
                chain.base, chain.n = i * (2 * LINKS) + after, 0

            phase_a(dve, slot, in_loop)

            roots.base, roots.n = B + 1, 0
            dve.wait_ge(z_counted, B)
            for h in range(HT):
                ins = nc.vector.bn_aggr(zmv[:, h, :], zstats[:, h, :, :].rearrange("p b s -> p (b s)"))
            chain.link(ins)
            nc.vector.tensor_tensor(sh1[:], zmv[:, :, 0], bn1s[:, 0, :], ALU.add)
            roots.ask(dve, nc.vector.tensor_scalar(sc1[:], zmv[:, :, 1], EPS, None, ALU.add))
            nc.vector.tensor_tensor(sh1[:], bn1s[:, 0, :], sh1[:], ALU.subtract)
            chain.link(nc.vector.tensor_tensor(sc1[:], sc1[:], bn1s[:, 1, :], ALU.mult))
            chain.link(nc.vector.tensor_tensor(sh1[:], sh1[:], sc1[:], ALU.mult))
            nc.vector.tensor_tensor(sh1[:], sh1[:], bn1s[:, 2, :], ALU.add).then_inc(bn1_ready, 1)

            def split_r(b, par):
                dve.wait_ge(r_ready, b + 1)
                need(dve, o2_done, b - 1)
                nc.vector.tensor_copy(r_h[:, par, :, :], act1[:, par, :, :]).then_inc(r_hi, 1)
                dve.wait_ge(r_hi, b + 1)
                nc.vector.tensor_tensor(r_l[:, par, 1, :], act1[:, par, 1, :], f32(r_h[:, par, 1, :]),
                                        ALU.subtract).then_inc(r_lo[1], 1)

            def count_o2(b, par):
                dve.wait_ge(o2_kept, b + 1)
                nc.vector.bn_stats(ostats[:, b, :], o2[:, par, :]).then_inc(o2_counted, 1)

            split_r(0, 0)
            split_r(1, 1)
            count_o2(0, 0)
            with dve.Fori(1, B // 2) as i:
                split_r(2 * i, 0)
                count_o2(2 * i - 1, 1)
                split_r(2 * i + 1, 1)
                count_o2(2 * i, 0)
            count_o2(B - 1, 1)
            dve.wait_ge(o2_counted, B)
            chain.link(nc.vector.bn_aggr(omv[:], ostats[:].rearrange("p b s -> p (b s)")))
            nc.vector.tensor_tensor(shift2[:], omv[:, 0:1], bn2s[:, 0:1], ALU.add)
            roots.ask(dve, nc.vector.tensor_scalar(scale2[:], omv[:, 1:2], EPS, None, ALU.add))
            nc.vector.tensor_tensor(shift2[:], bn2s[:, 0:1], shift2[:], ALU.subtract)
            chain.link(nc.vector.tensor_tensor(scale2[:], scale2[:], bn2s[:, 1:2], ALU.mult))
            chain.link(nc.vector.tensor_tensor(shift2[:], shift2[:], scale2[:], ALU.mult))
            chain.link(nc.vector.tensor_tensor(shift2[:], shift2[:], bn2s[:, 2:3], ALU.add))

        @block.tensor
        def _(pe):
            pe.wait_ge(c_nv, 32)
            for t in range(NT):
                mm = pe.matmul(banks[t][:], tile(nv1s[:], t), nv2s[:], start=True, stop=True)
            mm.then_inc(pe_setup, 1)
            pe.wait_ge(dinv_spread, 1)
            for t in range(NT):
                mm = pe.matmul(tile(banks[7][:], t), ones[:], diag[:, t, :], start=True, stop=True)
            mm.then_inc(pe_setup, 1)
            pe.wait_ge(weights_ready, 1)

            def products(b, par, t):
                if t == 0:
                    pe.wait_ge(xt_hi, b + 1)
                    pe.wait_ge(xt_lo, b + 1)
                    need(pe, mix_done, b - 1)
                if t % 2 == 0:
                    need(pe, mixed, 2 * b + t // 2 - 1)
                x = (tile(xth[:, par, :], t), tile(xtl[:, par, :], t))
                wh, wl = wmix_h[:].rearrange("p k d -> p (k d)"), wmix_l[:].rearrange("p k d -> p (k d)")
                base = tile(BASE[par][:], t)
                pe.matmul(base, ones_r[:], bias_h[:], start=True, stop=False)
                pe.matmul(base, ones_r[:], bias_l[:], start=False, stop=False)
                matmul3(pe, base, x, (wh[:, 0:D], wl[:, 0:D]), False, True)
                matmul3(pe, PROD[t][:], x, (wh[:, D:5 * D], wl[:, D:5 * D]), True, True).then_inc(prod_done, 1)

            def slot(b, par, now, one, two):
                if now:
                    for t in range(NT):
                        products(b, par, t)
                if two:
                    if isinstance(b, int) and b == 2:
                        pe.wait_ge(weights_ready, 2)
                    pe.wait_ge(agg_lo, b - 1)
                    for h in range(HT):
                        matmul3(pe, ZB[h][:], (tile(w1h[:], h), tile(w1l[:], h)), (aggh[:], aggl[:]),
                                True, True).then_inc(z_done, 1)
                if one:
                    if isinstance(b, int) and b == 1:
                        pe.wait_ge(weights_ready, 2)
                    pe.wait_ge(x1_lo, b)
                    need(pe, z_kept, HT * (b - 2) + 1)
                    for t in range(NT):
                        mm = matmul3(pe, AGG[:], (x1h[:, t, :], x1l[:, t, :]), (ahat_h[:, t, :], ahat_l[:, t, :]),
                                     t == 0, t == NT - 1)
                    mm.then_inc(agg_done, 1)

            phase_a(pe, slot)

            def second(b, par):
                pe.wait_ge(r_hi, b + 1)
                for h in range(HT):
                    pe.wait_ge(r_lo[h], b + 1)
                need(pe, o2_kept, b - 1)
                for h in range(HT):
                    mm = matmul3(pe, banks[par][:], (w2h[:, h, :], w2l[:, h, :]),
                                 (r_h[:, par, h, :], r_l[:, par, h, :]), h == 0, h == HT - 1)
                mm.then_inc(o2_done, 1)

            second(0, 0)
            second(1, 1)
            with pe.Fori(1, B // 2) as i:
                second(2 * i, 0)
                second(2 * i + 1, 1)


BABY = 3
POWERS = [1, 2, 3, 6]
KS = STEPS + 1


def second_half(nc, sem, banks, ident, exponent, scale2, shift2, adj_n, adj_t, bg0, bg1, alpha, l3_w_t, l3_d,
                fc_w, fc_b, adj_h, adj_l, wih_h, wih_l, whh_h, whh_l, wg_h, wg_l, gate_bias,
                x1_dram, o2_dram, x2_dram, out):
    with ExitStack() as ctx:
        def sb(name, shape, dt=F32):
            return ctx.enter_context(nc.sbuf_tensor(name, shape, dt))

        pow_h = sb("pow_h", [P, len(POWERS), NT, N], F32R)
        pow_l = sb("pow_l", [P, len(POWERS), NT, N], F32R)
        e_h, e_l = sb("e_h", [P, BABY, BABY, D], F32R), sb("e_l", [P, BABY, BABY, D], F32R)
        conv_bias = sb("conv_bias", [P, NT, D])
        rows_bc = sb("rows_bc", [P, N])
        bg1s = sb("bg1s", [P, 1])
        euler_bias = sb("euler_bias", [P, NT, D])
        ident_r = sb("ident_r", [P, P], F32R)
        o2 = sb("o2b", [P, N])
        x1 = sb("x1b", [P, NT, D])
        x2 = sb("x2b", [P, NT, D])
        node_h, node_l = sb("node_h", [P, NT, D], F32R), sb("node_l", [P, NT, D], F32R)
        gat_h, gat_l = sb("gat_h", [P, N], F32R), sb("gat_l", [P, N], F32R)
        pre = sb("pre", [P, N])
        stats, mv, rstd = sb("lstats", [P, NT, 6]), sb("lmv", [P, 3, NT]), sb("lrstd", [P, NT])
        stats8, mv8, rstd8 = sb("stats8", [P, NT * GB, 6]), sb("mv8", [P, 3, NT * GB]), sb("rstd8", [P, NT * GB])
        hh, hl = sb("hh", [P, GB, N], F32R), sb("hl", [P, GB, N], F32R)
        with ExitStack() as early:
            def scratch(name, shape, dt=F32):
                return early.enter_context(nc.sbuf_tensor(name, shape, dt))

            an, at = scratch("an", [P, NT, N]), scratch("at", [P, NT, N])
            nat_h, nat_l = scratch("nat_h", [P, NT, N], F32R), scratch("nat_l", [P, NT, N], F32R)
            ones2 = scratch("ones2", [P, P])
            cols, alphas = scratch("cols", [P, 2, NT]), scratch("alphas", [P, NT])
            diags = scratch("diags", [P, 2, NT, P])
            bg0s = scratch("bg0s", [P, D])
            lw, lws, ld = scratch("lw", [P, D]), scratch("lws", [P, D]), scratch("ld", [P, 1])
            fcw, fcb = scratch("fcw", [P, D]), scratch("fcb", [P, 1])
            bp = scratch("bp", [P, KS, D])
            e = scratch("e", [P, BABY, BABY, D])
            bcols = scratch("bcols", [P, KS, KS])
            vec = scratch("vec", [P, NT, 3])
            vpad = scratch("vpad", [P, BABY, NT, KS])
            vpad_h, vpad_l = scratch("vpad_h", [P, BABY, NT, KS], F32R), scratch("vpad_l", [P, BABY, NT, KS], F32R)
            vec_t = scratch("vec_t", [KS, N])
            bc = scratch("bc", [KS, D])
        gate = [sb(f"gate{i}", [P, N]) for i in range(4)]
        cell, tanc = sb("cell", [P, N]), sb("tanc", [P, N])
        st_h, st_l = sb("st_h", [P, N], F32R), sb("st_l", [P, N], F32R)
        y = sb("y", [P, NT, GB, D])
        x3h, x3l = sb("x3h", [P, NT, D], F32R), sb("x3l", [P, NT, D], F32R)
        th, tl = sb("th", [P, BABY, N], F32R), sb("tl", [P, BABY, N], F32R)
        gh, gl = sb("gh", [P, 2, NT, GB, D], F32R), sb("gl", [P, 2, NT, GB, D], F32R)

        k_adj, k_small = sem("k_adj"), sem("k_small")
        k_bc, k_alpha, cols_ready, lws_ready, bcols_zero, vpad_zero = (
            sem(k) for k in ("k_bc", "k_alpha", "cols_ready", "lws_ready", "bcols_zero", "vpad_zero"))
        weff_done, a_ready, nat_hi, a_hi, k_chain = (sem(k) for k in ("weff_done", "a_ready", "nat_hi", "a_hi", "k_chain"))
        p_done, p_hi, p_lo = sem("p_done"), sem("p_hi"), sem("p_lo")
        b_done, b_kept, v2_done, v_kept, f_done, f_kept = (sem(k) for k in ("b_done", "b_kept", "v2_done", "v_kept", "f_done", "f_kept"))
        e_ready, e_hi, bc_done, vt_done, vt_kept, q_done, constants_ready = (
            sem(k) for k in ("e_ready", "e_hi", "bc_done", "vt_done", "vt_kept", "q_done", "constants_ready"))
        s = {name: sem(name) for name in (
            "front_loaded", "normed2", "o2_turned", "x2_ready", "x2_stored", "x2_hi", "x2_lo", "h1_hi", "h1_lo",
            "gathered", "gat_hi", "gat_lo", "weighted", "pre0_ready", "pre1_ready", "h_hi", "h_ready",
            "gate_sum", "gate_on", "cell_ready", "tanh_ready", "state_ready",
            "y_loaded", "h_turned", "x3_ready", "x3_hi", "x3_lo", "power_done", "power_hi", "power_lo",
            "coef_done", "coef_hi", "coef_lo", "giant_done", "y_summed", "out_ready", "out_stored", "links")}
        front_loaded, normed2, o2_turned, x2_ready, x2_stored = (s[k] for k in ("front_loaded", "normed2", "o2_turned", "x2_ready", "x2_stored"))
        x2_hi, x2_lo, h1_hi, h1_lo, gathered, gat_hi, gat_lo = (s[k] for k in ("x2_hi", "x2_lo", "h1_hi", "h1_lo", "gathered", "gat_hi", "gat_lo"))
        weighted, pre0_ready, pre1_ready, h_hi, h_ready = (s[k] for k in ("weighted", "pre0_ready", "pre1_ready", "h_hi", "h_ready"))
        gate_sum, gate_on, cell_ready, tanh_ready, state_ready = (s[k] for k in ("gate_sum", "gate_on", "cell_ready", "tanh_ready", "state_ready"))
        y_loaded, h_turned, x3_ready, x3_hi, x3_lo = (s[k] for k in ("y_loaded", "h_turned", "x3_ready", "x3_hi", "x3_lo"))
        power_done, power_hi, power_lo, coef_done, coef_hi, coef_lo = (s[k] for k in ("power_done", "power_hi", "power_lo", "coef_done", "coef_hi", "coef_lo"))
        giant_done, y_summed, out_ready, out_stored, links = (s[k] for k in ("giant_done", "y_summed", "out_ready", "out_stored", "links"))

        GATE_BANK = {0: 0, 2: 1, 1: 2, 3: 3}
        FB = banks[4:6]
        UB = banks[6:8]
        out_v = out.rearrange("b (t p) d -> b p t d", p=P)

        def tile(ap, i):
            return ap[:, i * P:(i + 1) * P]

        def flat(ap):
            return ap.rearrange("p t d -> p (t d)")

        def shape_of(c):
            p, t, j = PAIRS[c]
            nw = N // p
            first = next(i for i, q in enumerate(PAIRS) if q[0] == p)
            return p, t, j, nw, (N if j is not None else GB * nw), sum(GATES[:c]), first

        def window(ap, c):
            p, t, j, nw, _, _, _ = shape_of(c)
            return ap[:, j, :] if j is not None else ap[:, :, t:p * (nw - 1) + t + 1:p]

        def flat_like(ap, c):
            _, _, j, nw, n, _, _ = shape_of(c)
            return ap[:, 0:n] if j is not None else ap[:, 0:n].rearrange("p (j w) -> p j w", j=GB)

        FILL = [["turn_0", "x3t_0"], ["powers_0", "gather0_0"], ["weight0_0", "coefs_0"], ["gather1_0", "x3t_1"],
                ["weight1_0", "prep_1", "powers_1"], ["turn_1", "coefs_1"], ["gather0_1"], ["giant_0", "weight0_1"],
                ["giant_1"], ["gather1_1"], ["weight1_1"]]
        L3_NAMES = ("x3t", "powers", "coefs", "giant")
        START = ["prep_0", "const_0", "turn_0", "const_1", "gather0_0", "const_2", "weight0_0", "const_3", "gather1_0",
                 "const_4", "weight1_0", "prep_1", "turn_1", "const_5", "gather0_1", "const_6", "weight0_1", "const_7",
                 "gather1_1", "const_8", "weight1_1"]

        def step(g, cell_step, pieces, lstm, l3, front, last, const):
            if isinstance(g, int) and g == -1:
                for name in START:
                    kind, i = name.split("_")
                    if kind == "const":
                        const(int(i))
                    elif kind in pieces:
                        pieces[kind](g + 1, int(i))
            else:
                if front and "prep" in pieces:
                    pieces["prep"](g + 1, 0)
                for c in range(CELLS):
                    if lstm and cell_step:
                        cell_step(g, c)
                    for name in FILL[c]:
                        kind, i = name.split("_")
                        if kind not in pieces:
                            continue
                        if kind in L3_NAMES:
                            if l3:
                                pieces[kind](g - 1, int(i))
                        elif front:
                            pieces[kind](g + 1, int(i))
            last(g, lstm, front)

        def run(eng, cell_step, pieces, last, const, counters=()):
            step(-1, cell_step, pieces, False, False, True, last, const)
            eng.wait_ge(constants_ready, 2)
            step(0, cell_step, pieces, True, False, True, last, const)
            ahead = [c.n for c, _ in counters]
            with eng.Fori(1, G - 1) as g:
                for (c, per_step), n in zip(counters, ahead):
                    c.base, c.n = (g - 1) * per_step + n, 0
                step(g, cell_step, pieces, True, True, True, last, const)
                assert all(c.n == per_step for c, per_step in counters)
            for (c, per_step), n in zip(counters, ahead):
                c.base, c.n = (G - 2) * per_step + n, 0
            step(G - 1, cell_step, pieces, True, True, False, last, const)
            step(G, cell_step, pieces, False, True, False, last, const)

        LINKS_STEP = 0
        LINKS_STEP += GB * (1 + LN_LINKS)
        LINKS_STEP += sum(1 for _, t, _ in PAIRS if t > 0) + CELLS
        LINKS_STEP += GB * (1 + LN_LINKS)
        LINKS_STEP += LN_LINKS

        ROOTS_STEP = 2 * GB + 1
        asked2, rooted2 = sem("asked2"), sem("rooted2")

        block = ctx.enter_context(nc.Block())

        @block.sync
        def _(sp):
            def prep(g, j):
                n = GB * g + j
                need(sp, x2_ready, n)
                sp.dma_start(o2[:], o2_dram[n]).then_inc(front_loaded, 16)
                sp.dma_start(flat(x1[:]), x1_dram[n]).then_inc(front_loaded, 16)

            def turn(g, j):
                n = GB * g + j
                sp.wait_ge(x2_ready, n + 1)
                sp.dma_start(x2_dram[n], flat(x2[:])).then_inc(x2_stored, 16)

            def giant(g, half):
                if half == 1:
                    sp.wait_ge(out_ready, g + 1)
                    for j in range(GB):
                        sp.dma_start(out_v[GB * g + j], y[:, :, j, :]).then_inc(out_stored, 16)

            def last(g, lstm, front):
                if lstm:
                    need(sp, out_stored, 16 * GB * g)
                    for j in range(GB):
                        n = GB * g + j
                        sp.wait_ge(x2_stored, 16 * (n + 1))
                        sp.dma_start(y[:, :, j, :], x2_dram[n].rearrange("p (t d) -> p t d", d=D)).then_inc(y_loaded, 16)

            def const(i):
                if i == 0:
                    sp.dma_start(an[:], adj_n).then_inc(k_adj, 16)
                    sp.dma_start(at[:], adj_t).then_inc(k_adj, 16)
                    for dst, src in ((alphas, alpha), (lw, l3_w_t), (ld, l3_d), (fcw, fc_w), (fcb, fc_b), (bg0s, bg0), (bg1s, bg1)):
                        sp.dma_start(dst[:], src).then_inc(k_small, 16)

            run(sp, None, {"prep": prep, "turn": turn, "giant": giant}, last, const)
            sp.wait_ge(out_stored, 16 * B)

        @block.gpsimd
        def _(pool):
            roots = Roots(asked2, rooted2, exponent)

            def turn(g, j):
                n = GB * g + j
                roots.answer(nc, pool, rstd[:])
                pool.wait_ge(x2_hi, n + 1)
                nc.gpsimd.tensor_tensor(node_l[:], x2[:], f32(node_h[:]), ALU.subtract).then_inc(x2_lo, 1)

            def x3t(g, j):
                n = GB * g + j
                pool.wait_ge(x3_hi, n + 1)
                nc.gpsimd.tensor_tensor(x3l[:], y[:, :, j, :], f32(x3h[:]), ALU.subtract).then_inc(x3_lo, 1)

            def giant(g, half):
                if half == 1:
                    roots.answer(nc, pool, rstd8[:])

            def last(g, lstm, front):
                if lstm:
                    for j in range(GB):
                        roots.answer(nc, pool, rstd[:])

            def const(i):
                if i == 0:
                    nc.gpsimd.memset(bcols[:], 0.0).then_inc(bcols_zero, 1)
                    nc.gpsimd.memset(vpad[:], 0.0).then_inc(vpad_zero, 1)

            run(pool, None, {"turn": turn, "x3t": x3t, "giant": giant}, last, const, ((roots, ROOTS_STEP),))

        @block.scalar
        def _(act):
            def cell_step(g, c):
                p, t, j, nw, n, before, first = shape_of(c)
                gates = [q for q in (0, 2, 1, 3) if t > 0 or q != 1]
                need(act, cell_ready, CELLS * g + c)
                for i, q in enumerate(gates):
                    act.wait_ge(gate_sum, GATES_ALL * g + before + i + 1)
                    if q in (1, 3):
                        need(act, state_ready, CELLS * g + c)
                    nc.scalar.activation(gate[q][:, 0:n], banks[GATE_BANK[q]][:, 0:n], ACT.Tanh if q == 2 else ACT.Sigmoid,
                                         bias=gate_bias[:, p - 1, q:q + 1]).then_inc(gate_on, 1)
                act.wait_ge(cell_ready, CELLS * g + c + 1)
                nc.scalar.activation(tanc[:, 0:n], cell[:, 0:n], ACT.Tanh).then_inc(tanh_ready, 1)

            def turn(g, j):
                n = GB * g + j
                act.wait_ge(x2_ready, n + 1)
                nc.scalar.copy(node_h[:], x2[:]).then_inc(x2_hi, 1)

            def gather(g, j, conv):
                act.wait_ge(gathered, 2 * (GB * g + j) + conv + 1)
                nc.scalar.copy(gat_h[:], FB[j][:]).then_inc(gat_hi, 1)

            def weight0(g, j):
                act.wait_ge(pre0_ready, GB * g + j + 1)
                nc.scalar.activation(flat(node_h[:]), pre[:], ACT.Relu).then_inc(h1_hi, 1)

            def x3t(g, j):
                n = GB * g + j
                act.wait_ge(x3_ready, n + 1)
                nc.scalar.copy(x3h[:], y[:, :, j, :]).then_inc(x3_hi, 1)
                act.wait_ge(power_done, BABY * n + 1)
                nc.scalar.copy(th[:, 0, :], UB[j][:]).then_inc(power_hi, 1)

            def powers(g, j):
                for k in range(1, BABY):
                    act.wait_ge(power_done, BABY * (GB * g + j) + k + 1)
                    nc.scalar.copy(th[:, k, :], UB[(j + k) % 2][:]).then_inc(power_hi, 1)

            def coefs(g, j):
                for t in range(NT):
                    act.wait_ge(coef_done, NT * (GB * g + j) + t + 1)
                    nc.scalar.copy(gh[:, :, t, j, :], UB[t % 2][:, D:3 * D].rearrange("p (k d) -> p k d", d=D)).then_inc(coef_hi, 1)

            def last(g, lstm, front):
                if front:
                    for j in range(GB):
                        act.wait_ge(pre1_ready, GB * (g + 1) + j + 1)
                        nc.scalar.activation(hh[:, j, :], pre[:], ACT.Relu).then_inc(h_hi, 1)

            def high(dst, first):
                for t in range(NT):
                    act.wait_ge(p_done, first + t + 1)
                    nc.scalar.copy(dst[:, t, :], banks[t][:]).then_inc(p_hi, 1)

            def const(i):
                if i == 0:
                    act.wait_ge(k_small, 16 * 7)
                    nc.scalar.activation(alphas[:], alphas[:], ACT.Sigmoid).then_inc(k_alpha, 1)
                if i == 1:
                    act.wait_ge(a_ready, 1)
                    nc.scalar.copy(nat_h[:], an[:]).then_inc(nat_hi, 1)
                    nc.scalar.copy(pow_h[:, 0, :, :], at[:]).then_inc(a_hi, 1)
                if i == 2:
                    high(pow_h[:, 1, :, :], 0)
                if i == 4:
                    high(pow_h[:, 2, :, :], NT)
                if i == 5:
                    high(nat_h, 2 * NT)
                if i == 6:
                    high(pow_h[:, 3, :, :], 3 * NT)
                if i == 7:
                    act.wait_ge(e_ready, 1)
                    nc.scalar.copy(e_h[:], e[:]).then_inc(e_hi, 1)

            run(act, cell_step, {"turn": turn, "gather0": lambda g, j: gather(g, j, 0), "gather1": lambda g, j: gather(g, j, 1),
                                 "weight0": weight0, "x3t": x3t, "powers": powers, "coefs": coefs}, last, const)

        @block.vector
        def _(dve):
            chain = Chain(dve, links)
            roots = Roots(asked2, rooted2, exponent)

            def cell_step(g, c):
                p, t, j, nw, n, before, first = shape_of(c)
                dve.wait_ge(gate_on, GATES_ALL * g + before + 2)
                if t == 0:
                    need(dve, tanh_ready, CELLS * g + c)
                    nc.vector.tensor_tensor(cell[:, 0:n], gate[0][:, 0:n], gate[2][:, 0:n], ALU.mult).then_inc(cell_ready, 1)
                else:
                    nc.vector.tensor_tensor(gate[0][:, 0:n], gate[0][:, 0:n], gate[2][:, 0:n], ALU.mult)
                    dve.wait_ge(gate_on, GATES_ALL * g + before + 3)
                    chain.link(nc.vector.tensor_tensor(gate[1][:, 0:n], gate[1][:, 0:n], cell[:, 0:n], ALU.mult))
                    nc.vector.tensor_tensor(cell[:, 0:n], gate[0][:, 0:n], gate[1][:, 0:n], ALU.add).then_inc(cell_ready, 1)
                dve.wait_ge(tanh_ready, CELLS * g + c + 1)
                dve.wait_ge(gate_on, GATES_ALL * g + before + GATES[c])
                if t == p - 1:
                    dst_h, dst_l = window(hh, c), window(hl, c)
                else:
                    dst_h, dst_l = flat_like(st_h, c), flat_like(st_l, c)
                o, tc, whole_h = flat_like(gate[3], c), flat_like(tanc, c), flat_like(gate[1], c)
                nc.vector.tensor_tensor(dst_h, o, tc, ALU.mult)
                chain.link(nc.vector.tensor_tensor(whole_h, o, tc, ALU.mult))
                nc.vector.tensor_tensor(dst_l, whole_h, f32(dst_h), ALU.subtract).then_inc(state_ready, 1)

            def prep(g, j):
                dve.wait_ge(front_loaded, 32 * (GB * g + j + 1))
                nc.vector.tensor_scalar(o2[:], o2[:], scale2[:, 0:1], shift2[:, 0:1], ALU.mult, ALU.add).then_inc(normed2, 1)

            def turn(g, j):
                n = GB * g + j
                dve.wait_ge(o2_turned, n + 1)
                need(dve, x2_stored, 16 * n)
                need(dve, x2_lo, n)
                chain.link(nc.vector.tensor_tensor(flat(x2[:]), FB[j][:], flat(x1[:]), ALU.add))
                tiles = [x2[:, t, :] for t in range(NT)]
                layer_norm(nc, dve, chain, roots, tiles, tiles, stats, mv, rstd, NT).then_inc(x2_ready, 1)

            def gather(g, j, conv):
                dve.wait_ge(gat_hi, 2 * (GB * g + j) + conv + 1)
                nc.vector.tensor_tensor(gat_l[:], FB[j][:], f32(gat_h[:]), ALU.subtract).then_inc(gat_lo, 1)

            def weight0(g, j):
                n = GB * g + j
                dve.wait_ge(weighted, 2 * n + 1)
                nc.vector.tensor_tensor(pre[:], FB[j][:], flat(conv_bias[:]), ALU.add).then_inc(pre0_ready, 1)
                dve.wait_ge(h1_hi, n + 1)
                nc.vector.scalar_tensor_tensor(out=flat(node_l[:]), in0=pre[:], scalar=0.0, in1=f32(flat(node_h[:])),
                                               op0=ALU.max, op1=ALU.subtract).then_inc(h1_lo, 1)

            def x3t(g, j):
                n = GB * g + j
                dve.wait_ge(power_hi, BABY * n + 1)
                nc.vector.tensor_tensor(tl[:, 0, :], UB[j][:], f32(th[:, 0, :]), ALU.subtract).then_inc(power_lo, 1)

            def powers(g, j):
                for k in range(1, BABY):
                    dve.wait_ge(power_hi, BABY * (GB * g + j) + k + 1)
                    nc.vector.tensor_tensor(tl[:, k, :], UB[(j + k) % 2][:], f32(th[:, k, :]), ALU.subtract).then_inc(power_lo, 1)

            def coefs(g, j):
                n = GB * g + j
                dve.wait_ge(x3_lo, n + 1)
                for t in range(NT):
                    dve.wait_ge(coef_hi, NT * n + t + 1)
                    nc.vector.tensor_tensor(y[:, t, j, :], UB[t % 2][:, 0:D], euler_bias[:, t, :], ALU.add)
                    nc.vector.tensor_tensor(gl[:, :, t, j, :], UB[t % 2][:, D:3 * D].rearrange("p (k d) -> p k d", d=D),
                                            f32(gh[:, :, t, j, :]), ALU.subtract).then_inc(coef_lo, 1)

            def giant(g, half):
                dve.wait_ge(giant_done, 2 * g + half + 1)
                part = y[:, 2 * half:2 * half + 2, :, :].rearrange("p t j d -> p (t j d)")
                ins = nc.vector.tensor_tensor(part, part, UB[half][:], ALU.add)
                ins.then_inc(y_summed, 1)
                if half == 1:
                    dve.wait_ge(y_summed, 2 * g + 2)
                    tiles = [y[:, t, j, :] for t in range(NT) for j in range(GB)]
                    layer_norm(nc, dve, chain, roots, tiles, tiles, stats8, mv8, rstd8, NT * GB).then_inc(out_ready, 1)

            def last(g, lstm, front):
                if front:
                    for j in range(GB):
                        n = GB * (g + 1) + j
                        dve.wait_ge(weighted, 2 * n + 2)
                        need(dve, h_ready, n)
                        dve.wait_ge(h1_lo, GB * (g + 2))
                        if lstm:
                            dve.wait_ge(h_turned, GB * (g + 1))
                        nc.vector.scalar_tensor_tensor(out=pre[:], in0=rows_bc[:], scalar=bg1s[:, 0:1], in1=FB[j][:],
                                                       op0=ALU.mult, op1=ALU.add).then_inc(pre1_ready, 1)
                        dve.wait_ge(h_hi, n + 1)
                        nc.vector.scalar_tensor_tensor(out=hl[:, j, :], in0=pre[:], scalar=0.0, in1=f32(hh[:, j, :]),
                                                       op0=ALU.max, op1=ALU.subtract).then_inc(h_ready, 1)
                if lstm:
                    for j in range(GB):
                        n = GB * g + j
                        dve.wait_ge(y_loaded, 16 * GB * (g + 1))
                        dve.wait_ge(h_turned, n + 1)
                        chain.link(nc.vector.tensor_tensor(y[:, :, j, :], UB[j][:].rearrange("p (t d) -> p t d", d=D),
                                                           y[:, :, j, :], ALU.add))
                        tiles = [y[:, t, j, :] for t in range(NT)]
                        layer_norm(nc, dve, chain, roots, tiles, tiles, stats, mv, rstd, NT).then_inc(x3_ready, 1)

            own = Chain(dve, k_chain)

            def low(dst, hi, first):
                for t in range(NT):
                    dve.wait_ge(p_hi, first + t + 1)
                    nc.vector.tensor_tensor(dst[:, t, :], banks[t][:], f32(hi[:, t, :]), ALU.subtract).then_inc(p_lo, 1)

            def scale_f(k, bank, m):
                return nc.vector.tensor_scalar(e[:, k % BABY, k // BABY, :], tile(bank[:], m), float(comb(STEPS, k)), None, ALU.mult)

            def const(i):
                if i == 0:
                    nc.vector.memset(ones2[:], 1.0)
                    nc.vector.tensor_copy(ident_r[:], ident[:])
                    nc.vector.tensor_copy(bp[:, 0, :], ident[:])
                    dve.wait_ge(k_adj, 32)
                    own.link(nc.vector.reduce_sum(cols[:, 0, :], an[:], AX_X))
                    dve.wait_ge(k_alpha, 1)
                    own.link(nc.vector.tensor_scalar(cols[:, 1, :], alphas[:], DT * 0.5, None, ALU.mult))
                    for v in range(2):
                        for t in range(NT):
                            ins = nc.vector.tensor_scalar(diags[:, v, t, :], ident[:], cols[:, v, t:t + 1], None, ALU.mult)
                    ins.then_inc(cols_ready, 1)
                    own.link(nc.vector.tensor_scalar(ld[:], ld[:], 0.0, 1.0, ALU.max, ALU.min))
                    nc.vector.tensor_scalar(lws[:], lw[:], ld[:, 0:1], None, ALU.mult).then_inc(lws_ready, 1)
                    for t in range(NT):
                        nc.vector.tensor_tensor(tile(an[:, t, :], t), tile(an[:, t, :], t), ident[:], ALU.subtract)
                        ins = nc.vector.tensor_tensor(tile(at[:, t, :], t), tile(at[:, t, :], t), ident[:], ALU.subtract)
                    own.link(ins)
                    dve.wait_ge(k_bc, 2)
                    nc.vector.tensor_copy(rows_bc[:], banks[0][:])
                    for t in range(NT):
                        nc.vector.tensor_scalar(an[:, t, :], an[:, t, :], cols[:, 1, t:t + 1], None, ALU.mult)
                        ins = nc.vector.tensor_tensor(at[:, t, :], at[:, t, :], banks[1][:], ALU.mult)
                    ins.then_inc(a_ready, 1)
                if i == 1:
                    dve.wait_ge(a_ready, 1)
                    nc.vector.memset(vec[:, :, 0], 1.0)
                    own.link(nc.vector.reduce_sum(vec[:, :, 1], an[:], AX_X))
                    dve.sem_inc(v_kept, 1)
                    dve.wait_ge(nat_hi, 1)
                    nc.vector.tensor_tensor(nat_l[:], an[:], f32(nat_h[:]), ALU.subtract)
                    dve.wait_ge(a_hi, 1)
                    nc.vector.tensor_tensor(pow_l[:, 0, :, :], at[:], f32(pow_h[:, 0, :, :]), ALU.subtract).then_inc(p_lo, 1)
                    for t in range(NT):
                        nc.vector.tensor_scalar(conv_bias[:, t, :], bg0s[:], cols[:, 0, t:t + 1], None, ALU.mult)
                    own.link(nc.vector.tensor_scalar(bp[:, 1, :], ident[:], 1.0 - DT, None, ALU.mult))
                    dve.wait_ge(weff_done, 1)
                    nc.vector.scalar_tensor_tensor(out=bp[:, 1, :], in0=tile(banks[6][:], 0), scalar=DT, in1=bp[:, 1, :],
                                                   op0=ALU.mult, op1=ALU.add).then_inc(b_kept, 1)
                    dve.wait_ge(bcols_zero, 1)
                    for k in range(KS):
                        ins = nc.vector.tensor_scalar(bcols[:, k, k:k + 1], fcb[:], float(comb(STEPS, k)), None, ALU.mult)
                    own.link(ins)
                if i == 2:
                    low(pow_l[:, 1, :, :], pow_h[:, 1, :, :], 0)
                    dve.wait_ge(b_done, 1)
                    nc.vector.tensor_copy(bp[:, 2, :], tile(banks[6][:], 0)).then_inc(b_kept, 1)
                if i == 3:
                    dve.wait_ge(b_done, 2)
                    nc.vector.tensor_copy(bp[:, 3:5, :].rearrange("p k d -> p (k d)"), banks[7][:, 0:2 * D]).then_inc(b_kept, 1)
                    dve.wait_ge(v2_done, 1)
                    own.link(nc.vector.tensor_copy(vec[:, :, 2], banks[6][:, 0:NT]))
                    dve.wait_ge(vpad_zero, 1)
                    for q in range(BABY):
                        ins = nc.vector.tensor_copy(vpad[:, q, :, BABY * q:BABY * (q + 1)], vec[:])
                    own.link(ins)
                    own.link(nc.vector.tensor_copy(vpad_h[:], vpad[:]))
                    nc.vector.tensor_tensor(vpad_l[:], vpad[:], f32(vpad_h[:]), ALU.subtract).then_inc(v_kept, 1)
                if i == 4:
                    low(pow_l[:, 2, :, :], pow_h[:, 2, :, :], NT)
                    dve.wait_ge(b_done, 3)
                    nc.vector.tensor_copy(bp[:, 5:9, :].rearrange("p k d -> p (k d)"), banks[7][:]).then_inc(b_kept, 1)
                if i == 5:
                    low(nat_l, nat_h, 2 * NT)
                    dve.wait_ge(f_done, 1)
                    for m in range(4):
                        ins = scale_f(STEPS - m, banks[6], m)
                    ins.then_inc(f_kept, 1)
                    dve.wait_ge(f_done, 2)
                    for m in range(4):
                        ins = scale_f(4 - m, banks[7], m)
                    ins.then_inc(f_kept, 1)
                    dve.wait_ge(f_done, 3)
                    own.link(scale_f(0, banks[6], 0))
                if i == 6:
                    for j in range(STEPS):
                        for k in range(STEPS - j):
                            ek = e[:, k % BABY, k // BABY, :]
                            factor = DT * comb(j + k, k) + (1.0 if j == 0 and k == 0 else 0.0)
                            ins = nc.vector.scalar_tensor_tensor(out=ek, in0=bp[:, j, :], scalar=factor, in1=ek,
                                                                 op0=ALU.mult, op1=ALU.add)
                        if j < STEPS - 1:
                            own.link(ins)
                    ins.then_inc(e_ready, 1)
                    low(pow_l[:, 3, :, :], pow_h[:, 3, :, :], 3 * NT)
                if i == 7:
                    dve.wait_ge(e_hi, 1)
                    nc.vector.tensor_tensor(e_l[:], e[:], f32(e_h[:]), ALU.subtract)
                    dve.wait_ge(bc_done, 1)
                    nc.vector.tensor_copy(bc[:], banks[7][0:KS, 0:D])
                    dve.wait_ge(vt_done, 1)
                    nc.vector.tensor_copy(vec_t[:], banks[6][0:KS, :]).then_inc(vt_kept, 1)
                if i == 8:
                    dve.wait_ge(q_done, 1)
                    nc.vector.tensor_copy(euler_bias[:].rearrange("p t d -> p (t d)"), banks[7][:]).then_inc(constants_ready, 2)

            run(dve, cell_step, {"prep": prep, "turn": turn, "gather0": lambda g, j: gather(g, j, 0), "gather1": lambda g, j: gather(g, j, 1),
                                 "weight0": weight0, "x3t": x3t, "powers": powers,
                                 "coefs": coefs, "giant": giant}, last, const, ((chain, LINKS_STEP), (roots, ROOTS_STEP)))

        @block.tensor
        def _(pe):
            def cell_step(g, c):
                p, t, j, nw, n, before, first = shape_of(c)
                gates = [q for q in (0, 2, 1, 3) if t > 0 or q != 1]
                if j is not None:
                    pe.wait_ge(h_ready, GB * g + j + 1)
                else:
                    pe.wait_ge(state_ready, CELLS * g + first)
                need(pe, gate_on, GATES_ALL * g + before)
                for q in gates:
                    mm = matmul3(pe, flat_like(banks[GATE_BANK[q]], c), (tile(wih_h[:, p - 1, :], q), tile(wih_l[:, p - 1, :], q)),
                                 (window(hh, c), window(hl, c)), True, t == 0)
                    if t == 0:
                        mm.then_inc(gate_sum, 1)
                if t > 0:
                    pe.wait_ge(state_ready, CELLS * g + c)
                    for q in gates:
                        matmul3(pe, banks[GATE_BANK[q]][:, 0:n], (tile(whh_h[:, p - 2, :], q), tile(whh_l[:, p - 2, :], q)),
                                (st_h[:, 0:n], st_l[:, 0:n]), False, True).then_inc(gate_sum, 1)

            def turn(g, j):
                n = GB * g + j
                pe.wait_ge(normed2, n + 1)
                need(pe, pre1_ready, n - 1)
                for t in range(NT):
                    mm = pe.transpose(tile(FB[j][:], t), tile(o2[:], t), ident[:])
                mm.then_inc(o2_turned, 1)

            def gather(g, j, conv):
                n = GB * g + j
                if conv == 0:
                    pe.wait_ge(x2_lo, n + 1)
                else:
                    pe.wait_ge(h1_lo, n + 1)
                for t in range(NT):
                    mm = matmul3(pe, FB[j][:], (node_h[:, t, :], node_l[:, t, :]), (adj_h[:, t, :], adj_l[:, t, :]),
                                 t == 0, t == NT - 1)
                mm.then_inc(gathered, 1)

            def weight0(g, j):
                pe.wait_ge(gat_lo, 2 * (GB * g + j) + 1)
                for t in range(NT):
                    mm = matmul3(pe, tile(FB[j][:], t), (tile(gat_h[:], t), tile(gat_l[:], t)),
                                 (wg_h[:, 0, :], wg_l[:, 0, :]), True, True)
                mm.then_inc(weighted, 1)

            def weight1(g, j):
                pe.wait_ge(gat_lo, 2 * (GB * g + j) + 2)
                matmul3(pe, FB[j][:], (wg_h[:, 1, :], wg_l[:, 1, :]), (gat_h[:], gat_l[:]), True, True).then_inc(weighted, 1)

            def x3t(g, j):
                n = GB * g + j
                pe.wait_ge(x3_ready, n + 1)
                if j > 0:
                    pe.wait_ge(coef_lo, NT * n)
                for t in range(NT):
                    mm = pe.transpose(tile(UB[j][:], t), y[:, t, j, :], ident[:])
                mm.then_inc(power_done, 1)

            def powers(g, j):
                n = GB * g + j
                pe.wait_ge(x3_lo, n + 1)
                pe.wait_ge(x3_ready, GB * (g + 1))
                for k in range(1, BABY):
                    if j > 0 or k > 1:
                        pe.wait_ge(power_lo, BABY * n + k - 1)
                    for t in range(NT):
                        mm = matmul3(pe, UB[(j + k) % 2][:], (x3h[:, t, :], x3l[:, t, :]),
                                     (pow_h[:, k - 1, t, :], pow_l[:, k - 1, t, :]), t == 0, t == NT - 1)
                    mm.then_inc(power_done, 1)

            def coefs(g, j):
                n = GB * g + j
                pe.wait_ge(power_lo, BABY * (n + 1))
                for t in range(NT):
                    if t >= 2:
                        pe.wait_ge(coef_lo, NT * n + t - 1)
                    for k in range(BABY):
                        mm = matmul3(pe, UB[t % 2][:, 0:3 * D], (tile(th[:, k, :], t), tile(tl[:, k, :], t)),
                                     (e_h[:, k, :, :].rearrange("p a d -> p (a d)"), e_l[:, k, :, :].rearrange("p a d -> p (a d)")),
                                     k == 0, k == BABY - 1)
                    mm.then_inc(coef_done, 1)

            def giant(g, half):
                pe.wait_ge(coef_lo, NT * GB * (g + 1))
                for t in (2 * half, 2 * half + 1):
                    dst = UB[half][:, (t % 2) * GB * D:(t % 2 + 1) * GB * D]
                    for k in range(2):
                        for m in range(NT):
                            mm = matmul3(pe, dst, (tile(pow_h[:, 2 + k, m, :], t), tile(pow_l[:, 2 + k, m, :], t)),
                                         (gh[:, k, m, :, :].rearrange("p j d -> p (j d)"), gl[:, k, m, :, :].rearrange("p j d -> p (j d)")),
                                         k == 0 and m == 0, k == 1 and m == NT - 1)
                mm.then_inc(giant_done, 1)

            def last(g, lstm, front):
                if lstm:
                    pe.wait_ge(state_ready, CELLS * (g + 1))
                    need(pe, y_summed, 2 * g)
                    for j in range(GB):
                        for t in range(NT):
                            pe.matmul(tile(UB[j][:], t), tile(hh[:, j, :], t), ident_r[:], start=True, stop=False)
                            mm = pe.matmul(tile(UB[j][:], t), tile(hl[:, j, :], t), ident_r[:], start=False, stop=True)
                        mm.then_inc(h_turned, 1)

            def bflat(a, b):
                return bp[:, a:b, :].rearrange("p k d -> p (k d)")

            def product(right, first):
                for t in range(NT):
                    for m in range(NT):
                        mm = matmul3(pe, banks[t][:], (tile(nat_h[:, m, :], t), tile(nat_l[:, m, :], t)),
                                     (pow_h[:, right, m, :], pow_l[:, right, m, :]), m == 0, m == NT - 1)
                    mm.then_inc(p_done, 1)

            def const(i):
                if i == 0:
                    pe.wait_ge(cols_ready, 1)
                    for v in range(2):
                        for t in range(NT):
                            mm = pe.matmul(tile(banks[v][:], t), ones2[:], diags[:, v, t, :], start=True, stop=True)
                        mm.then_inc(k_bc, 1)
                    pe.wait_ge(lws_ready, 1)
                    pe.matmul(tile(banks[6][:], 0), lws[:], lw[:], start=True, stop=True).then_inc(weff_done, 1)
                if i == 2:
                    pe.wait_ge(p_lo, 1)
                    product(0, 0)
                    pe.wait_ge(b_kept, 1)
                    pe.matmul(tile(banks[6][:], 0), bp[:, 1, :], bp[:, 1, :], start=True, stop=True).then_inc(b_done, 1)
                if i == 3:
                    pe.wait_ge(b_kept, 2)
                    pe.matmul(banks[7][:, 0:2 * D], bp[:, 2, :], bflat(1, 3), start=True, stop=True).then_inc(b_done, 1)
                    pe.wait_ge(v_kept, 1)
                    for t in range(NT):
                        for m in range(NT):
                            mm = pe.matmul(banks[6][:, t:t + 1], tile(at[:, m, :], t), vec[:, m, 1:2],
                                           start=(m == 0), stop=(m == NT - 1))
                    mm.then_inc(v2_done, 1)
                if i == 4:
                    pe.wait_ge(p_lo, 1 + NT)
                    product(1, NT)
                    pe.wait_ge(b_kept, 3)
                    pe.matmul(banks[7][:], bp[:, 4, :], bflat(1, 5), start=True, stop=True).then_inc(b_done, 1)
                if i == 5:
                    pe.wait_ge(p_lo, 1 + 2 * NT)
                    for t in range(NT):
                        for m in range(NT):
                            pe.matmul(tile(banks[t][:], m), tile(pow_h[:, 2, m, :], t), ident_r[:], start=True, stop=False)
                            mm = pe.matmul(tile(banks[t][:], m), tile(pow_l[:, 2, m, :], t), ident_r[:], start=False, stop=True)
                        mm.then_inc(p_done, 1)
                    pe.wait_ge(v_kept, 2)
                    pe.matmul(banks[6][:], fcw[:], bflat(0, 4), start=True, stop=True).then_inc(f_done, 1)
                    pe.wait_ge(b_kept, 4)
                    pe.matmul(banks[7][:], fcw[:], bflat(4, 8), start=True, stop=True).then_inc(f_done, 1)
                    pe.wait_ge(f_kept, 1)
                    pe.matmul(banks[6][:, 0:D], fcw[:], bflat(8, 9), start=True, stop=True).then_inc(f_done, 1)
                if i == 6:
                    pe.wait_ge(p_lo, 1 + 3 * NT)
                    product(2, 3 * NT)
                if i == 7:
                    pe.wait_ge(f_kept, 2)
                    for k in range(KS):
                        mm = pe.matmul(banks[7][0:KS, 0:D], bcols[:, k, :], bp[:, STEPS - k, :], start=(k == 0), stop=(k == KS - 1))
                    mm.then_inc(bc_done, 1)
                    pe.wait_ge(p_lo, 1 + 4 * NT)
                    for q in (2, 1):
                        for m in range(NT):
                            matmul3(pe, banks[6][0:KS, :], (vpad_h[:, q, m, :], vpad_l[:, q, m, :]),
                                    (pow_h[:, 1 + q, m, :], pow_l[:, 1 + q, m, :]), q == 2 and m == 0, False, skip_group_check=True)
                    for m in range(NT):
                        pe.matmul(tile(banks[6][0:KS, :], m), vpad_h[:, 0, m, :], ident_r[:], start=False, stop=False, skip_group_check=True)
                        mm = pe.matmul(tile(banks[6][0:KS, :], m), vpad_l[:, 0, m, :], ident_r[:], start=False, stop=(m == NT - 1),
                                       skip_group_check=True)
                    mm.then_inc(vt_done, 1)
                if i == 8:
                    pe.wait_ge(vt_kept, 1)
                    for t in range(NT):
                        mm = pe.matmul(tile(banks[7][:], t), tile(vec_t[:], t), bc[:], start=True, stop=True)
                    mm.then_inc(q_done, 1)

            run(pe, cell_step, {"turn": turn, "gather0": lambda g, j: gather(g, j, 0), "gather1": lambda g, j: gather(g, j, 1),
                                "weight0": weight0, "weight1": weight1, "x3t": x3t, "powers": powers,
                                "coefs": coefs, "giant": giant}, last, const)


def kernel(**inputs):
    import numpy as np
    import concourse.bacc as bacc
    from concourse.bass_utils import run_bass_kernel_spmd

    v = {k: np.asarray(a) for k, a in inputs.items()}

    def rows(a):
        return a.reshape(-1, P, a.shape[-1]).transpose(1, 0, 2)

    def column(a):
        return a.reshape(-1, P).T

    laid = [
        ("x_t", v["x"].transpose(0, 2, 1)),
        ("adj_n", rows(v["adj"])),
        ("adj_t", rows(v["adj"].T)),
        ("nv1_t", v["L0_gnn_node_vec1"].T),
        ("nv2", v["L0_gnn_node_vec2"]),
        ("l0_w", rows(v["L0_gnn_W"])),
        ("l0_b", v["L0_gnn_b"][None, :]),
        ("w1_t", v["L1_gnn_W1"].T),
        ("bn1", np.stack([column(v["L1_gnn_" + k]) for k in ("b1", "g1", "be1")], 1)),
        ("w2_t", rows(v["L1_gnn_W2"].T)),
        ("bn2", np.stack([v["L1_gnn_" + k] for k in ("b2", "g2", "be2")], 1)),
        ("wg", np.stack([v["L2_gnn_Wg0"], v["L2_gnn_Wg1"]], 1)),
        ("bg0", np.tile(v["L2_gnn_bg0"], (P, 1))),
        ("bg1", v["L2_gnn_bg1"][:, None]),
        ("wih_t", v["L2_gnn_Wih"].transpose(2, 0, 1)),
        ("whh_t", v["L2_gnn_Whh"][1:].transpose(2, 0, 1)),
        ("bih", v["L2_gnn_bih"].reshape(SKIPS, 4, P).transpose(2, 0, 1)),
        ("bhh", v["L2_gnn_bhh"].reshape(SKIPS, 4, P).transpose(2, 0, 1)),
        ("alpha", column(v["L3_gnn_alpha_train"])),
        ("l3_w_t", v["L3_gnn_w"].T),
        ("l3_d", v["L3_gnn_d"][:, None]),
        ("fc_w", v["L3_gnn_fc_in_w"]),
        ("fc_b", v["L3_gnn_fc_in_b"][:, None]),
        ("eye", np.eye(P, dtype=np.float32)),
    ]
    nc = bacc.Bacc("TRN2", target_bir_lowering=False, num_devices=1)
    arrays, args = {}, []
    for name, a in laid:
        a = np.ascontiguousarray(a)
        arrays[f"in_{name}_dram"] = a
        args.append(nc.dram_tensor(f"in_{name}_dram", a.shape, mybir.dt.from_np(a.dtype), kind="ExternalInput").ap())
    args.append(nc.dram_tensor("out_dram", (B, N, D), F32, kind="ExternalOutput").ap())
    program(nc, *args)
    r = run_bass_kernel_spmd(nc, [arrays], core_ids=[0])
    return r.results[0]["out_dram"]
```

```python
from contextlib import ExitStack
from math import comb

import concourse.bass as bass
from concourse import mybir

F32 = mybir.dt.float32
F32R = mybir.dt.float32r
ALU = mybir.AluOpType
ACT = mybir.ActivationFunctionType
AX_X = mybir.AxisListType.X

P = 128
B = 16
N = 512
D = 128
NT = N // P
HID = 256
HT = HID // P
SKIPS = 4
GB = 2
G = B // GB
STEPS = 8
DT = 1.0 / STEPS
EPS = 1e-5
PAIRS = [(p, t, j) for p in range(1, SKIPS + 1) for t in range(p) for j in (range(GB) if p == 1 else [None])]
CELLS = len(PAIRS)
GATES = [3 if t == 0 else 4 for _, t, _ in PAIRS]
GATES_ALL = sum(GATES)


def need(eng, sem, value):
    if isinstance(value, int) and value <= 0:
        return
    eng.wait_ge(sem, value)


class Chain:

    def __init__(self, eng, sem):
        self.eng, self.sem, self.base, self.n = eng, sem, 0, 0

    def link(self, ins):
        self.n += 1
        ins.then_inc(self.sem, 1)
        self.eng.wait_ge(self.sem, self.base + self.n)


def f32(ap):
    return ap.bitcast(F32)


def program(nc, x_t, adj_n, adj_t, nv1_t, nv2, l0_w, l0_b, w1_t, bn1, w2_t, bn2, wg, bg0, bg1,
            wih_t, whh_t, bih, bhh, alpha, l3_w_t, l3_d, fc_w, fc_b, eye, out):
    o2_dram = nc.dram_tensor("o2_spill", (B, P, N), F32, kind="Internal").ap()
    x1_dram = nc.dram_tensor("x1_spill", (B, P, N), F32, kind="Internal").ap()
    x2_dram = nc.dram_tensor("x2_spill", (B, P, N), F32, kind="Internal").ap()
    with ExitStack() as whole:
        def sem(name):
            return whole.enter_context(nc.semaphore(name))

        def sb(name, shape, dt=F32):
            return whole.enter_context(nc.sbuf_tensor(name, shape, dt))

        exponent = whole.enter_context(nc.sbuf_tensor("exponent", [P, 8], F32))
        banks = [whole.enter_context(nc.psum_tensor(f"bank{i}", [P, 512], F32)) for i in range(8)]
        ident = whole.enter_context(nc.sbuf_tensor("ident", [P, P], F32))
        scale2 = whole.enter_context(nc.sbuf_tensor("scale2", [P, 1], F32))
        shift2 = whole.enter_context(nc.sbuf_tensor("shift2", [P, 1], F32))
        adj_h, adj_l = sb("adj_h", [P, NT, N], F32R), sb("adj_l", [P, NT, N], F32R)
        wih_h, wih_l = sb("wih_h", [P, SKIPS, 4 * D], F32R), sb("wih_l", [P, SKIPS, 4 * D], F32R)
        whh_h, whh_l = sb("whh_h", [P, SKIPS - 1, 4 * D], F32R), sb("whh_l", [P, SKIPS - 1, 4 * D], F32R)
        wg_h, wg_l = sb("wg_h", [P, 2, D], F32R), sb("wg_l", [P, 2, D], F32R)
        gate_bias = sb("gate_bias", [P, SKIPS, 4])
        row_sums = sb("row_sums", [P, NT])
        first_half(nc, sem, banks, ident, exponent, scale2, shift2, x_t, adj_n, adj_t, nv1_t, nv2, l0_w, l0_b,
                   w1_t, bn1, w2_t, bn2, eye, wg, wih_t, whh_t, bih, bhh, adj_h, adj_l, wih_h, wih_l, whh_h, whh_l,
                   wg_h, wg_l, gate_bias, row_sums, x1_dram, o2_dram)
        second_half(nc, sem, banks, ident, exponent, scale2, shift2, adj_n, adj_t, bg0, bg1, alpha, l3_w_t, l3_d,
                    fc_w, fc_b, adj_h, adj_l, wih_h, wih_l, whh_h, whh_l, wg_h, wg_l, gate_bias, row_sums,
                    x1_dram, o2_dram, x2_dram, out)


class Roots:

    def __init__(self, asked, rooted, exponent):
        self.asked, self.rooted, self.exponent, self.base, self.n = asked, rooted, exponent, 0, 0

    def ask(self, dve, ins):
        self.n += 1
        ins.then_inc(self.asked, 1)
        dve.wait_ge(self.rooted, self.base + self.n)

    def answer(self, nc, pool, ap):
        self.n += 1
        pool.wait_ge(self.asked, self.base + self.n)
        nc.gpsimd.tensor_tensor(ap, ap, self.exponent[:, 0:ap.shape[-1]], ALU.pow).then_inc(self.rooted, 1)


def moments(nc, chain, stats, mv, tiles):
    even, odd = stats[:, 0:tiles, 0:3], stats[:, 0:tiles, 3:6]
    nc.vector.tensor_tensor(mv[:, 0, :], even[:, :, 1], odd[:, :, 1], ALU.add)
    nc.vector.tensor_tensor(mv[:, 1, :], even[:, :, 1], odd[:, :, 1], ALU.subtract)
    chain.link(nc.vector.tensor_tensor(mv[:, 2, :], even[:, :, 2], odd[:, :, 2], ALU.add))
    nc.vector.tensor_scalar(mv[:, 0, :], mv[:, 0, :], 0.5, None, ALU.mult)
    nc.vector.tensor_scalar(mv[:, 2, :], mv[:, 2, :], 1.0 / D, EPS, ALU.mult, ALU.add)
    chain.link(nc.vector.scalar_tensor_tensor(out=mv[:, 1, :], in0=mv[:, 1, :], scalar=0.25, in1=mv[:, 1, :],
                                              op0=ALU.mult, op1=ALU.mult))


def layer_norm(nc, dve, chain, roots, src, dst, stats, mv, rstd, tiles):
    for i in range(tiles):
        ins = nc.vector.bn_stats(stats[:, i, :], src[i])
    chain.link(ins)
    moments(nc, chain, stats, mv, tiles)
    roots.ask(dve, nc.vector.tensor_tensor(rstd[:, 0:tiles], mv[:, 1, :], mv[:, 2, :], ALU.add))
    for i in range(tiles):
        ins = nc.vector.tensor_scalar(dst[i], src[i], mv[:, 0, i:i + 1], rstd[:, i:i + 1], ALU.subtract, ALU.mult)
    return ins


class Norm:

    def __init__(self, sb, name, tiles):
        self.tiles = tiles
        self.stats, self.mv = sb(name + "_stats", [P, tiles, 6]), sb(name + "_mv", [P, 3, tiles])
        self.rstd, self.shift = sb(name + "_rstd", [P, tiles]), sb(name + "_shift", [P, tiles])


LN_LINKS = 3
AHEAD = 3


def matmul3(pe, dst, lhs, rhs, start, stop, **kw):
    (lh, ll), (rh, rl) = lhs, rhs
    pe.matmul(dst, lh, rh, start=start, stop=False, **kw)
    pe.matmul(dst, lh, rl, start=False, stop=False, **kw)
    return pe.matmul(dst, ll, rh, start=False, stop=stop, **kw)


def first_half(nc, sem, banks, ident, exponent, scale2, shift2, x_t, adj_n, adj_t, nv1_t, nv2, l0_w, l0_b,
               w1_t, bn1, w2_t, bn2, eye, wg, wih_t, whh_t, bih, bhh, adj_h, adj_l, wih_h, wih_l, whh_h, whh_l,
               wg_h, wg_l, gate_bias, row_sums, x1_dram, o2_dram):
    RANK = nv2.shape[0]
    with ExitStack() as ctx:
        def sb(name, shape, dt=F32):
            return ctx.enter_context(nc.sbuf_tensor(name, shape, dt))

        adjn = sb("adjn", [P, NT, N])
        adjt = sb("adjt", [P, NT, N])
        logits = sb("logits", [P, NT, N])
        nv1s = sb("nv1s", [RANK, N])
        nv2s = sb("nv2s", [RANK, N])
        wraw = sb("wraw", [P, 7, D])
        wmix = sb("wmix", [P, 5, D])
        wmix_h, wmix_l = sb("wmix_h", [P, 5, D], F32R), sb("wmix_l", [P, 5, D], F32R)
        ahat_h, ahat_l = sb("ahat_h", [P, NT, N], F32R), sb("ahat_l", [P, NT, N], F32R)
        w1raw, w2raw = sb("w1raw", [P, HID]), sb("w2raw", [P, HT, D])
        w1h, w1l = sb("w1h", [P, HID], F32R), sb("w1l", [P, HID], F32R)
        w2h, w2l = sb("w2h", [P, HT, D], F32R), sb("w2l", [P, HT, D], F32R)
        bias0, bias_h, bias_l = sb("bias0", [1, D]), sb("bias_h", [1, D], F32R), sb("bias_l", [1, D], F32R)
        wgs, bihs, bhhs = sb("wgs", [P, 2, D]), sb("bihs", [P, SKIPS, 4]), sb("bhhs", [P, SKIPS, 4])
        bn1s, bn2s = sb("bn1s", [P, 3, HT]), sb("bn2s", [P, 3])
        ones, ones_r = sb("ones", [P, P]), sb("ones_r", [1, P], F32R)
        coef = sb("coef", [P, 4, NT])
        deg = sb("deg", [P, 4, NT])
        dinv = sb("dinv", [P, NT])
        diag = sb("diag", [P, NT, P])
        smax = sb("smax", [P, 4, NT])
        xt = sb("xt", [P, 2, N])
        xth, xtl = sb("xth", [P, 2, N], F32R), sb("xtl", [P, 2, N], F32R)
        mix = sb("mix", [P, 2, NT, D])
        x1 = sb("x1", [P, 2, NT, D])
        x1h, x1l = sb("x1h", [P, NT, D], F32R), sb("x1l", [P, NT, D], F32R)
        aggh, aggl = sb("aggh", [P, N], F32R), sb("aggl", [P, N], F32R)
        z = sb("z", [P, HT, B, N])
        zstats = sb("zstats", [P, HT, B, 6])
        stats, mv, rstd, shift = sb("stats", [P, NT, 6]), sb("mv", [P, 3, NT]), sb("rstd", [P, NT]), sb("shift", [P, NT])
        zmv, sc1, sh1 = sb("zmv", [P, HT, 2]), sb("sc1", [P, HT]), sb("sh1", [P, HT])
        act1 = adjn[:].rearrange("p (q h) n -> p q h n", q=2)
        r_h, r_l = ahat_h[:].rearrange("p (q h) n -> p q h n", q=2), ahat_l[:].rearrange("p (q h) n -> p q h n", q=2)
        o2 = xt
        ostats, omv = sb("ostats", [P, B, 6]), sb("omv", [P, 2])

        asked, rooted = sem("asked"), sem("rooted")
        exponent_ready = sem("exponent_ready")
        c_adj, c_w, c_nv, c_rest, c_again = sem("c_adj"), sem("c_w"), sem("c_nv"), sem("c_rest"), sem("c_again")
        dve1, pe_setup = sem("dve1"), sem("pe_setup")
        logits_ready, max_ready, exp_ready = sem("logits_ready"), sem("max_ready"), sem("exp_ready")
        wmix_ready, wmix_hi, dinv_spread, ahat_ready, ahat_hi = (
            sem(k) for k in ("wmix_ready", "wmix_hi", "dinv_spread", "ahat_ready", "ahat_hi"))
        wsmall_hi, kept_hi = sem("wsmall_hi"), sem("kept_hi")
        weights_ready = sem("weights_ready")
        xt_loaded, xt_hi, xt_lo = [sem("xt_loaded0"), sem("xt_loaded1")], sem("xt_hi"), sem("xt_lo")
        prod_done, scaled, mixed, mix_done = sem("prod_done"), sem("scaled"), sem("mixed"), sem("mix_done")
        shift_ready = sem("shift_ready")
        x1_ready, x1_hi, x1_lo, x1_stored = sem("x1_ready"), sem("x1_hi"), sem("x1_lo"), [sem("x1_stored0"), sem("x1_stored1")]
        agg_done, agg_hi, agg_lo = sem("agg_done"), sem("agg_hi"), sem("agg_lo")
        z_done, z_kept, z_counted = sem("z_done"), sem("z_kept"), sem("z_counted")
        bn1_ready = sem("bn1_ready")
        r_ready, r_hi = sem("r_ready"), sem("r_hi")
        r_lo = [sem("r_lo0"), sem("r_lo1")]
        o2_done, o2_kept, o2_counted, o2_stored = sem("o2_done"), sem("o2_kept"), sem("o2_counted"), [sem("o2_stored0"), sem("o2_stored1")]

        PROD = banks[0:4]
        BASE = banks[4:6]
        AGG = banks[6]
        ZB = [banks[6], banks[7]]

        block = ctx.enter_context(nc.Block())

        def tile(ap, i):
            return ap[:, i * P:(i + 1) * P]

        def stores_before(b, par):
            return 8 * (b - par)

        def phase_a(eng, slot, in_loop=None):
            for b in range(AHEAD):
                slot(b, b % 2, True, b >= 1, b >= 2)
            after = in_loop(None, None) if in_loop else None
            with eng.Fori(0, (B - AHEAD - 1) // 2) as i:
                if in_loop:
                    in_loop(i, after)
                slot(2 * i + AHEAD, 1, True, True, True)
                slot(2 * i + AHEAD + 1, 0, True, True, True)
            if in_loop:
                in_loop((B - AHEAD - 1) // 2, after)
            for b in range(B - 1, B + 2):
                slot(b, b % 2, b < B, b < B + 1, True)

        @block.sync
        def _(sp):
            sp.dma_start(nv1s[:], nv1_t).then_inc(c_nv, 16)
            sp.dma_start(nv2s[:], nv2).then_inc(c_nv, 16)
            sp.dma_start(adjn[:], adj_n).then_inc(c_adj, 16)
            sp.dma_start(xt[:, 0, :], x_t[0]).then_inc(xt_loaded[0], 16)
            sp.dma_start(adjt[:], adj_t).then_inc(c_adj, 16)
            for dst, src in ((w1raw, w1_t), (w2raw, w2_t), (bn1s, bn1), (bn2s, bn2), (wgs, wg), (bihs, bih), (bhhs, bhh)):
                sp.dma_start(dst[:], src).then_inc(c_rest, 16)

            def slot(b, par, now, one, two):
                if now and not (isinstance(b, int) and b == B - 1):
                    need(sp, xt_hi, b)
                    need(sp, xt_lo, b)
                    sp.dma_start(xt[:, 1 - par, :], x_t[b + 1]).then_inc(xt_loaded[1 - par], 16)
                if one:
                    sp.wait_ge(x1_ready, b)
                    sp.dma_start(x1_dram[b - 1], x1[:, 1 - par, :, :].rearrange("p t d -> p (t d)")).then_inc(x1_stored[1 - par], 16)
                if isinstance(b, int) and b == 1:
                    sp.wait_ge(weights_ready, 2)
                    for dst, src in ((adjt[:], adj_t), (adjn[:], wih_t), (logits[:, 0:SKIPS - 1, :], whh_t)):
                        sp.dma_start(dst, src).then_inc(c_again, 16)

            phase_a(sp, slot)

            def spill(b, par):
                sp.wait_ge(o2_kept, b + 1)
                sp.dma_start(o2_dram[b], o2[:, par, :]).then_inc(o2_stored[par], 16)

            with sp.Fori(0, B // 2) as i:
                spill(2 * i, 0)
                spill(2 * i + 1, 1)
            for par in range(2):
                sp.wait_ge(x1_stored[par], 16 * B // 2)
                sp.wait_ge(o2_stored[par], 16 * B // 2)

        @block.gpsimd
        def _(pool):
            roots = Roots(asked, rooted, exponent)
            nc.gpsimd.memset(exponent[:], -0.5).then_inc(exponent_ready, 1)
            pool.wait_ge(exponent_ready, 1)

            def split_x(b, par):
                pool.wait_ge(xt_hi, b + 1)
                nc.gpsimd.tensor_tensor(xtl[:, par, :], xt[:, par, :], f32(xth[:, par, :]),
                                        ALU.subtract).then_inc(xt_lo, 1)

            def slot(b, par, now, one, two):
                if one:
                    pool.wait_ge(x1_hi, b)
                    nc.gpsimd.tensor_tensor(x1l[:], x1[:, 1 - par, :, :], f32(x1h[:]), ALU.subtract).then_inc(x1_lo, 1)
                if now and not (isinstance(b, int) and b == B - 1):
                    split_x(b + 1, 1 - par)
                if now:
                    roots.answer(nc, pool, rstd[:])

            def in_loop(i, after):
                if i is not None:
                    roots.base, roots.n = i * 2 + AHEAD + 1, 0

            split_x(0, 0)
            roots.answer(nc, pool, dinv[:])
            phase_a(pool, slot, in_loop)
            roots.answer(nc, pool, sc1[:])
            pool.wait_ge(kept_hi, 2)
            nc.gpsimd.tensor_tensor(whh_l[:], logits[:, 0:SKIPS - 1, :], f32(whh_h[:]), ALU.subtract)
            nc.gpsimd.tensor_tensor(wg_l[:], wgs[:], f32(wg_h[:]), ALU.subtract)
            nc.gpsimd.tensor_tensor(gate_bias[:], bihs[:], bhhs[:], ALU.add)

            def low_r(b, par):
                pool.wait_ge(r_hi, b + 1)
                need(pool, o2_done, b - 1)
                nc.gpsimd.tensor_tensor(r_l[:, par, 0, :], act1[:, par, 0, :], f32(r_h[:, par, 0, :]),
                                        ALU.subtract).then_inc(r_lo[0], 1)

            low_r(0, 0)
            low_r(1, 1)
            with pool.Fori(1, B // 2) as i:
                low_r(2 * i, 0)
                low_r(2 * i + 1, 1)
            roots.answer(nc, pool, scale2[:])

        @block.scalar
        def _(act):
            act.dma_start(ident[:], eye).then_inc(c_w, 16)
            act.dma_start(wraw[:], l0_w).then_inc(c_w, 16)
            act.dma_start(bias0[:], l0_b).then_inc(c_w, 16)
            act.wait_ge(pe_setup, 1)
            for t in range(NT):
                ins = nc.scalar.activation(logits[:, t, :], banks[t][:], ACT.Relu)
            ins.then_inc(logits_ready, 1)
            act.wait_ge(wmix_ready, 1)
            nc.scalar.copy(wmix_h[:], wmix[:])
            nc.scalar.copy(bias_h[:], bias0[:]).then_inc(wmix_hi, 1)

            def split_x(b, par):
                act.wait_ge(xt_loaded[par], stores_before(b, par) + 16)
                need(act, prod_done, NT * (b - 1))
                nc.scalar.copy(xth[:, par, :], xt[:, par, :]).then_inc(xt_hi, 1)

            split_x(0, 0)
            act.wait_ge(max_ready, 1)
            for t in range(NT):
                ins = nc.scalar.activation(logits[:, t, :], logits[:, t, :], ACT.Exp, bias=smax[:, 1, t:t + 1],
                                           accum_out=smax[:, 2, t:t + 1])
            ins.then_inc(exp_ready, 1)

            def scale_first(b, par, t):
                act.wait_ge(prod_done, NT * b + t + 1)
                nc.scalar.activation(mix[:, par, t, :], tile(PROD[t][:], 0), ACT.Identity,
                                     scale=coef[:, 0, t:t + 1]).then_inc(scaled, 1)

            def norm(b, par):
                act.wait_ge(shift_ready, b + 1)
                need(act, x1_stored[par], stores_before(b, par))
                need(act, x1_lo, b - 1)
                for t in range(NT):
                    ins = nc.scalar.activation(x1[:, par, t, :], mix[:, par, t, :], ACT.Identity,
                                               scale=rstd[:, t:t + 1], bias=shift[:, t:t + 1])
                ins.then_inc(x1_ready, 1)
                act.wait_ge(x1_ready, b + 1)
                need(act, agg_done, b)
                nc.scalar.copy(x1h[:], x1[:, par, :, :]).then_inc(x1_hi, 1)

            def slot(b, par, now, one, two):
                if two:
                    act.wait_ge(agg_done, b - 1)
                    nc.scalar.copy(aggh[:], AGG[:]).then_inc(agg_hi, 1)
                if now:
                    if isinstance(b, int) and b == 0:
                        act.wait_ge(dinv_spread, 1)
                    scale_first(b, par, 0)
                    scale_first(b, par, 1)
                if one:
                    norm(b - 1, 1 - par)
                if now:
                    scale_first(b, par, 2)
                    scale_first(b, par, 3)
                    if not (isinstance(b, int) and b == B - 1):
                        split_x(b + 1, 1 - par)
                if two:
                    for h in range(HT):
                        act.wait_ge(z_done, HT * (b - 2) + h + 1)
                        nc.scalar.copy(z[:, h, b - 2, :], ZB[h][:]).then_inc(z_kept, 1)
                if isinstance(b, int) and b == 0:
                    act.wait_ge(ahat_ready, 1)
                    nc.scalar.copy(ahat_h[:], adjt[:]).then_inc(ahat_hi, 1)
                    act.wait_ge(c_rest, 16 * 7)
                    nc.scalar.copy(w1h[:], w1raw[:])
                    nc.scalar.copy(w2h[:], w2raw[:]).then_inc(wsmall_hi, 1)
                if isinstance(b, int) and b == 2:
                    act.wait_ge(c_again, 48)
                    nc.scalar.copy(adj_h[:], adjt[:])
                    nc.scalar.copy(wih_h[:], adjn[:]).then_inc(kept_hi, 1)
                    nc.scalar.copy(whh_h[:], logits[:, 0:SKIPS - 1, :])
                    nc.scalar.copy(wg_h[:], wgs[:]).then_inc(kept_hi, 1)

            phase_a(act, slot)
            act.wait_ge(bn1_ready, 1)

            def relu(b, par):
                for h in range(HT):
                    need(act, r_lo[h], b - 1)
                for h in range(HT):
                    ins = nc.scalar.activation(act1[:, par, h, :], z[:, h, b, :], ACT.Relu,
                                               bias=sh1[:, h:h + 1], scale=sc1[:, h:h + 1])
                ins.then_inc(r_ready, 1)

            def keep_o2(b, par):
                act.wait_ge(o2_done, b + 1)
                need(act, o2_stored[par], stores_before(b, par))
                need(act, o2_counted, b - 1)
                nc.scalar.copy(o2[:, par, :], banks[par][:]).then_inc(o2_kept, 1)

            relu(0, 0)
            relu(1, 1)
            relu(2, 0)
            keep_o2(0, 0)
            relu(3, 1)
            keep_o2(1, 1)
            with act.Fori(1, B // 2 - 1) as i:
                relu(2 * i + 2, 0)
                keep_o2(2 * i, 0)
                relu(2 * i + 3, 1)
                keep_o2(2 * i + 1, 1)
            keep_o2(B - 2, 0)
            keep_o2(B - 1, 1)

        @block.vector
        def _(dve):
            chain = Chain(dve, dve1)
            roots = Roots(asked, rooted, exponent)
            chain.link(nc.vector.memset(ones[:], 1.0))
            chain.link(nc.vector.tensor_copy(ones_r[:], ones[0:1, :]))
            dve.wait_ge(c_w, 48)
            nc.vector.tensor_tensor(wmix[:, 0, :], wraw[:, 0, :], ident[:], ALU.add)
            nc.vector.tensor_tensor(wmix[:, 1:3, :], wraw[:, 1:3, :], wraw[:, 3:5, :], ALU.add)
            nc.vector.tensor_copy(wmix[:, 3:5, :], wraw[:, 5:7, :]).then_inc(wmix_ready, 1)
            dve.wait_ge(logits_ready, 1)
            chain.link(nc.vector.reduce_max(smax[:, 0, :], logits[:], AX_X))
            nc.vector.tensor_scalar(smax[:, 1, :], smax[:, 0, :], -1.0, None, ALU.mult).then_inc(max_ready, 1)
            dve.wait_ge(wmix_hi, 1)
            nc.vector.tensor_tensor(bias_l[:], bias0[:], f32(bias_h[:]), ALU.subtract)
            nc.vector.tensor_tensor(wmix_l[:], wmix[:], f32(wmix_h[:]), ALU.subtract).then_inc(weights_ready, 1)
            dve.wait_ge(c_adj, 32)
            nc.vector.reduce_sum(coef[:, 0, :], adjn[:], AX_X)
            nc.vector.reduce_sum(deg[:, 0, :], adjt[:], AX_X)
            for t in range(NT):
                ins = nc.vector.tensor_tensor(diag[:, t, :], tile(adjn[:, t, :], t), ident[:], ALU.mult)
            chain.link(ins)
            nc.vector.tensor_copy(row_sums[:], coef[:, 0, :])
            nc.vector.reduce_sum(deg[:, 1, :], diag[:], AX_X)
            chain.link(nc.vector.tensor_tensor(deg[:, 2, :], coef[:, 0, :], deg[:, 0, :], ALU.add))
            chain.link(nc.vector.tensor_tensor(deg[:, 3, :], deg[:, 2, :], deg[:, 1, :], ALU.subtract))
            roots.ask(dve, nc.vector.tensor_scalar(dinv[:], deg[:, 3, :], 1.0, None, ALU.add))
            for t in range(NT):
                nc.vector.tensor_tensor(tile(adjt[:, t, :], t), tile(adjt[:, t, :], t), ident[:], ALU.add)
                ins = nc.vector.tensor_scalar(diag[:, t, :], ident[:], dinv[:, t:t + 1], None, ALU.mult)
            ins.then_inc(dinv_spread, 1)
            dve.wait_ge(exp_ready, 1)
            chain.link(nc.vector.reciprocal(smax[:, 3, :], smax[:, 2, :]))
            for t in range(NT):
                ins = nc.vector.tensor_scalar(logits[:, t, :], logits[:, t, :], smax[:, 3, t:t + 1], None, ALU.mult)
            chain.link(ins)
            nc.vector.tensor_tensor(coef[:, 1, :], coef[:, 0, :], coef[:, 0, :], ALU.mult)
            chain.link(nc.vector.reduce_sum(coef[:, 2, :], logits[:], AX_X))
            chain.link(nc.vector.tensor_tensor(coef[:, 3, :], coef[:, 2, :], coef[:, 2, :], ALU.mult))

            def ahat():
                dve.wait_ge(pe_setup, 2)
                for t in range(NT):
                    ins = nc.vector.scalar_tensor_tensor(out=adjt[:, t, :], in0=adjt[:, t, :], scalar=dinv[:, t:t + 1],
                                                         in1=banks[7][:], op0=ALU.mult, op1=ALU.mult)
                ins.then_inc(ahat_ready, 1)
                dve.wait_ge(ahat_hi, 1)
                nc.vector.tensor_tensor(ahat_l[:], adjt[:], f32(ahat_h[:]), ALU.subtract)
                dve.wait_ge(wsmall_hi, 1)
                nc.vector.tensor_tensor(w1l[:], w1raw[:], f32(w1h[:]), ALU.subtract)
                nc.vector.tensor_tensor(w2l[:], w2raw[:], f32(w2h[:]), ALU.subtract).then_inc(weights_ready, 1)

            def combine(b, par, first):
                for k in (1, 2, 3):
                    for t in (first, first + 1):
                        if k == 1:
                            dve.wait_ge(scaled, NT * b + t + 1)
                        ins = nc.vector.scalar_tensor_tensor(
                            out=mix[:, par, t, :], in0=tile(PROD[t][:], k), scalar=coef[:, k, t:t + 1],
                            in1=mix[:, par, t, :], op0=ALU.mult, op1=ALU.add)
                    if k < 3:
                        chain.link(ins)
                ins.then_inc(mixed, 1)

            def slot(b, par, now, one, two):
                if one:
                    dve.wait_ge(rooted, b + 1)
                    nc.vector.scalar_tensor_tensor(out=shift[:], in0=mv[:, 0, :], scalar=-1.0, in1=rstd[:],
                                                   op0=ALU.mult, op1=ALU.mult).then_inc(shift_ready, 1)
                if now:
                    combine(b, par, 0)
                if two:
                    dve.wait_ge(agg_hi, b - 1)
                    nc.vector.tensor_tensor(aggl[:], AGG[:], f32(aggh[:]), ALU.subtract).then_inc(agg_lo, 1)
                if now:
                    combine(b, par, 2)
                    dve.wait_ge(mixed, 2 * b + 2)
                    m = mix[:, par, :, :].rearrange("p t d -> p (t d)")
                    nc.vector.tensor_tensor(m, m, BASE[par][:], ALU.add).then_inc(mix_done, 1)
                    dve.wait_ge(mix_done, b + 1)
                    need(dve, x1_ready, b)
                    for t in range(NT):
                        ins = nc.vector.bn_stats(stats[:, t, :], mix[:, par, t, :])
                    chain.link(ins)
                    moments(nc, chain, stats, mv, NT)
                    roots.n += 1
                    nc.vector.tensor_tensor(rstd[:], mv[:, 1, :], mv[:, 2, :], ALU.add).then_inc(asked, 1)
                if isinstance(b, int) and b == 0:
                    ahat()
                if two:
                    for h in range(HT):
                        dve.wait_ge(z_kept, HT * (b - 2) + h + 1)
                        ins = nc.vector.bn_stats(zstats[:, h, b - 2, :], z[:, h, b - 2, :])
                    ins.then_inc(z_counted, 1)
                if isinstance(b, int) and b == 2:
                    dve.wait_ge(kept_hi, 1)
                    nc.vector.tensor_tensor(adj_l[:], adjt[:], f32(adj_h[:]), ALU.subtract)
                    nc.vector.tensor_tensor(wih_l[:], adjn[:], f32(wih_h[:]), ALU.subtract)

            LINKS = 2 * 2 + LN_LINKS

            def in_loop(i, after):
                if i is None:
                    return chain.n
                chain.base, chain.n = i * (2 * LINKS) + after, 0

            phase_a(dve, slot, in_loop)

            roots.base, roots.n = B + 1, 0
            dve.wait_ge(z_counted, B)
            for h in range(HT):
                ins = nc.vector.bn_aggr(zmv[:, h, :], zstats[:, h, :, :].rearrange("p b s -> p (b s)"))
            chain.link(ins)
            nc.vector.tensor_tensor(sh1[:], zmv[:, :, 0], bn1s[:, 0, :], ALU.add)
            roots.ask(dve, nc.vector.tensor_scalar(sc1[:], zmv[:, :, 1], EPS, None, ALU.add))
            nc.vector.tensor_tensor(sh1[:], bn1s[:, 0, :], sh1[:], ALU.subtract)
            chain.link(nc.vector.tensor_tensor(sc1[:], sc1[:], bn1s[:, 1, :], ALU.mult))
            chain.link(nc.vector.tensor_tensor(sh1[:], sh1[:], sc1[:], ALU.mult))
            nc.vector.tensor_tensor(sh1[:], sh1[:], bn1s[:, 2, :], ALU.add).then_inc(bn1_ready, 1)

            def split_r(b, par):
                dve.wait_ge(r_ready, b + 1)
                need(dve, o2_done, b - 1)
                nc.vector.tensor_copy(r_h[:, par, :, :], act1[:, par, :, :]).then_inc(r_hi, 1)
                dve.wait_ge(r_hi, b + 1)
                nc.vector.tensor_tensor(r_l[:, par, 1, :], act1[:, par, 1, :], f32(r_h[:, par, 1, :]),
                                        ALU.subtract).then_inc(r_lo[1], 1)

            def count_o2(b, par):
                dve.wait_ge(o2_kept, b + 1)
                nc.vector.bn_stats(ostats[:, b, :], o2[:, par, :]).then_inc(o2_counted, 1)

            split_r(0, 0)
            split_r(1, 1)
            with dve.Fori(1, B // 2) as i:
                split_r(2 * i, 0)
                count_o2(2 * i - 2, 0)
                split_r(2 * i + 1, 1)
                count_o2(2 * i - 1, 1)
            count_o2(B - 2, 0)
            count_o2(B - 1, 1)
            dve.wait_ge(o2_counted, B)
            chain.link(nc.vector.bn_aggr(omv[:], ostats[:].rearrange("p b s -> p (b s)")))
            nc.vector.tensor_tensor(shift2[:], omv[:, 0:1], bn2s[:, 0:1], ALU.add)
            roots.ask(dve, nc.vector.tensor_scalar(scale2[:], omv[:, 1:2], EPS, None, ALU.add))
            nc.vector.tensor_tensor(shift2[:], bn2s[:, 0:1], shift2[:], ALU.subtract)
            chain.link(nc.vector.tensor_tensor(scale2[:], scale2[:], bn2s[:, 1:2], ALU.mult))
            chain.link(nc.vector.tensor_tensor(shift2[:], shift2[:], scale2[:], ALU.mult))
            chain.link(nc.vector.tensor_tensor(shift2[:], shift2[:], bn2s[:, 2:3], ALU.add))

        @block.tensor
        def _(pe):
            pe.wait_ge(c_nv, 32)
            for t in range(NT):
                mm = pe.matmul(banks[t][:], tile(nv1s[:], t), nv2s[:], start=True, stop=True)
            mm.then_inc(pe_setup, 1)
            pe.wait_ge(weights_ready, 1)

            def products(b, par, t):
                if t == 0:
                    pe.wait_ge(xt_hi, b + 1)
                    pe.wait_ge(xt_lo, b + 1)
                    need(pe, mix_done, b - 1)
                if t % 2 == 0:
                    need(pe, mixed, 2 * b + t // 2 - 1)
                x = (tile(xth[:, par, :], t), tile(xtl[:, par, :], t))
                wh, wl = wmix_h[:].rearrange("p k d -> p (k d)"), wmix_l[:].rearrange("p k d -> p (k d)")
                base = tile(BASE[par][:], t)
                pe.matmul(base, ones_r[:], bias_h[:], start=True, stop=False)
                pe.matmul(base, ones_r[:], bias_l[:], start=False, stop=False)
                matmul3(pe, base, x, (wh[:, 0:D], wl[:, 0:D]), False, True)
                matmul3(pe, PROD[t][:], x, (wh[:, D:5 * D], wl[:, D:5 * D]), True, True).then_inc(prod_done, 1)

            def slot(b, par, now, one, two):
                if now:
                    for t in range(NT):
                        products(b, par, t)
                if isinstance(b, int) and b == 0:
                    pe.wait_ge(dinv_spread, 1)
                    for t in range(NT):
                        mm = pe.matmul(tile(banks[7][:], t), ones[:], diag[:, t, :], start=True, stop=True)
                    mm.then_inc(pe_setup, 1)
                if two:
                    if isinstance(b, int) and b == 2:
                        pe.wait_ge(weights_ready, 2)
                    pe.wait_ge(agg_lo, b - 1)
                    for h in range(HT):
                        matmul3(pe, ZB[h][:], (tile(w1h[:], h), tile(w1l[:], h)), (aggh[:], aggl[:]),
                                True, True).then_inc(z_done, 1)
                if one:
                    if isinstance(b, int) and b == 1:
                        pe.wait_ge(weights_ready, 2)
                    pe.wait_ge(x1_lo, b)
                    need(pe, z_kept, HT * (b - 2) + 1)
                    for t in range(NT):
                        mm = matmul3(pe, AGG[:], (x1h[:, t, :], x1l[:, t, :]), (ahat_h[:, t, :], ahat_l[:, t, :]),
                                     t == 0, t == NT - 1)
                    mm.then_inc(agg_done, 1)

            phase_a(pe, slot)

            def second(b, par):
                pe.wait_ge(r_hi, b + 1)
                for h in range(HT):
                    pe.wait_ge(r_lo[h], b + 1)
                need(pe, o2_kept, b - 1)
                for h in range(HT):
                    mm = matmul3(pe, banks[par][:], (w2h[:, h, :], w2l[:, h, :]),
                                 (r_h[:, par, h, :], r_l[:, par, h, :]), h == 0, h == HT - 1)
                mm.then_inc(o2_done, 1)

            second(0, 0)
            second(1, 1)
            with pe.Fori(1, B // 2) as i:
                second(2 * i, 0)
                second(2 * i + 1, 1)


BABY = 3
POWERS = [1, 2, 3, 6]
KS = STEPS + 1


def second_half(nc, sem, banks, ident, exponent, scale2, shift2, adj_n, adj_t, bg0, bg1, alpha, l3_w_t, l3_d,
                fc_w, fc_b, adj_h, adj_l, wih_h, wih_l, whh_h, whh_l, wg_h, wg_l, gate_bias, row_sums,
                x1_dram, o2_dram, x2_dram, out):
    with ExitStack() as ctx:
        def sb(name, shape, dt=F32):
            return ctx.enter_context(nc.sbuf_tensor(name, shape, dt))

        pow_h = sb("pow_h", [P, len(POWERS), NT, N], F32R)
        pow_l = sb("pow_l", [P, len(POWERS), NT, N], F32R)
        e_h, e_l = sb("e_h", [P, BABY, BABY, D], F32R), sb("e_l", [P, BABY, BABY, D], F32R)
        conv_bias = sb("conv_bias", [P, NT, D])
        rows_bc = sb("rows_bc", [P, N])
        bg1s = sb("bg1s", [P, 1])
        euler_bias = sb("euler_bias", [P, NT, D])
        ident_r = sb("ident_r", [P, P], F32R)
        o2 = sb("o2b", [P, N])
        x1 = sb("x1b", [P, NT, D])
        x2 = sb("x2b", [P, NT, D])
        node_h, node_l = sb("node_h", [P, NT, D], F32R), sb("node_l", [P, NT, D], F32R)
        gat_h, gat_l = sb("gat_h", [P, N], F32R), sb("gat_l", [P, N], F32R)
        pre = sb("pre", [P, GB, N])
        x2_norm, out_norm = Norm(sb, "x2", NT), Norm(sb, "out", NT * GB)
        x3_norm = [Norm(sb, f"x3{j}", NT) for j in range(GB)]
        hh, hl = sb("hh", [P, GB, N], F32R), sb("hl", [P, GB, N], F32R)
        with ExitStack() as early:
            def scratch(name, shape, dt=F32):
                return early.enter_context(nc.sbuf_tensor(name, shape, dt))

            an, at = scratch("an", [P, NT, N]), scratch("at", [P, NT, N])
            nat_h, nat_l = scratch("nat_h", [P, NT, N], F32R), scratch("nat_l", [P, NT, N], F32R)
            ones2 = scratch("ones2", [P, P])
            rates, alphas = scratch("rates", [P, NT]), scratch("alphas", [P, NT])
            diags = scratch("diags", [P, 2, NT, P])
            bg0s = scratch("bg0s", [P, D])
            lw, lws, ld = scratch("lw", [P, D]), scratch("lws", [P, D]), scratch("ld", [P, 1])
            fcw, fcb = scratch("fcw", [P, D]), scratch("fcb", [P, 1])
            bp = scratch("bp", [P, KS, D])
            e = scratch("e", [P, BABY, BABY, D])
            bcols = scratch("bcols", [P, KS, KS])
            vec = scratch("vec", [P, NT, 3])
            vpad = scratch("vpad", [P, BABY, NT, KS])
            vpad_h, vpad_l = scratch("vpad_h", [P, BABY, NT, KS], F32R), scratch("vpad_l", [P, BABY, NT, KS], F32R)
            vec_t = scratch("vec_t", [KS, N])
            bc = scratch("bc", [KS, D])
        gate = [sb(f"gate{i}", [P, N]) for i in range(4)]
        cell = sb("cell", [P, N])
        st_h, st_l = sb("st_h", [P, N], F32R), sb("st_l", [P, N], F32R)
        x3 = sb("x3", [P, GB, NT, D])
        y = sb("y", [P, NT, GB, D])
        x3h, x3l = sb("x3h", [P, NT, D], F32R), sb("x3l", [P, NT, D], F32R)
        th, tl = sb("th", [P, BABY, N], F32R), sb("tl", [P, BABY, N], F32R)
        gh, gl = sb("gh", [P, 2, NT, GB, D], F32R), sb("gl", [P, 2, NT, GB, D], F32R)

        k_adj, k_small = sem("k_adj"), sem("k_small")
        k_bc, k_alpha, cols_ready, lws_ready, bcols_zero, vpad_zero = (
            sem(k) for k in ("k_bc", "k_alpha", "cols_ready", "lws_ready", "bcols_zero", "vpad_zero"))
        weff_done, a_ready, nat_hi, a_hi, k_chain = (sem(k) for k in ("weff_done", "a_ready", "nat_hi", "a_hi", "k_chain"))
        p_done, p_hi, p_lo = sem("p_done"), sem("p_hi"), sem("p_lo")
        b_done, b_kept, v2_done, v_kept, f_done, f_kept = (sem(k) for k in ("b_done", "b_kept", "v2_done", "v_kept", "f_done", "f_kept"))
        e_ready, e_hi, bc_done, vt_done, vt_kept, q_done, constants_ready = (
            sem(k) for k in ("e_ready", "e_hi", "bc_done", "vt_done", "vt_kept", "q_done", "constants_ready"))
        s = {name: sem(name) for name in (
            "front_loaded", "normed2", "o2_turned", "x2_summed", "x2_asked", "x2_rooted", "x2_shift", "x2_ready", "x2_stored", "x2_hi", "x2_lo", "h1_hi", "h1_lo",
            "gathered", "gat_hi", "gat_lo", "weighted", "pre0_ready", "pre1_ready", "h_hi", "h_ready",
            "gate_sum", "gate_on", "cell_ready", "tanh_ready", "state_hi", "state_ready",
            "x3_loaded", "h_turned", "x3_summed", "x3_asked", "x3_rooted", "x3_shift", "x3_ready", "x3_hi", "x3_lo", "power_done", "power_hi", "power_lo",
            "coef_done", "coef_hi", "coef_lo", "giant_done", "y_summed", "out_asked", "out_rooted", "out_shift", "out_ready", "links")}
        front_loaded, normed2, o2_turned, x2_summed, x2_ready, x2_stored = (
            s[k] for k in ("front_loaded", "normed2", "o2_turned", "x2_summed", "x2_ready", "x2_stored"))
        x2_asked, x2_rooted, x2_shift = (s[k] for k in ("x2_asked", "x2_rooted", "x2_shift"))
        x3_asked, x3_rooted, x3_shift = (s[k] for k in ("x3_asked", "x3_rooted", "x3_shift"))
        out_asked, out_rooted, out_shift = (s[k] for k in ("out_asked", "out_rooted", "out_shift"))
        x2_hi, x2_lo, h1_hi, h1_lo, gathered, gat_hi, gat_lo = (s[k] for k in ("x2_hi", "x2_lo", "h1_hi", "h1_lo", "gathered", "gat_hi", "gat_lo"))
        weighted, pre0_ready, pre1_ready, h_hi, h_ready = (s[k] for k in ("weighted", "pre0_ready", "pre1_ready", "h_hi", "h_ready"))
        gate_sum, gate_on, cell_ready, tanh_ready = (s[k] for k in ("gate_sum", "gate_on", "cell_ready", "tanh_ready"))
        state_hi, state_ready = s["state_hi"], s["state_ready"]
        x3_loaded, h_turned, x3_summed, x3_ready, x3_hi, x3_lo = (
            s[k] for k in ("x3_loaded", "h_turned", "x3_summed", "x3_ready", "x3_hi", "x3_lo"))
        power_done, power_hi, power_lo, coef_done, coef_hi, coef_lo = (s[k] for k in ("power_done", "power_hi", "power_lo", "coef_done", "coef_hi", "coef_lo"))
        giant_done, y_summed, out_ready, links = (s[k] for k in ("giant_done", "y_summed", "out_ready", "links"))
        out_stored = [sem(f"out_stored{j}") for j in range(GB)]

        GATE_BANK = {0: 0, 2: 1, 1: 2, 3: 3}
        FB = banks[4:6]
        UB = banks[6:8]
        HB = [banks[GATE_BANK[1]], UB[0]]
        out_v = out.rearrange("b (t p) d -> b p t d", p=P)

        def tile(ap, i):
            return ap[:, i * P:(i + 1) * P]

        def flat(ap):
            return ap.rearrange("p t d -> p (t d)")

        def shape_of(c):
            p, t, j = PAIRS[c]
            nw = N // p
            first = next(i for i, q in enumerate(PAIRS) if q[0] == p)
            return p, t, j, nw, (N if j is not None else GB * nw), sum(GATES[:c]), first

        def window(ap, c):
            p, t, j, nw, _, _, _ = shape_of(c)
            return ap[:, j, :] if j is not None else ap[:, :, t:p * (nw - 1) + t + 1:p]

        def flat_like(ap, c):
            _, _, j, nw, n, _, _ = shape_of(c)
            return ap[:, 0:n] if j is not None else ap[:, 0:n].rearrange("p (j w) -> p j w", j=GB)

        FILL_PE = [["giant1b"], ["turn_0"], ["x3t_0", "power1_0"], ["gather0_0", "power2_0"], ["weight0_0", "coefs0_0"],
                   ["gather1_0", "coefs1_0", "turn_1"], ["x3t_1", "power1_1", "weight1_0"], ["power2_1", "gather0_1"],
                   ["weight0_1", "coefs0_1"], ["gather1_1", "coefs1_1"], ["weight1_1", "giant0"]]
        FILL_ACT = [["prep_0"], ["x3norm_0", "x3split_0"], ["x3t_0", "norm_0", "power1_0"],
                    ["gather0_0", "power2_0", "out_0", "x3norm_1"], ["weight0_0", "coefs0_0", "prep_1", "x3split_1"],
                    ["gather1_0", "coefs1_0", "out_1"], ["x3t_1", "norm_1", "power1_1"], ["power2_1", "gather0_1"],
                    ["weight0_1", "coefs0_1"], ["gather1_1", "coefs1_1"], []]
        FILL_DVE = [["x3norm_0"], ["ysum", "turn_0"], ["norm_0", "x3t_0", "x3sum_1", "power1_0", "outsum"],
                    ["gather0_0", "power2_0", "out_0", "x3norm_1"], ["weight0_0", "coefs0_0"], ["gather1_0", "coefs1_0", "turn_1"],
                    ["norm_1", "x3t_1", "power1_1", "weight1_0"], ["power2_1", "gather0_1"], ["weight0_1", "coefs0_1"],
                    ["gather1_1", "coefs1_1"], ["weight1_1", "giant0"]]
        FILL_POOL = [[], ["x3split_0", "turn_0"], ["norm_0", "x3sum_1", "outsum"], [], ["x3split_1"], ["turn_1"], ["norm_1"],
                     [], [], [], []]
        FILL_SP = [["prep_0"], [], ["norm_0"], ["out_0", "prep_1"], [], ["out_1"], ["norm_1"], [], [], [], []]
        L3_NAMES = ("x3sum", "x3norm", "x3split", "x3t", "power1", "power2", "coefs0", "coefs1", "giant0")
        DONE_NAMES = ("giant1b", "ysum", "outsum", "out")
        START = ["prep_0", "const_0", "turn_0", "norm_0", "const_9", "const_1", "gather0_0", "const_2", "weight0_0", "const_3",
                 "gather1_0", "const_4", "weight1_0", "prep_1", "turn_1", "norm_1", "const_5", "gather0_1", "const_6",
                 "weight0_1", "const_7", "gather1_1", "const_8", "weight1_1"]

        def step(g, cell_step, pieces, fill, lstm, l3, front, done, const):
            def piece(name):
                kind, *i = name.split("_")
                if kind not in pieces:
                    return
                i = [int(k) for k in i]
                if kind in L3_NAMES:
                    if l3:
                        pieces[kind](g - 1, *i)
                elif kind in DONE_NAMES:
                    if done:
                        pieces[kind](g - 2, *i)
                elif front:
                    pieces[kind](g + 1, *i)

            if isinstance(g, int) and g == -1:
                for name in START:
                    if name.startswith("const"):
                        const(int(name.split("_")[1]))
                    else:
                        piece(name)
            else:
                for c in range(CELLS):
                    if lstm and cell_step:
                        cell_step(g, c)
                    for name in fill[c]:
                        piece(name)
            if "last" in pieces:
                pieces["last"](g, lstm, l3, front)

        def run(eng, cell_step, pieces, const, fill, chain=None):
            step(-1, cell_step, pieces, fill, False, False, True, False, const)
            eng.wait_ge(constants_ready, 2)
            step(0, cell_step, pieces, fill, True, False, True, False, const)
            step(1, cell_step, pieces, fill, True, True, True, False, const)
            ahead = chain.n if chain else 0
            with eng.Fori(2, G - 1) as g:
                if chain:
                    chain.base, chain.n = (g - 2) * LINKS_STEP + ahead, 0
                step(g, cell_step, pieces, fill, True, True, True, True, const)
                assert chain is None or chain.n == LINKS_STEP
            if chain:
                chain.base, chain.n = (G - 3) * LINKS_STEP + ahead, 0
            step(G - 1, cell_step, pieces, fill, True, True, False, True, const)
            step(G, cell_step, pieces, fill, False, True, False, True, const)
            step(G + 1, cell_step, pieces, fill, False, False, False, True, const)

        LINKS_STEP = LN_LINKS * (2 * GB + 1) + sum(1 for _, t, _ in PAIRS if t > 0) + CELLS

        block = ctx.enter_context(nc.Block())

        @block.sync
        def _(sp):
            def prep(g, j):
                n = GB * g + j
                need(sp, x2_summed, n)
                sp.dma_start(o2[:], o2_dram[n]).then_inc(front_loaded, 16)
                sp.dma_start(flat(x1[:]), x1_dram[n]).then_inc(front_loaded, 16)

            def norm(g, j):
                n = GB * g + j
                sp.wait_ge(x2_ready, n + 1)
                sp.dma_start(x2_dram[n], flat(x2[:])).then_inc(x2_stored, 16)

            def out_piece(g, j):
                sp.wait_ge(out_ready, GB * g + j + 1)
                sp.dma_start(out_v[GB * g + j], y[:, :, j, :]).then_inc(out_stored[j], 16)

            def last(g, lstm, l3, front):
                if lstm:
                    if l3:
                        sp.wait_ge(power_lo, BABY * GB * g)
                    for j in range(GB):
                        n = GB * g + j
                        sp.wait_ge(x2_stored, 16 * (n + 1))
                        sp.dma_start(flat(x3[:, j, :, :]), x2_dram[n]).then_inc(x3_loaded, 16)

            def const(i):
                if i == 0:
                    for dst, src in ((alphas, alpha), (lw, l3_w_t), (ld, l3_d), (fcw, fc_w), (fcb, fc_b), (bg0s, bg0), (bg1s, bg1)):
                        sp.dma_start(dst[:], src).then_inc(k_small, 16)
                    sp.dma_start(an[:], adj_n).then_inc(k_adj, 16)
                    sp.dma_start(at[:], adj_t).then_inc(k_adj, 16)

            run(sp, None, {"prep": prep, "norm": norm, "out": out_piece, "last": last}, const, FILL_SP)
            for j in range(GB):
                sp.wait_ge(out_stored[j], 16 * G)

        @block.gpsimd
        def _(pool):
            def root(norm, asked, rooted, count):
                pool.wait_ge(asked, count)
                nc.gpsimd.tensor_tensor(norm.rstd[:], norm.rstd[:], exponent[:, 0:norm.tiles], ALU.pow).then_inc(rooted, 1)

            def turn(g, j):
                root(x2_norm, x2_asked, x2_rooted, GB * g + j + 1)

            def norm(g, j):
                n = GB * g + j
                pool.wait_ge(x2_hi, n + 1)
                nc.gpsimd.tensor_tensor(node_l[:], x2[:], f32(node_h[:]), ALU.subtract).then_inc(x2_lo, 1)

            def x3sum(g, j):
                root(x3_norm[j], x3_asked, x3_rooted, GB * g + j + 1)

            def x3split(g, j):
                n = GB * g + j
                pool.wait_ge(x3_hi, n + 1)
                nc.gpsimd.tensor_tensor(x3l[:], x3[:, j, :, :], f32(x3h[:]), ALU.subtract).then_inc(x3_lo, 1)

            def last(g, lstm, l3, front):
                if lstm:
                    x3sum(g, 0)

            def outsum(g):
                root(out_norm, out_asked, out_rooted, g + 1)

            def const(i):
                if i == 0:
                    nc.gpsimd.memset(bcols[:], 0.0).then_inc(bcols_zero, 1)
                    nc.gpsimd.memset(vpad[:], 0.0).then_inc(vpad_zero, 1)

            run(pool, None, {"turn": turn, "norm": norm, "x3sum": x3sum, "x3split": x3split, "outsum": outsum,
                              "last": last}, const, FILL_POOL)

        @block.scalar
        def _(act):
            def cell_step(g, c):
                p, t, j, nw, n, before, first = shape_of(c)
                gates = [q for q in (0, 2, 1, 3) if t > 0 or q != 1]
                need(act, cell_ready, CELLS * g + c)
                for i, q in enumerate(gates):
                    act.wait_ge(gate_sum, GATES_ALL * g + before + i + 1)
                    if q != 0:
                        need(act, state_ready, CELLS * g + c)
                    nc.scalar.activation(gate[q][:, 0:n], banks[GATE_BANK[q]][:, 0:n], ACT.Tanh if q == 2 else ACT.Sigmoid,
                                         bias=gate_bias[:, p - 1, q:q + 1]).then_inc(gate_on, 1)
                act.wait_ge(cell_ready, CELLS * g + c + 1)
                nc.scalar.activation(gate[2][:, 0:n], cell[:, 0:n], ACT.Tanh).then_inc(tanh_ready, 1)

            def apply(norm, tiles, first=0):
                for t, ap in enumerate(tiles, first):
                    ins = nc.scalar.activation(ap, ap, ACT.Identity, scale=norm.rstd[:, t:t + 1], bias=norm.shift[:, t:t + 1])
                return ins

            def prep(g, j):
                n = GB * g + j
                act.wait_ge(front_loaded, 32 * (n + 1))
                nc.scalar.activation(o2[:], o2[:], ACT.Identity, scale=scale2[:, 0:1], bias=shift2[:, 0:1]).then_inc(normed2, 1)

            def norm(g, j):
                n = GB * g + j
                act.wait_ge(x2_shift, n + 1)
                apply(x2_norm, [x2[:, t, :] for t in range(NT)]).then_inc(x2_ready, 1)
                act.wait_ge(x2_ready, n + 1)
                need(act, gathered, 2 * n)
                nc.scalar.copy(node_h[:], x2[:]).then_inc(x2_hi, 1)

            def gather(g, j, conv):
                act.wait_ge(gathered, 2 * (GB * g + j) + conv + 1)
                nc.scalar.copy(gat_h[:], FB[j][:]).then_inc(gat_hi, 1)

            def weight0(g, j):
                act.wait_ge(pre0_ready, GB * g + j + 1)
                nc.scalar.activation(flat(node_h[:]), pre[:, j, :], ACT.Relu).then_inc(h1_hi, 1)

            def x3norm(g, j):
                act.wait_ge(x3_shift, GB * g + j + 1)
                apply(x3_norm[j], [x3[:, j, t, :] for t in range(NT)]).then_inc(x3_ready, 1)

            def x3split(g, j):
                n = GB * g + j
                act.wait_ge(x3_ready, n + 1)
                need(act, power_done, BABY * n)
                nc.scalar.copy(x3h[:], x3[:, j, :, :]).then_inc(x3_hi, 1)

            def x3t(g, j):
                n = GB * g + j
                act.wait_ge(power_done, BABY * n + 1)
                need(act, coef_done, NT * n)
                nc.scalar.copy(th[:, 0, :], UB[j][:]).then_inc(power_hi, 1)

            def power(g, j, k):
                act.wait_ge(power_done, BABY * (GB * g + j) + k + 1)
                nc.scalar.copy(th[:, k, :], UB[(j + k) % 2][:]).then_inc(power_hi, 1)

            def coefs(g, j, half):
                need(act, giant_done, 2 * g)
                for t in (2 * half, 2 * half + 1):
                    act.wait_ge(coef_done, NT * (GB * g + j) + t + 1)
                    nc.scalar.copy(gh[:, :, t, j, :], UB[t % 2][:, D:3 * D].rearrange("p (k d) -> p k d", d=D)).then_inc(coef_hi, 1)

            def out_piece(g, j):
                act.wait_ge(out_shift, g + 1)
                apply(out_norm, [y[:, t, j, :] for t in range(NT)], j * NT).then_inc(out_ready, 1)

            def last(g, lstm, l3, front):
                if front:
                    for j in range(GB):
                        if lstm:
                            act.wait_ge(h_turned, GB * g + j + 1)
                        act.wait_ge(pre1_ready, GB * (g + 1) + j + 1)
                        nc.scalar.activation(hh[:, j, :], pre[:, j, :], ACT.Relu).then_inc(h_hi, 1)

            def high(dst, first):
                for t in range(NT):
                    act.wait_ge(p_done, first + t + 1)
                    nc.scalar.copy(dst[:, t, :], banks[t][:]).then_inc(p_hi, 1)

            def const(i):
                if i == 0:
                    act.wait_ge(k_small, 16 * 7)
                    nc.scalar.activation(alphas[:], alphas[:], ACT.Sigmoid).then_inc(k_alpha, 1)
                if i == 1:
                    act.wait_ge(a_ready, 1)
                    nc.scalar.copy(nat_h[:], an[:]).then_inc(nat_hi, 1)
                    nc.scalar.copy(pow_h[:, 0, :, :], at[:]).then_inc(a_hi, 1)
                if i == 2:
                    high(pow_h[:, 1, :, :], 0)
                if i == 4:
                    high(pow_h[:, 2, :, :], NT)
                if i == 5:
                    high(nat_h, 2 * NT)
                if i == 6:
                    high(pow_h[:, 3, :, :], 3 * NT)
                if i == 7:
                    act.wait_ge(e_ready, 1)
                    nc.scalar.copy(e_h[:], e[:]).then_inc(e_hi, 1)

            run(act, cell_step, {"gather0": lambda g, j: gather(g, j, 0), "gather1": lambda g, j: gather(g, j, 1),
                            "power1": lambda g, j: power(g, j, 1), "power2": lambda g, j: power(g, j, 2),
                            "coefs0": lambda g, j: coefs(g, j, 0), "coefs1": lambda g, j: coefs(g, j, 1),
                            "prep": prep, "norm": norm, "weight0": weight0, "x3norm": x3norm, "x3split": x3split,
                            "x3t": x3t, "out": out_piece, "last": last}, const, FILL_ACT)

        @block.vector
        def _(dve):
            chain = Chain(dve, links)

            def cell_step(g, c):
                p, t, j, nw, n, before, first = shape_of(c)
                dve.wait_ge(gate_on, GATES_ALL * g + before + 2)
                if t == 0:
                    need(dve, tanh_ready, CELLS * g + c)
                    nc.vector.tensor_tensor(cell[:, 0:n], gate[0][:, 0:n], gate[2][:, 0:n], ALU.mult).then_inc(cell_ready, 1)
                else:
                    nc.vector.tensor_tensor(gate[0][:, 0:n], gate[0][:, 0:n], gate[2][:, 0:n], ALU.mult)
                    dve.wait_ge(gate_on, GATES_ALL * g + before + 3)
                    chain.link(nc.vector.tensor_tensor(gate[1][:, 0:n], gate[1][:, 0:n], cell[:, 0:n], ALU.mult))
                    nc.vector.tensor_tensor(cell[:, 0:n], gate[0][:, 0:n], gate[1][:, 0:n], ALU.add).then_inc(cell_ready, 1)
                dve.wait_ge(tanh_ready, CELLS * g + c + 1)
                dve.wait_ge(gate_on, GATES_ALL * g + before + GATES[c])
                if t == p - 1:
                    dst_h, dst_l = window(hh, c), window(hl, c)
                else:
                    dst_h, dst_l = flat_like(st_h, c), flat_like(st_l, c)
                o, tc, whole_h = flat_like(gate[3], c), flat_like(gate[2], c), flat_like(gate[1], c)
                nc.vector.tensor_tensor(dst_h, o, tc, ALU.mult).then_inc(state_hi, 1)
                chain.link(nc.vector.tensor_tensor(whole_h, o, tc, ALU.mult))
                nc.vector.tensor_tensor(dst_l, whole_h, f32(dst_h), ALU.subtract).then_inc(state_ready, 1)

            def moments_of(norm, tiles, asked):
                for i, ap in enumerate(tiles):
                    ins = nc.vector.bn_stats(norm.stats[:, i, :], ap)
                chain.link(ins)
                moments(nc, chain, norm.stats, norm.mv, norm.tiles)
                nc.vector.tensor_tensor(norm.rstd[:], norm.mv[:, 1, :], norm.mv[:, 2, :], ALU.add).then_inc(asked, 1)

            def shift_of(norm, shifted):
                nc.vector.scalar_tensor_tensor(out=norm.shift[:], in0=norm.mv[:, 0, :], scalar=-1.0, in1=norm.rstd[:],
                                               op0=ALU.mult, op1=ALU.mult).then_inc(shifted, 1)

            def turn(g, j):
                n = GB * g + j
                need(dve, x2_stored, 16 * n)
                need(dve, x2_lo, n)
                dve.wait_ge(o2_turned, n + 1)
                nc.vector.tensor_tensor(flat(x2[:]), FB[j][:], flat(x1[:]), ALU.add).then_inc(x2_summed, 1)
                dve.wait_ge(x2_summed, n + 1)
                moments_of(x2_norm, [x2[:, t, :] for t in range(NT)], x2_asked)

            def norm(g, j):
                dve.wait_ge(x2_rooted, GB * g + j + 1)
                shift_of(x2_norm, x2_shift)

            def gather(g, j, conv):
                dve.wait_ge(gat_hi, 2 * (GB * g + j) + conv + 1)
                nc.vector.tensor_tensor(gat_l[:], FB[j][:], f32(gat_h[:]), ALU.subtract).then_inc(gat_lo, 1)

            def weight0(g, j):
                n = GB * g + j
                need(dve, h_ready, n - GB + 1)
                dve.wait_ge(weighted, 2 * n + 1)
                nc.vector.tensor_tensor(pre[:, j, :], FB[j][:], flat(conv_bias[:]), ALU.add).then_inc(pre0_ready, 1)
                dve.wait_ge(h1_hi, n + 1)
                nc.vector.scalar_tensor_tensor(out=flat(node_l[:]), in0=pre[:, j, :], scalar=0.0, in1=f32(flat(node_h[:])),
                                               op0=ALU.max, op1=ALU.subtract).then_inc(h1_lo, 1)

            def weight1(g, j):
                n = GB * g + j
                dve.wait_ge(weighted, 2 * n + 2)
                dve.wait_ge(h1_lo, n + 1)
                nc.vector.scalar_tensor_tensor(out=pre[:, j, :], in0=rows_bc[:], scalar=bg1s[:, 0:1], in1=FB[j][:],
                                               op0=ALU.mult, op1=ALU.add).then_inc(pre1_ready, 1)

            def x3sum(g, j):
                dve.wait_ge(x3_summed, GB * (g + 1))
                need(dve, x3_ready, GB * g + j + 1 - GB)
                moments_of(x3_norm[j], [x3[:, j, t, :] for t in range(NT)], x3_asked)

            def x3norm(g, j):
                dve.wait_ge(x3_rooted, GB * g + j + 1)
                shift_of(x3_norm[j], x3_shift)

            def x3t(g, j):
                n = GB * g + j
                dve.wait_ge(power_hi, BABY * n + 1)
                nc.vector.tensor_tensor(tl[:, 0, :], UB[j][:], f32(th[:, 0, :]), ALU.subtract).then_inc(power_lo, 1)

            def power(g, j, k):
                dve.wait_ge(power_hi, BABY * (GB * g + j) + k + 1)
                nc.vector.tensor_tensor(tl[:, k, :], UB[(j + k) % 2][:], f32(th[:, k, :]), ALU.subtract).then_inc(power_lo, 1)

            def coefs(g, j, half):
                n = GB * g + j
                need(dve, out_stored[j], 16 * g)
                for t in (2 * half, 2 * half + 1):
                    dve.wait_ge(coef_hi, NT * n + t + 1)
                    nc.vector.tensor_tensor(y[:, t, j, :], UB[t % 2][:, 0:D], euler_bias[:, t, :], ALU.add)
                    nc.vector.tensor_tensor(gl[:, :, t, j, :], UB[t % 2][:, D:3 * D].rearrange("p (k d) -> p k d", d=D),
                                            f32(gh[:, :, t, j, :]), ALU.subtract).then_inc(coef_lo, 1)

            def giant(g, half):
                dve.wait_ge(coef_lo, NT * GB * (g + 1))
                dve.wait_ge(giant_done, 2 * g + half + 1)
                part = y[:, 2 * half:2 * half + 2, :, :].rearrange("p t j d -> p (t j d)")
                nc.vector.tensor_tensor(part, part, UB[half][:], ALU.add).then_inc(y_summed, 1)

            def out_piece(g, j):
                if j == 0:
                    dve.wait_ge(out_rooted, g + 1)
                    shift_of(out_norm, out_shift)

            def last(g, lstm, l3, front):
                if front:
                    for j in range(GB):
                        dve.wait_ge(h_hi, GB * (g + 1) + j + 1)
                        nc.vector.scalar_tensor_tensor(out=hl[:, j, :], in0=pre[:, j, :], scalar=0.0, in1=f32(hh[:, j, :]),
                                                       op0=ALU.max, op1=ALU.subtract).then_inc(h_ready, 1)
                if lstm:
                    dve.wait_ge(x3_loaded, 16 * GB * (g + 1))
                    for j in range(GB):
                        dve.wait_ge(h_turned, GB * g + j + 1)
                        nc.vector.tensor_tensor(flat(x3[:, j, :, :]), HB[j][:], flat(x3[:, j, :, :]), ALU.add).then_inc(x3_summed, 1)
                    x3sum(g, 0)

            def outsum(g):
                dve.wait_ge(y_summed, 2 * (g + 1))
                need(dve, out_ready, GB * g)
                moments_of(out_norm, [y[:, t, j, :] for j in range(GB) for t in range(NT)], out_asked)

            own = Chain(dve, k_chain)

            def low(dst, hi, first):
                for t in range(NT):
                    dve.wait_ge(p_hi, first + t + 1)
                    nc.vector.tensor_tensor(dst[:, t, :], banks[t][:], f32(hi[:, t, :]), ALU.subtract).then_inc(p_lo, 1)

            def scale_f(k, bank, m):
                return nc.vector.tensor_scalar(e[:, k % BABY, k // BABY, :], tile(bank[:], m), float(comb(STEPS, k)), None, ALU.mult)

            def const(i):
                if i == 0:
                    nc.vector.memset(ones2[:], 1.0)
                    nc.vector.tensor_copy(ident_r[:], ident[:])
                    nc.vector.tensor_copy(bp[:, 0, :], ident[:])
                    dve.wait_ge(k_alpha, 1)
                    own.link(nc.vector.tensor_scalar(rates[:], alphas[:], DT * 0.5, None, ALU.mult))
                    for v, cols in enumerate((row_sums, rates)):
                        for t in range(NT):
                            ins = nc.vector.tensor_scalar(diags[:, v, t, :], ident[:], cols[:, t:t + 1], None, ALU.mult)
                    ins.then_inc(cols_ready, 1)
                    own.link(nc.vector.tensor_scalar(ld[:], ld[:], 0.0, 1.0, ALU.max, ALU.min))
                    nc.vector.tensor_scalar(lws[:], lw[:], ld[:, 0:1], None, ALU.mult).then_inc(lws_ready, 1)
                    dve.wait_ge(k_bc, 2)
                    nc.vector.tensor_copy(rows_bc[:], banks[0][:])
                if i == 9:
                    dve.wait_ge(k_adj, 32)
                    for t in range(NT):
                        nc.vector.tensor_tensor(tile(an[:, t, :], t), tile(an[:, t, :], t), ident[:], ALU.subtract)
                        ins = nc.vector.tensor_tensor(tile(at[:, t, :], t), tile(at[:, t, :], t), ident[:], ALU.subtract)
                    own.link(ins)
                    for t in range(NT):
                        nc.vector.tensor_scalar(an[:, t, :], an[:, t, :], rates[:, t:t + 1], None, ALU.mult)
                        ins = nc.vector.tensor_tensor(at[:, t, :], at[:, t, :], banks[1][:], ALU.mult)
                    ins.then_inc(a_ready, 1)
                if i == 1:
                    dve.wait_ge(a_ready, 1)
                    nc.vector.memset(vec[:, :, 0], 1.0)
                    own.link(nc.vector.reduce_sum(vec[:, :, 1], an[:], AX_X))
                    dve.sem_inc(v_kept, 1)
                    dve.wait_ge(nat_hi, 1)
                    nc.vector.tensor_tensor(nat_l[:], an[:], f32(nat_h[:]), ALU.subtract)
                    dve.wait_ge(a_hi, 1)
                    nc.vector.tensor_tensor(pow_l[:, 0, :, :], at[:], f32(pow_h[:, 0, :, :]), ALU.subtract).then_inc(p_lo, 1)
                    for t in range(NT):
                        nc.vector.tensor_scalar(conv_bias[:, t, :], bg0s[:], row_sums[:, t:t + 1], None, ALU.mult)
                    own.link(nc.vector.tensor_scalar(bp[:, 1, :], ident[:], 1.0 - DT, None, ALU.mult))
                    dve.wait_ge(weff_done, 1)
                    nc.vector.scalar_tensor_tensor(out=bp[:, 1, :], in0=tile(banks[6][:], 0), scalar=DT, in1=bp[:, 1, :],
                                                   op0=ALU.mult, op1=ALU.add).then_inc(b_kept, 1)
                    dve.wait_ge(bcols_zero, 1)
                    for k in range(KS):
                        ins = nc.vector.tensor_scalar(bcols[:, k, k:k + 1], fcb[:], float(comb(STEPS, k)), None, ALU.mult)
                    own.link(ins)
                if i == 2:
                    low(pow_l[:, 1, :, :], pow_h[:, 1, :, :], 0)
                    dve.wait_ge(b_done, 1)
                    nc.vector.tensor_copy(bp[:, 2, :], tile(banks[6][:], 0)).then_inc(b_kept, 1)
                if i == 3:
                    dve.wait_ge(b_done, 2)
                    nc.vector.tensor_copy(bp[:, 3:5, :].rearrange("p k d -> p (k d)"), banks[7][:, 0:2 * D]).then_inc(b_kept, 1)
                    dve.wait_ge(v2_done, 1)
                    own.link(nc.vector.tensor_copy(vec[:, :, 2], banks[6][:, 0:NT]))
                    dve.wait_ge(vpad_zero, 1)
                    for q in range(BABY):
                        ins = nc.vector.tensor_copy(vpad[:, q, :, BABY * q:BABY * (q + 1)], vec[:])
                    own.link(ins)
                    own.link(nc.vector.tensor_copy(vpad_h[:], vpad[:]))
                    nc.vector.tensor_tensor(vpad_l[:], vpad[:], f32(vpad_h[:]), ALU.subtract).then_inc(v_kept, 1)
                if i == 4:
                    low(pow_l[:, 2, :, :], pow_h[:, 2, :, :], NT)
                    dve.wait_ge(b_done, 3)
                    nc.vector.tensor_copy(bp[:, 5:9, :].rearrange("p k d -> p (k d)"), banks[7][:]).then_inc(b_kept, 1)
                if i == 5:
                    low(nat_l, nat_h, 2 * NT)
                    dve.wait_ge(f_done, 1)
                    for m in range(4):
                        ins = scale_f(STEPS - m, banks[6], m)
                    ins.then_inc(f_kept, 1)
                    dve.wait_ge(f_done, 2)
                    for m in range(4):
                        ins = scale_f(4 - m, banks[7], m)
                    ins.then_inc(f_kept, 1)
                    dve.wait_ge(f_done, 3)
                    own.link(scale_f(0, banks[6], 0))
                if i == 6:
                    for j in range(STEPS):
                        for k in range(STEPS - j):
                            ek = e[:, k % BABY, k // BABY, :]
                            factor = DT * comb(j + k, k) + (1.0 if j == 0 and k == 0 else 0.0)
                            ins = nc.vector.scalar_tensor_tensor(out=ek, in0=bp[:, j, :], scalar=factor, in1=ek,
                                                                 op0=ALU.mult, op1=ALU.add)
                        if j < STEPS - 1:
                            own.link(ins)
                    ins.then_inc(e_ready, 1)
                    low(pow_l[:, 3, :, :], pow_h[:, 3, :, :], 3 * NT)
                if i == 7:
                    dve.wait_ge(e_hi, 1)
                    nc.vector.tensor_tensor(e_l[:], e[:], f32(e_h[:]), ALU.subtract)
                    dve.wait_ge(bc_done, 1)
                    nc.vector.tensor_copy(bc[:], banks[7][0:KS, 0:D])
                    dve.wait_ge(vt_done, 1)
                    nc.vector.tensor_copy(vec_t[:], banks[6][0:KS, :]).then_inc(vt_kept, 1)
                if i == 8:
                    dve.wait_ge(q_done, 1)
                    nc.vector.tensor_copy(euler_bias[:].rearrange("p t d -> p (t d)"), banks[7][:]).then_inc(constants_ready, 2)

            run(dve, cell_step, {"gather0": lambda g, j: gather(g, j, 0), "gather1": lambda g, j: gather(g, j, 1),
                            "power1": lambda g, j: power(g, j, 1), "power2": lambda g, j: power(g, j, 2),
                            "coefs0": lambda g, j: coefs(g, j, 0), "coefs1": lambda g, j: coefs(g, j, 1),
                            "turn": turn, "norm": norm, "weight0": weight0, "weight1": weight1, "x3sum": x3sum,
                            "x3norm": x3norm, "x3t": x3t, "giant0": lambda g: giant(g, 0),
                            "ysum": lambda g: giant(g, 1), "outsum": outsum, "out": out_piece, "last": last}, const, FILL_DVE, chain)

        @block.tensor
        def _(pe):
            def cell_step(g, c):
                p, t, j, nw, n, before, first = shape_of(c)
                gates = [q for q in (0, 2, 1, 3) if t > 0 or q != 1]
                if j is not None:
                    pe.wait_ge(h_ready, GB * g + j + 1)
                else:
                    pe.wait_ge(state_ready, CELLS * g + first)
                need(pe, gate_on, GATES_ALL * g + before)
                if c == PAIRS.index((2, 1, None)):
                    need(pe, x3_summed, GB * g)
                for q in gates:
                    mm = matmul3(pe, flat_like(banks[GATE_BANK[q]], c), (tile(wih_h[:, p - 1, :], q), tile(wih_l[:, p - 1, :], q)),
                                 (window(hh, c), window(hl, c)), True, t == 0)
                    if t == 0:
                        mm.then_inc(gate_sum, 1)
                if t > 0:
                    pe.wait_ge(state_hi, CELLS * g + c)
                    for q in gates:
                        bank = banks[GATE_BANK[q]][:, 0:n]
                        pe.matmul(bank, tile(whh_h[:, p - 2, :], q), st_h[:, 0:n], start=False, stop=False)
                        pe.matmul(bank, tile(whh_l[:, p - 2, :], q), st_h[:, 0:n], start=False, stop=False)
                    pe.wait_ge(state_ready, CELLS * g + c)
                    for q in gates:
                        pe.matmul(banks[GATE_BANK[q]][:, 0:n], tile(whh_h[:, p - 2, :], q), st_l[:, 0:n],
                                  start=False, stop=True).then_inc(gate_sum, 1)

            def turn(g, j):
                n = GB * g + j
                pe.wait_ge(normed2, n + 1)
                need(pe, pre1_ready, n - 1)
                for t in range(NT):
                    mm = pe.transpose(tile(FB[j][:], t), tile(o2[:], t), ident[:])
                mm.then_inc(o2_turned, 1)

            def gather(g, j, conv):
                n = GB * g + j
                if conv == 0:
                    pe.wait_ge(x2_lo, n + 1)
                else:
                    pe.wait_ge(h1_lo, n + 1)
                for t in range(NT):
                    mm = matmul3(pe, FB[j][:], (node_h[:, t, :], node_l[:, t, :]), (adj_h[:, t, :], adj_l[:, t, :]),
                                 t == 0, t == NT - 1)
                mm.then_inc(gathered, 1)

            def weight0(g, j):
                pe.wait_ge(gat_lo, 2 * (GB * g + j) + 1)
                for t in range(NT):
                    mm = matmul3(pe, tile(FB[j][:], t), (tile(gat_h[:], t), tile(gat_l[:], t)),
                                 (wg_h[:, 0, :], wg_l[:, 0, :]), True, True)
                mm.then_inc(weighted, 1)

            def weight1(g, j):
                pe.wait_ge(gat_lo, 2 * (GB * g + j) + 2)
                matmul3(pe, FB[j][:], (wg_h[:, 1, :], wg_l[:, 1, :]), (gat_h[:], gat_l[:]), True, True).then_inc(weighted, 1)

            def x3t(g, j):
                n = GB * g + j
                pe.wait_ge(x3_ready, n + 1)
                if j == 0:
                    pe.wait_ge(x3_summed, GB * (g + 1))
                else:
                    pe.wait_ge(coef_lo, NT * n)
                for t in range(NT):
                    mm = pe.transpose(tile(UB[j][:], t), x3[:, j, t, :], ident[:])
                mm.then_inc(power_done, 1)

            def power(g, j, k):
                n = GB * g + j
                pe.wait_ge(x3_lo, n + 1)
                if k == 1 and j == 0:
                    need(pe, y_summed, 2 * g)
                if k > 1:
                    pe.wait_ge(power_lo, BABY * n + k - 1)
                for t in range(NT):
                    mm = matmul3(pe, UB[(j + k) % 2][:], (x3h[:, t, :], x3l[:, t, :]),
                                 (pow_h[:, k - 1, t, :], pow_l[:, k - 1, t, :]), t == 0, t == NT - 1)
                mm.then_inc(power_done, 1)

            def coefs(g, j, half):
                n = GB * g + j
                pe.wait_ge(power_lo, BABY * (n + 1))
                for t in (2 * half, 2 * half + 1):
                    if t >= 2:
                        pe.wait_ge(coef_lo, NT * n + t - 1)
                    for k in range(BABY):
                        mm = matmul3(pe, UB[t % 2][:, 0:3 * D], (tile(th[:, k, :], t), tile(tl[:, k, :], t)),
                                     (e_h[:, k, :, :].rearrange("p a d -> p (a d)"), e_l[:, k, :, :].rearrange("p a d -> p (a d)")),
                                     k == 0, k == BABY - 1)
                    mm.then_inc(coef_done, 1)

            def giant(g, half, parts=(0, 1)):
                pe.wait_ge(coef_lo, NT * GB * (g + 1))
                for t in (2 * half + part for part in parts):
                    dst = UB[half][:, (t % 2) * GB * D:(t % 2 + 1) * GB * D]
                    for k in range(2):
                        for m in range(NT):
                            mm = matmul3(pe, dst, (tile(pow_h[:, 2 + k, m, :], t), tile(pow_l[:, 2 + k, m, :], t)),
                                         (gh[:, k, m, :, :].rearrange("p j d -> p (j d)"), gl[:, k, m, :, :].rearrange("p j d -> p (j d)")),
                                         k == 0 and m == 0, k == 1 and m == NT - 1)
                if parts[-1] == 1:
                    mm.then_inc(giant_done, 1)

            def last(g, lstm, l3, front):
                if lstm:
                    pe.wait_ge(state_ready, CELLS * (g + 1))
                    for j in range(GB):
                        if j == 1 and l3:
                            pe.wait_ge(y_summed, 2 * g - 1)
                        for t in range(NT):
                            pe.matmul(tile(HB[j][:], t), tile(hh[:, j, :], t), ident_r[:], start=True, stop=False)
                            mm = pe.matmul(tile(HB[j][:], t), tile(hl[:, j, :], t), ident_r[:], start=False, stop=True)
                        mm.then_inc(h_turned, 1)
                if l3:
                    giant(g - 1, 1, (0,))

            def bflat(a, b):
                return bp[:, a:b, :].rearrange("p k d -> p (k d)")

            def product(right, first):
                for t in range(NT):
                    for m in range(NT):
                        mm = matmul3(pe, banks[t][:], (tile(nat_h[:, m, :], t), tile(nat_l[:, m, :], t)),
                                     (pow_h[:, right, m, :], pow_l[:, right, m, :]), m == 0, m == NT - 1)
                    mm.then_inc(p_done, 1)

            def const(i):
                if i == 0:
                    pe.wait_ge(cols_ready, 1)
                    for v in range(2):
                        for t in range(NT):
                            mm = pe.matmul(tile(banks[v][:], t), ones2[:], diags[:, v, t, :], start=True, stop=True)
                        mm.then_inc(k_bc, 1)
                    pe.wait_ge(lws_ready, 1)
                    pe.matmul(tile(banks[6][:], 0), lws[:], lw[:], start=True, stop=True).then_inc(weff_done, 1)
                if i == 2:
                    pe.wait_ge(p_lo, 1)
                    product(0, 0)
                    pe.wait_ge(b_kept, 1)
                    pe.matmul(tile(banks[6][:], 0), bp[:, 1, :], bp[:, 1, :], start=True, stop=True).then_inc(b_done, 1)
                if i == 3:
                    pe.wait_ge(b_kept, 2)
                    pe.matmul(banks[7][:, 0:2 * D], bp[:, 2, :], bflat(1, 3), start=True, stop=True).then_inc(b_done, 1)
                    pe.wait_ge(v_kept, 1)
                    for t in range(NT):
                        for m in range(NT):
                            mm = pe.matmul(banks[6][:, t:t + 1], tile(at[:, m, :], t), vec[:, m, 1:2],
                                           start=(m == 0), stop=(m == NT - 1))
                    mm.then_inc(v2_done, 1)
                if i == 4:
                    pe.wait_ge(p_lo, 1 + NT)
                    product(1, NT)
                    pe.wait_ge(b_kept, 3)
                    pe.matmul(banks[7][:], bp[:, 4, :], bflat(1, 5), start=True, stop=True).then_inc(b_done, 1)
                if i == 5:
                    pe.wait_ge(p_lo, 1 + 2 * NT)
                    for t in range(NT):
                        for m in range(NT):
                            pe.matmul(tile(banks[t][:], m), tile(pow_h[:, 2, m, :], t), ident_r[:], start=True, stop=False)
                            mm = pe.matmul(tile(banks[t][:], m), tile(pow_l[:, 2, m, :], t), ident_r[:], start=False, stop=True)
                        mm.then_inc(p_done, 1)
                    pe.wait_ge(v_kept, 2)
                    pe.matmul(banks[6][:], fcw[:], bflat(0, 4), start=True, stop=True).then_inc(f_done, 1)
                    pe.wait_ge(b_kept, 4)
                    pe.matmul(banks[7][:], fcw[:], bflat(4, 8), start=True, stop=True).then_inc(f_done, 1)
                    pe.wait_ge(f_kept, 1)
                    pe.matmul(banks[6][:, 0:D], fcw[:], bflat(8, 9), start=True, stop=True).then_inc(f_done, 1)
                if i == 6:
                    pe.wait_ge(p_lo, 1 + 3 * NT)
                    product(2, 3 * NT)
                if i == 7:
                    pe.wait_ge(f_kept, 2)
                    for k in range(KS):
                        mm = pe.matmul(banks[7][0:KS, 0:D], bcols[:, k, :], bp[:, STEPS - k, :], start=(k == 0), stop=(k == KS - 1))
                    mm.then_inc(bc_done, 1)
                    pe.wait_ge(p_lo, 1 + 4 * NT)
                    for q in (2, 1):
                        for m in range(NT):
                            matmul3(pe, banks[6][0:KS, :], (vpad_h[:, q, m, :], vpad_l[:, q, m, :]),
                                    (pow_h[:, 1 + q, m, :], pow_l[:, 1 + q, m, :]), q == 2 and m == 0, False, skip_group_check=True)
                    for m in range(NT):
                        pe.matmul(tile(banks[6][0:KS, :], m), vpad_h[:, 0, m, :], ident_r[:], start=False, stop=False, skip_group_check=True)
                        mm = pe.matmul(tile(banks[6][0:KS, :], m), vpad_l[:, 0, m, :], ident_r[:], start=False, stop=(m == NT - 1),
                                       skip_group_check=True)
                    mm.then_inc(vt_done, 1)
                if i == 8:
                    pe.wait_ge(vt_kept, 1)
                    for t in range(NT):
                        mm = pe.matmul(tile(banks[7][:], t), tile(vec_t[:], t), bc[:], start=True, stop=True)
                    mm.then_inc(q_done, 1)

            run(pe, cell_step, {"gather0": lambda g, j: gather(g, j, 0), "gather1": lambda g, j: gather(g, j, 1),
                            "power1": lambda g, j: power(g, j, 1), "power2": lambda g, j: power(g, j, 2),
                            "coefs0": lambda g, j: coefs(g, j, 0), "coefs1": lambda g, j: coefs(g, j, 1),
                            "turn": turn, "weight0": weight0, "weight1": weight1, "x3t": x3t,
                            "giant0": lambda g: giant(g, 0), "giant1b": lambda g: giant(g, 1, (1,)),
                            "last": last}, const, FILL_PE)


def kernel(**inputs):
    import numpy as np
    import concourse.bacc as bacc
    from concourse.bass_utils import run_bass_kernel_spmd

    v = {k: np.asarray(a) for k, a in inputs.items()}

    def rows(a):
        return a.reshape(-1, P, a.shape[-1]).transpose(1, 0, 2)

    def column(a):
        return a.reshape(-1, P).T

    laid = [
        ("x_t", v["x"].transpose(0, 2, 1)),
        ("adj_n", rows(v["adj"])),
        ("adj_t", rows(v["adj"].T)),
        ("nv1_t", v["L0_gnn_node_vec1"].T),
        ("nv2", v["L0_gnn_node_vec2"]),
        ("l0_w", rows(v["L0_gnn_W"])),
        ("l0_b", v["L0_gnn_b"][None, :]),
        ("w1_t", v["L1_gnn_W1"].T),
        ("bn1", np.stack([column(v["L1_gnn_" + k]) for k in ("b1", "g1", "be1")], 1)),
        ("w2_t", rows(v["L1_gnn_W2"].T)),
        ("bn2", np.stack([v["L1_gnn_" + k] for k in ("b2", "g2", "be2")], 1)),
        ("wg", np.stack([v["L2_gnn_Wg0"], v["L2_gnn_Wg1"]], 1)),
        ("bg0", np.tile(v["L2_gnn_bg0"], (P, 1))),
        ("bg1", v["L2_gnn_bg1"][:, None]),
        ("wih_t", v["L2_gnn_Wih"].transpose(2, 0, 1)),
        ("whh_t", v["L2_gnn_Whh"][1:].transpose(2, 0, 1)),
        ("bih", v["L2_gnn_bih"].reshape(SKIPS, 4, P).transpose(2, 0, 1)),
        ("bhh", v["L2_gnn_bhh"].reshape(SKIPS, 4, P).transpose(2, 0, 1)),
        ("alpha", column(v["L3_gnn_alpha_train"])),
        ("l3_w_t", v["L3_gnn_w"].T),
        ("l3_d", v["L3_gnn_d"][:, None]),
        ("fc_w", v["L3_gnn_fc_in_w"]),
        ("fc_b", v["L3_gnn_fc_in_b"][:, None]),
        ("eye", np.eye(P, dtype=np.float32)),
    ]
    nc = bacc.Bacc("TRN2", target_bir_lowering=False, num_devices=1)
    arrays, args = {}, []
    for name, a in laid:
        a = np.ascontiguousarray(a)
        arrays[f"in_{name}_dram"] = a
        args.append(nc.dram_tensor(f"in_{name}_dram", a.shape, mybir.dt.from_np(a.dtype), kind="ExternalInput").ap())
    args.append(nc.dram_tensor("out_dram", (B, N, D), F32, kind="ExternalOutput").ap())
    program(nc, *args)
    r = run_bass_kernel_spmd(nc, [arrays], core_ids=[0])
    return r.results[0]["out_dram"]
```
